# Optimizing a Trainium2 kernel written in Bass

```python
import numpy as np
import jax
import jax.numpy as jnp

def _softmax(x, axis=-1):
    return jax.nn.softmax(x, axis=axis)

def _gelu(x):
    return jax.nn.gelu(x, approximate=True)

def _silu(x):
    return jax.nn.silu(x)

def _sigmoid(x):
    return jax.nn.sigmoid(x)

def _layernorm(x, axis=-1, eps=1e-05):
    m = jnp.mean(x, axis=axis, keepdims=True)
    v = jnp.var(x, axis=axis, keepdims=True)
    return (x - m) / jnp.sqrt(v + eps)

def _scatter_add(tgt, idx, src, axis=0):
    return tgt.at[idx].add(src)

def _segment_sum(src, seg, n):
    return jax.ops.segment_sum(src, seg, n)
kernel_name = 'mk_perceiver_d1_seqx_r2_dfcae1'

def setup_inputs(seed: int=0):
    np.random.seed(seed)
    _w = jnp.asarray

    def _rec_inputs():
        import jax
        import jax.numpy as jnp
        _rk = jax.random.key(seed)
        x = -0.0003929 + 0.9999 * jax.random.normal(jax.random.fold_in(_rk, 1), (32, 32, 512), jnp.float32)
        _lenS = 32 - jax.random.randint(jax.random.fold_in(_rk, 7), (32,), 0, max(1, 32 // 4) + 1, jnp.int32)
        _lenS2 = 257 - jax.random.randint(jax.random.fold_in(_rk, 8), (32,), 0, max(1, 257 // 4) + 1, jnp.int32)
        _ctx_768P = jax.random.normal(jax.random.fold_in(_rk, 11), (32, 16, 384), jnp.float32)
        _ctx_768c = jax.random.dirichlet(jax.random.fold_in(_rk, 511), 0.3 * jnp.ones((16,), jnp.float32), (32, 257))
        _ctx_768t = jnp.einsum('bsk,bkd->bsd', _ctx_768c, _ctx_768P)
        _ctx_768t = _ctx_768t * jax.lax.rsqrt(jnp.mean(jnp.square(_ctx_768t)) + 1e-12) * 0.953939
        ctx_768 = 0.00095986 + 0.999812 * (_ctx_768t + 0.3 * jax.random.normal(jax.random.fold_in(_rk, 611), (32, 257, 384), jnp.float32))
        _validS = jnp.arange(32)[None, :] < _lenS[:, None]
        _validS2 = jnp.arange(257)[None, :] < _lenS2[:, None]
        _causal = jnp.tril(jnp.ones((32, 32), dtype=bool))
        mask_BxS2_bf1 = jnp.ones((32, 257), dtype=bool)
        return (x, ctx_768, mask_BxS2_bf1)
    x, ctx_768, mask_BxS2_bf1 = _rec_inputs()

    def _L0_xattn_setup():
        import jax, jax.numpy as jnp
        import numpy as np
        DIM = 512
        CTX_DIM = 384
        HEADS = 16
        key = jax.random.key(seed)
        ks = jax.random.split(key, 7)
        B, N, M = (4, 2048, 128)
        x = jax.random.normal(ks[0], (B, N, DIM), dtype=jnp.float32)
        context = jax.random.normal(ks[1], (B, M, CTX_DIM), dtype=jnp.float32)
        context_mask = jnp.ones((B, M), dtype=bool)
        s_d = 1.0 / np.sqrt(DIM)
        s_c = 1.0 / np.sqrt(CTX_DIM)
        Wq = jax.random.normal(ks[2], (DIM, DIM), dtype=jnp.float32) * s_d
        Wk = jax.random.normal(ks[3], (CTX_DIM, DIM), dtype=jnp.float32) * s_c
        Wv = jax.random.normal(ks[4], (CTX_DIM, DIM), dtype=jnp.float32) * s_c
        Wo = jax.random.normal(ks[5], (DIM, DIM), dtype=jnp.float32) * s_d
        return {'x': x, 'context': context, 'context_mask': context_mask, 'Wq': Wq, 'Wk': Wk, 'Wv': Wv, 'Wo': Wo}
    _L0_xattn_all = _L0_xattn_setup()
    _L0_xattn_in = {k: v for k, v in _L0_xattn_all.items() if k in ('Wq', 'Wk', 'Wv', 'Wo')}
    del _L0_xattn_all

    def _L0_attn_setup():
        import jax, jax.numpy as jnp
        import numpy as np
        D_MODEL = 512
        NUM_HEADS = 16
        HEAD_DIM = D_MODEL // NUM_HEADS
        EPS = 1e-08
        key = jax.random.key(seed)
        ks = jax.random.split(key, 6)
        B, T = (4, 1024)
        s = 0.02
        return {'x': jax.random.normal(ks[0], (B, T, D_MODEL), dtype=jnp.float32), 'Wq': jax.random.normal(ks[1], (D_MODEL, D_MODEL), dtype=jnp.float32) * s, 'Wk': jax.random.normal(ks[2], (D_MODEL, D_MODEL), dtype=jnp.float32) * s, 'Wv': jax.random.normal(ks[3], (D_MODEL, D_MODEL), dtype=jnp.float32) * s, 'Wo': jax.random.normal(ks[4], (D_MODEL, D_MODEL), dtype=jnp.float32) * s, 'bo': jnp.zeros((D_MODEL,), dtype=jnp.float32)}
    _L0_attn_all = _L0_attn_setup()
    _L0_attn_in = {k: v for k, v in _L0_attn_all.items() if k in ('Wq', 'Wk', 'Wv', 'Wo', 'bo')}
    del _L0_attn_all

    def _L0_ffn_setup():
        import jax, jax.numpy as jnp
        import numpy as np
        D, H, NE, K, ED = (512, 16, 8, 2, 2048)
        B, S = (4, 512)
        EPS = 1e-06

        def rmsnorm(x, w):
            ms = jnp.mean(jnp.square(x.astype(jnp.float32)), axis=-1, keepdims=True)
            return x * jax.lax.rsqrt(ms + EPS).astype(x.dtype) * w

        def attn(x, qkv_w, o_w):
            b, s, d = x.shape
            hd = d // H
            qkv = (x @ qkv_w.T).reshape(b, s, 3, H, hd).transpose(2, 0, 3, 1, 4)
            q, k, v = (qkv[0], qkv[1], qkv[2])
            a = jnp.einsum('bhqd,bhkd->bhqk', q, k) * hd ** (-0.5)
            mask = jnp.triu(jnp.ones((s, s), dtype=bool), 1)
            a = jax.nn.softmax(jnp.where(mask, -1000000000.0, a), axis=-1)
            out = jnp.einsum('bhqk,bhkd->bhqd', a, v).transpose(0, 2, 1, 3).reshape(b, s, d)
            return out @ o_w.T

        def moe(x, gate_w, up_w, down_w):
            b, s, d = x.shape
            xf = x.reshape(b * s, d)
            gp = jax.nn.softmax(xf @ gate_w.T, axis=-1)
            ew, _ = jax.lax.top_k(gp, K)
            ew = ew / (jnp.sum(ew, axis=-1, keepdims=True) + 1e-09)
            ef = jax.nn.silu(xf @ up_w.T) @ down_w.T
            out = ef * jnp.sum(ew, axis=-1, keepdims=True)
            return out.reshape(b, s, d)
        key = jax.random.key(seed)
        ks = jax.random.split(key, 8)
        sd = 1.0 / np.sqrt(D)
        se = 1.0 / np.sqrt(ED)
        return {'x': jax.random.normal(ks[0], (B, S, D), dtype=jnp.float32), 'n1_w': jnp.ones((D,), jnp.float32), 'qkv_w': jax.random.normal(ks[1], (3 * D, D), jnp.float32) * sd, 'o_w': jax.random.normal(ks[2], (D, D), jnp.float32) * sd, 'n2_w': jnp.ones((D,), jnp.float32), 'gate_w': jax.random.normal(ks[3], (NE, D), jnp.float32) * sd, 'up_w': jax.random.normal(ks[4], (ED, D), jnp.float32) * sd, 'down_w': jax.random.normal(ks[5], (D, ED), jnp.float32) * se}
    _L0_ffn_all = _L0_ffn_setup()
    _L0_ffn_in = {k: v for k, v in _L0_ffn_all.items() if k in ('n1_w', 'qkv_w', 'o_w', 'n2_w', 'gate_w', 'up_w', 'down_w')}
    del _L0_ffn_all
    return {'x': x, 'ctx_768': ctx_768, 'mask_BxS2_bf1': mask_BxS2_bf1, 'L0_xattn_Wq': _L0_xattn_in['Wq'], 'L0_xattn_Wk': _L0_xattn_in['Wk'], 'L0_xattn_Wv': _L0_xattn_in['Wv'], 'L0_xattn_Wo': _L0_xattn_in['Wo'], 'L0_attn_Wq': _L0_attn_in['Wq'], 'L0_attn_Wk': _L0_attn_in['Wk'], 'L0_attn_Wv': _L0_attn_in['Wv'], 'L0_attn_Wo': _L0_attn_in['Wo'], 'L0_attn_bo': _L0_attn_in['bo'], 'L0_ffn_n1_w': _L0_ffn_in['n1_w'], 'L0_ffn_qkv_w': _L0_ffn_in['qkv_w'], 'L0_ffn_o_w': _L0_ffn_in['o_w'], 'L0_ffn_n2_w': _L0_ffn_in['n2_w'], 'L0_ffn_gate_w': _L0_ffn_in['gate_w'], 'L0_ffn_up_w': _L0_ffn_in['up_w'], 'L0_ffn_down_w': _L0_ffn_in['down_w']}

def reference(x, ctx_768, mask_BxS2_bf1, L0_xattn_Wq, L0_xattn_Wk, L0_xattn_Wv, L0_xattn_Wo, L0_attn_Wq, L0_attn_Wk, L0_attn_Wv, L0_attn_Wo, L0_attn_bo, L0_ffn_n1_w, L0_ffn_qkv_w, L0_ffn_o_w, L0_ffn_n2_w, L0_ffn_gate_w, L0_ffn_up_w, L0_ffn_down_w):
    import jax
    import jax.numpy as jnp

    def _L0_xattn_ref(x, context, context_mask, Wq, Wk, Wv, Wo):
        import jax, jax.numpy as jnp
        import numpy as np
        DIM = 512
        CTX_DIM = 384
        HEADS = 16
        B, N, _ = x.shape
        M = context.shape[1]
        hd = DIM // HEADS
        scale = hd ** (-0.5)
        q = (x @ Wq).reshape(B, N, HEADS, hd).transpose(0, 2, 1, 3)
        k = (context @ Wk).reshape(B, M, HEADS, hd).transpose(0, 2, 1, 3)
        v = (context @ Wv).reshape(B, M, HEADS, hd).transpose(0, 2, 1, 3)
        scores = jnp.einsum('bhid,bhjd->bhij', q, k) * scale
        max_neg = -jnp.finfo(scores.dtype).max
        scores = jnp.where(context_mask[:, None, None, :], scores, max_neg)
        attn = jax.nn.softmax(scores, axis=-1)
        out = jnp.einsum('bhij,bhjd->bhid', attn, v)
        out = out.transpose(0, 2, 1, 3).reshape(B, N, DIM)
        return out @ Wo

    def _L0_attn_ref(x, Wq, Wk, Wv, Wo, bo):
        import jax, jax.numpy as jnp
        import numpy as np
        D_MODEL = 512
        NUM_HEADS = 16
        HEAD_DIM = D_MODEL // NUM_HEADS
        EPS = 1e-08
        B, T, _ = x.shape
        H, D = (NUM_HEADS, HEAD_DIM)
        scale = jnp.sqrt(jnp.asarray(D, dtype=x.dtype))
        q = (x @ Wq.T).reshape(B, T, H, D).transpose(0, 2, 1, 3)
        k = (x @ Wk.T).reshape(B, T, H, D).transpose(0, 2, 1, 3)
        v = (x @ Wv.T).reshape(B, T, H, D).transpose(0, 2, 1, 3)
        s = jnp.einsum('bhtd,bhsd->bhts', q, k) / scale
        m = jnp.max(s, axis=-1, keepdims=True)
        e = jnp.exp(s - m)
        num = jnp.einsum('bhts,bhsd->bhtd', e, v)
        den = jnp.sum(e, axis=-1, keepdims=True) + EPS
        out = (num / den).transpose(0, 2, 1, 3).reshape(B, T, H * D)
        return out @ Wo.T + bo

    def _L0_ffn_ref(x, n1_w, qkv_w, o_w, n2_w, gate_w, up_w, down_w):
        import jax, jax.numpy as jnp
        import numpy as np
        D, H, NE, K, ED = (512, 16, 8, 2, 2048)
        B, S = (4, 512)
        EPS = 1e-06

        def rmsnorm(x, w):
            ms = jnp.mean(jnp.square(x.astype(jnp.float32)), axis=-1, keepdims=True)
            return x * jax.lax.rsqrt(ms + EPS).astype(x.dtype) * w

        def attn(x, qkv_w, o_w):
            b, s, d = x.shape
            hd = d // H
            qkv = (x @ qkv_w.T).reshape(b, s, 3, H, hd).transpose(2, 0, 3, 1, 4)
            q, k, v = (qkv[0], qkv[1], qkv[2])
            a = jnp.einsum('bhqd,bhkd->bhqk', q, k) * hd ** (-0.5)
            mask = jnp.triu(jnp.ones((s, s), dtype=bool), 1)
            a = jax.nn.softmax(jnp.where(mask, -1000000000.0, a), axis=-1)
            out = jnp.einsum('bhqk,bhkd->bhqd', a, v).transpose(0, 2, 1, 3).reshape(b, s, d)
            return out @ o_w.T

        def moe(x, gate_w, up_w, down_w):
            b, s, d = x.shape
            xf = x.reshape(b * s, d)
            gp = jax.nn.softmax(xf @ gate_w.T, axis=-1)
            ew, _ = jax.lax.top_k(gp, K)
            ew = ew / (jnp.sum(ew, axis=-1, keepdims=True) + 1e-09)
            ef = jax.nn.silu(xf @ up_w.T) @ down_w.T
            out = ef * jnp.sum(ew, axis=-1, keepdims=True)
            return out.reshape(b, s, d)
        x = x + attn(rmsnorm(x, n1_w), qkv_w, o_w)
        x = x + moe(rmsnorm(x, n2_w), gate_w, up_w, down_w)
        return x
    x = x + _L0_xattn_ref(_layernorm(x, axis=-1), ctx_768, mask_BxS2_bf1, L0_xattn_Wq, L0_xattn_Wk, L0_xattn_Wv, L0_xattn_Wo)
    x = x + _L0_attn_ref(_layernorm(x, axis=-1), L0_attn_Wq, L0_attn_Wk, L0_attn_Wv, L0_attn_Wo, L0_attn_bo)
    x = x + _L0_ffn_ref(_layernorm(x, axis=-1), L0_ffn_n1_w, L0_ffn_qkv_w, L0_ffn_o_w, L0_ffn_n2_w, L0_ffn_gate_w, L0_ffn_up_w, L0_ffn_down_w)
    return x

_drawn_inputs = setup_inputs


def setup_inputs(seed=0):
    import zlib

    import numpy as np

    out = dict(_drawn_inputs(seed))
    spreads = {'L0_attn_bo': (0.0, 0.1), 'L0_ffn_n1_w': (1.0, 0.2), 'L0_ffn_n2_w': (1.0, 0.2)}
    factors = {'L0_attn_Wq': 8.0, 'L0_attn_Wk': 8.0, 'L0_ffn_gate_w': 8.0}
    for name, (base, spread) in spreads.items():
        noise = np.random.default_rng([zlib.crc32(name.encode()), seed]).standard_normal(out[name].shape)
        drawn = base * np.exp(spread * noise) if base else spread * noise
        out[name] = jnp.asarray(drawn.astype(out[name].dtype))
    for name, factor in factors.items():
        out[name] = (out[name] * factor).astype(out[name].dtype)
    return out
```

```python
from contextlib import ExitStack

import concourse.bass as bass
from concourse import mybir

F32 = mybir.dt.float32
F32R = mybir.dt.float32r
U8 = mybir.dt.uint8
ALU = mybir.AluOpType
ACT = mybir.ActivationFunctionType
AX = mybir.AxisListType

P = 128
D = 512
KC = D // P
CC = 3
HD = 32
SEQ = 32
NB = 32
KEYS = 257
MAIN = KEYS - 1
PAIRS = NB // 2
TILES = NB * SEQ // P
HALVES = 2
HT = TILES // HALVES
HALF = HT * P
HPAIRS = PAIRS // HALVES
NE = 8
SCALE = float(HD) ** -0.5
BIG = 1.0e38
LN_EPS = 1e-5
RMS_EPS = 1e-6
DEN_EPS = 1e-8
TOPK_EPS = 1e-9

UNITS = ["x_wo", "a_v", "a_k", "a_q", "a_wo", "f_v", "f_k", "f_q", "f_wo",
         "up0", "up1", "down0", "down1", "up2", "up3", "down2", "down3"]
NU = len(UNITS)
RING = 3

USE_WO = (0, 16, 32)
USE_V = (4, 20)
USE_KQ = (8, 24)
USE_UP = (36, 44)
USES = 52 // 2
FREES = 36 // 2


class Chain:

    def __init__(self, eng, sem):
        self.eng, self.sem, self.base, self.n = eng, sem, 0, 0

    def step(self, ins):
        ins.then_inc(self.sem, 1)
        self.n += 1

    def wait(self):
        self.eng.wait_ge(self.sem, self.base + self.n)

    def enter(self, i, per):
        self.before, self.per = self.base + self.n, per
        self.base, self.n = self.before + per * i, 0

    def leave(self, count):
        assert self.n == self.per, self.n
        self.base, self.n = self.before + self.per * count, 0


def wait(eng, sem, value):
    if not isinstance(value, int) or value > 0:
        eng.wait_ge(sem, value)


def stand_alone(eng, passed):
    eng.sem_inc(passed, 1)


def product(pe, out, left, right, first, last):
    pe.matmul(out, left[0], right[0], start=first, stop=False)
    pe.matmul(out, left[0], right[1], start=False, stop=False)
    return pe.matmul(out, left[1], right[0], start=False, stop=last)


def build(nc, x, ctx_main, ctx_last, mask, wq, wk, wv, units, gate, n1, n2, bo, out):
    heads_dram = nc.dram_tensor("heads_scratch", (PAIRS, P, 256), F32, kind="Internal").ap()
    vlast_dram = nc.dram_tensor("vlast_scratch", (NB, 4, P), F32, kind="Internal").ap()
    with ExitStack() as stack:
        banks = {}
        for name in ("proj0", "proj1", "tr0", "tr1", "s0", "s1", "o0", "o1"):
            banks[name] = stack.enter_context(nc.psum_tensor(name, [P, 512], F32))
        ident = stack.enter_context(nc.sbuf_tensor("ident", [P, P], F32))
        cross_attention(nc, banks, ident, x, ctx_main, ctx_last, mask, wq, wk, wv,
                        heads_dram, vlast_dram)
        rest_of_layer(nc, banks, ident, x, heads_dram, units, gate, n1, n2, bo, out)


def cross_attention(nc, banks, ident, x, ctx_main, ctx_last, mask, wq, wk, wv,
                    heads_dram, vlast_dram):
    x_tiles = x.rearrange("(t p) d -> t p d", p=P)
    mask_pairs = mask.rearrange("(q b) j -> q b j", b=2)
    with ExitStack() as stack:
        def sb(name, shape, dt=F32):
            return stack.enter_context(nc.sbuf_tensor(name, shape, dt))

        def sem(name):
            return stack.enter_context(nc.semaphore(name))

        def split_pair(name, shape):
            return sb(name + "_hi", shape, F32R), sb(name + "_lo", shape, F32R)

        proj = [banks["proj0"], banks["proj1"]]
        tr = [banks["tr0"], banks["tr1"]]
        score_bank = [banks["s0"], banks["s1"]]
        out_bank = [banks["o0"], banks["o1"]]

        wk_raw, wv_raw, wq_raw = sb("wk_raw", [P, CC, D]), sb("wv_raw", [P, CC, D]), sb("wq_raw", [P, KC, D])
        wk_s, wv_s, wq_s = split_pair("wk", [P, CC, D]), split_pair("wv", [P, CC, D]), split_pair("wq", [P, KC, D])
        last_raw = sb("ctx_last_raw", [P, CC, NB])
        last_s = split_pair("ctx_last", [P, CC, P])
        k_last = sb("k_last", [P, KC, NB])
        v_last = sb("v_last", [NB, 4, 4, HD])
        v_last_all = sb("v_last_all", [P, NB, P])
        ctx_raw = [sb(f"ctx_raw{i}", [P, CC, 512]) for i in range(2)]
        ctx_s = [split_pair(f"ctx{i}", [P, CC, 512]) for i in range(2)]
        mask_raw = [sb(f"mask_raw{i}", [P, 2, KEYS], U8) for i in range(2)]
        mask_bias = [sb(f"mask_bias{i}", [P, 2, KEYS]) for i in range(2)]
        k_t = [sb(f"k_t{i}", [P, KC, 2, 258]) for i in range(2)]
        v_sb = [sb(f"v_sb{i}", [P, 2, 2, D]) for i in range(2)]
        probs = sb("probs", [P, 2, KC, KEYS])
        probs_t = sb("probs_t", [P, 2, 2, KC, P])
        x_raw = sb("x_raw", [P, D])
        x_hat = sb("x_hat", [P, D])
        x_t = split_pair("x_t", [P, KC, P])
        q_sb = sb("q_sb", [P, D])
        q_diag = sb("q_diag", [P, 4 * 4, P])
        stats = sb("stats", [P, 6])
        mean_var = sb("mean_var", [P, 2])
        var_eps = sb("var_eps", [P, 1])
        rstd = sb("rstd", [P, 1])
        minus_half = sb("minus_half", [P, 1])
        row_max = sb("row_max", [P, 2, KC])
        exp_bias = sb("exp_bias", [P, 2, KC])
        denom = sb("denom", [P, 2, KC])
        r_denom = sb("r_denom", [P, 8])
        last_part = sb("last_part", [P, 8, HD])
        heads = sb("heads", [P, 8, HD])
        heads_t = [sb(f"heads_t{i}", [P, 8 * SEQ]) for i in range(2)]

        passed_pool, passed_dve, passed_sp = sem("passed_pool"), sem("passed_dve"), sem("passed_sp")
        w_in = [sem(f"w_in{i}") for i in range(3)]
        w_hi, w_lo = sem("w_hi"), sem("w_lo")
        last_in, last_zero = sem("last_in"), sem("last_zero")
        last_k_full, last_v_full, last_k_done, last_v_done = (
            sem("last_k_full"), sem("last_v_full"), sem("last_k_done"), sem("last_v_done"))
        vlast_out, vlast_in = sem("vlast_out"), sem("vlast_in")
        ctx_in = [sem(f"ctx_in{i}") for i in range(2)]
        mask_in = [sem(f"mask_in{i}") for i in range(2)]
        x_in = sem("x_in")
        ctx_ready, mask_ready, k_last_ready = sem("ctx_ready"), sem("mask_ready"), sem("k_last_ready")
        ident_ready, diag_zero, pool_step, dve_step = sem("ident_ready"), sem("diag_zero"), sem("pool_step"), sem("dve_step")
        var_ready, rstd_ready, x_hat_ready = sem("var_ready"), sem("rstd_ready"), sem("x_hat_ready")
        xt_full, xt_hi, xt_lo = sem("xt_full"), sem("xt_hi"), sem("xt_lo")
        q_full, q_copied, qt_full, q_diag_ready = sem("q_full"), sem("q_copied"), sem("qt_full"), sem("q_diag_ready")
        k_full = [sem(f"k_full{i}") for i in range(2)]
        k_done = [sem(f"k_done{i}") for i in range(2)]
        v_full = [sem(f"v_full{i}") for i in range(2)]
        v_done = [sem(f"v_done{i}") for i in range(2)]
        s_full, s_read = sem("s_full"), sem("s_read")
        bias_ready, exp_done = sem("bias_ready"), sem("exp_done")
        pt_full = [sem(f"pt_full{i}") for i in range(2)]
        pt_done = [sem(f"pt_done{i}") for i in range(2)]
        pv_full, pv_read, heads_ready = sem("pv_full"), sem("pv_read"), sem("heads_ready")
        heads_out = [sem(f"heads_out{i}") for i in range(2)]

        block = stack.enter_context(nc.Block())

        @block.sync
        def _(sp):
            def load_pair(t, par):
                q = 2 * t + par
                sp.dma_start(ctx_raw[par][:], ctx_main[bass.ds(q, 1)].rearrange("o p c n -> (o p) c n")
                             ).then_inc(ctx_in[par], 16)

            def load_mask(t, par):
                q = 2 * t + par
                sp.dma_start(mask_raw[par][:],
                             mask_pairs[bass.ds(q, 1)].rearrange("o b j -> (o b) j").unsqueeze(0)
                             .to_broadcast([P, 2, KEYS])).then_inc(mask_in[par], 16)

            def store_heads(t, par):
                q = 2 * t + par
                sp.wait_ge(heads_ready, q + 1)
                stand_alone(sp, passed_sp)
                sp.dma_start(heads_dram[bass.ds(q, 1)].rearrange("o p n -> (o p) n"), heads_t[par][:]
                             ).then_inc(heads_out[par], 16)

            sp.dma_start(last_raw[:], ctx_last).then_inc(last_in, 16)
            sp.dma_start(wk_raw[:], wk).then_inc(w_in[0], 16)
            load_pair(0, 0)
            sp.dma_start(x_raw[:], x_tiles[0]).then_inc(x_in, 16)
            sp.dma_start(wv_raw[:], wv).then_inc(w_in[1], 16)
            sp.dma_start(wq_raw[:], wq).then_inc(w_in[2], 16)
            load_mask(0, 0)
            load_mask(0, 1)
            load_pair(0, 1)
            sp.wait_ge(last_v_done, 1)
            sp.dma_start(vlast_dram.rearrange("b a n -> b (a n)"),
                         v_last[:].rearrange("b a g d -> b (a g d)")).then_inc(vlast_out, 16)
            sp.wait_ge(vlast_out, 16)
            for a in range(4):
                sp.dma_start(v_last_all[32 * a:32 * a + 32],
                             vlast_dram[:, a, :].unsqueeze(0).to_broadcast([SEQ, NB, P])
                             ).then_inc(vlast_in, 16)
            with sp.Fori(0, TILES - 1) as t:
                sp.wait_ge(x_hat_ready, t + 1)
                stand_alone(sp, passed_sp)
                sp.dma_start(x_raw[:], x_tiles[bass.ds(t + 1, 1)].rearrange("o p d -> (o p) d")
                             ).then_inc(x_in, 16)
                for par in range(2):
                    sp.wait_ge(ctx_ready, 2 * t + par + 1)
                    stand_alone(sp, passed_sp)
                    load_pair(t + 1, par)
                    sp.wait_ge(mask_ready, 2 * t + par + 1)
                    stand_alone(sp, passed_sp)
                    load_mask(t + 1, par)
                    store_heads(t, par)
            for par in range(2):
                store_heads(TILES - 1, par)
            for par in range(2):
                sp.wait_ge(heads_out[par], 16 * TILES)

        @block.gpsimd
        def _(pool):
            chain = Chain(pool, pool_step)

            def split_ctx(t, par):
                q = 2 * t + par
                wait(pool, s_read, 8 * q - 6)
                pool.wait_ge(mask_in[par], 16 * t + 16)
                stand_alone(pool, passed_pool)
                pool.tensor_scalar(mask_bias[par][:], mask_raw[par][:], BIG, -BIG, ALU.mult, ALU.add
                                   ).then_inc(mask_ready, 1)
                wait(pool, v_full[1], 2 * q - 2)
                pool.wait_ge(ctx_in[par], 16 * t + 16)
                hi, lo = ctx_s[par]
                stand_alone(pool, passed_pool)
                chain.step(pool.tensor_scalar(hi[:], ctx_raw[par][:], 1.0, None, ALU.mult))
                chain.wait()
                pool.tensor_tensor(lo[:], ctx_raw[par][:], hi[:].bitcast(F32), ALU.subtract
                                   ).then_inc(ctx_ready, 1)

            def root(t):
                pool.wait_ge(var_ready, t + 1)
                stand_alone(pool, passed_pool)
                chain.step(pool.tensor_scalar(var_eps[:], mean_var[:, 1:2], LN_EPS, None, ALU.add))
                chain.wait()
                pool.tensor_tensor(rstd[:], var_eps[:], minus_half[:], ALU.pow).then_inc(rstd_ready, 1)

            for part in last_s:
                pool.memset(part[:].bitcast(F32), 0.0).then_inc(last_zero, 1)
            chain.step(pool.memset(minus_half[:], -0.5))
            chain.step(pool.memset(ident[:], 0.0))
            chain.wait()
            pool.affine_select(out=ident[:], in_=ident[:], compare_op=ALU.not_equal, fill=1.0, base=0,
                               pattern=[[-1, P]], channel_multiplier=1).then_inc(ident_ready, 1)
            split_ctx(0, 0)
            root(0)
            pool.memset(q_diag[:], 0.0).then_inc(diag_zero, 1)
            chain.enter(0, 3)
            with pool.Fori(0, TILES - 1) as t:
                chain.base = chain.before + 3 * t
                split_ctx(t, 1)
                root(t + 1)
                split_ctx(t + 1, 0)
            chain.leave(TILES - 1)
            split_ctx(TILES - 1, 1)

        @block.scalar
        def _(act):
            def copy_k(t, par, j):
                q = 2 * t + par
                act.wait_ge(k_full[0], 2 * q + j + 1)
                act.activation(k_t[par][:, 2 * j, :, 0:MAIN],
                               proj[0][:].rearrange("p (b n) -> p b n", b=2), ACT.Copy).then_inc(k_done[0], 1)

            def copy_v(t, par, j):
                q = 2 * t + par
                act.wait_ge(v_full[0], 2 * q + j + 1)
                act.activation(v_sb[par][:, j, 0, :], proj[0][:], ACT.Copy).then_inc(v_done[0], 1)

            def exps(t, par, b):
                q = 2 * t + par
                act.wait_ge(bias_ready, 2 * q + b + 1)
                for g in range(KC):
                    last = act.activation(probs[:, b, g, :], probs[:, b, g, :], ACT.Exp,
                                          bias=exp_bias[:, b, g:g + 1], scale=SCALE,
                                          accum_out=denom[:, b, g:g + 1])
                last.then_inc(exp_done, 1)

            def copy_pt(t, par, b):
                q = 2 * t + par
                act.wait_ge(pt_full[0], 2 * q + b + 1)
                act.activation(probs_t[:, b, 0].rearrange("p g n -> p (g n)"), tr[0][:], ACT.Copy
                               ).then_inc(pt_done[0], 1)

            def copy_xt(t):
                act.wait_ge(xt_full, t + 1)
                act.activation(x_t[0][:].rearrange("p c n -> p (c n)"), tr[0][:], ACT.Copy).then_inc(xt_hi, 1)

            def copy_q(t):
                act.wait_ge(qt_full, t + 1)
                for a in (0, 1):
                    rows = slice(32 * a, 32 * a + 32)
                    last = act.activation(q_diag[rows, :, rows],
                                          tr[0][rows, :].rearrange("p (n i) -> p n i", i=SEQ), ACT.Copy)
                last.then_inc(q_diag_ready, 1)

            for n, (raw, parts) in enumerate(((wk_raw, wk_s), (wv_raw, wv_s), (wq_raw, wq_s))):
                act.wait_ge(w_in[n], 16)
                act.activation(parts[0][:], raw[:], ACT.Copy).then_inc(w_hi, 1)
                if n == 0:
                    act.wait_ge(last_in, 16)
                    act.wait_ge(last_zero, 2)
                    act.activation(last_s[0][:, :, 0:NB], last_raw[:], ACT.Copy).then_inc(w_hi, 1)
            act.wait_ge(last_v_full, 1)
            act.activation(v_last[:], proj[1][0:NB, :].rearrange("p (g a d) -> p a g d", g=4, a=4), ACT.Copy
                           ).then_inc(last_v_done, 1)
            copy_xt(0)
            copy_k(0, 0, 0)
            copy_k(0, 0, 1)
            act.wait_ge(diag_zero, 1)
            copy_q(0)
            copy_v(0, 0, 0)
            copy_v(0, 0, 1)

            def even_pair(t):
                exps(t, 0, 0)
                copy_k(t, 1, 0)
                exps(t, 0, 1)
                copy_k(t, 1, 1)
                copy_pt(t, 0, 0)
                copy_pt(t, 0, 1)
                copy_v(t, 1, 0)
                copy_v(t, 1, 1)

            with act.Fori(0, TILES - 1) as t:
                even_pair(t)
                exps(t, 1, 0)
                copy_xt(t + 1)
                copy_k(t + 1, 0, 0)
                exps(t, 1, 1)
                copy_k(t + 1, 0, 1)
                copy_q(t + 1)
                copy_pt(t, 1, 0)
                copy_pt(t, 1, 1)
                copy_v(t + 1, 0, 0)
                copy_v(t + 1, 0, 1)
            even_pair(TILES - 1)
            exps(TILES - 1, 1, 0)
            exps(TILES - 1, 1, 1)
            copy_pt(TILES - 1, 1, 0)
            copy_pt(TILES - 1, 1, 1)

        @block.vector
        def _(dve):
            chain = Chain(dve, dve_step)

            def copy_k(t, par, j):
                q = 2 * t + par
                dve.wait_ge(k_full[1], 2 * q + j + 1)
                dve.tensor_copy(k_t[par][:, 2 * j + 1, :, 0:MAIN],
                                proj[1][:].rearrange("p (b n) -> p b n", b=2)).then_inc(k_done[1], 1)

            def last_key(t, par):
                q = 2 * t + par
                dve.tensor_scalar(k_t[par][:, :, :, MAIN], k_last[:, :, bass.ds(2 * q, 2)], 1.0, None, ALU.mult
                                  ).then_inc(k_last_ready, 1)

            def copy_v(t, par, j):
                q = 2 * t + par
                dve.wait_ge(v_full[1], 2 * q + j + 1)
                dve.tensor_copy(v_sb[par][:, j, 1, :], proj[1][:]).then_inc(v_done[1], 1)

            def mask_max(t, par):
                q = 2 * t + par
                dve.wait_ge(mask_ready, q + 1)
                for b in range(2):
                    for g in range(KC):
                        dve.wait_ge(s_full, 8 * q + 4 * b + g + 1)
                        stand_alone(dve, passed_dve)
                        dve.tensor_tensor_reduce(
                            out=probs[:, b, g, :], in0=score_bank[g % 2][:, 0:KEYS], in1=mask_bias[par][:, b, :],
                            scale=1.0, scalar=-3.0e38, op0=ALU.add, op1=ALU.max,
                            accum_out=row_max[:, b, g:g + 1]).then_inc(s_read, 1)
                    dve.wait_ge(s_read, 8 * q + 4 * b + 6)
                    dve.tensor_scalar(exp_bias[:, b, :], row_max[:, b, :], -SCALE, None, ALU.mult
                                      ).then_inc(bias_ready, 1)

            def copy_pt(t, par, b):
                q = 2 * t + par
                dve.wait_ge(pt_full[1], 2 * q + b + 1)
                dve.tensor_copy(probs_t[:, b, 1].rearrange("p g n -> p (g n)"), tr[1][:]).then_inc(pt_done[1], 1)

            def norm_stats(t):
                dve.wait_ge(x_in, 16 * t + 16)
                chain.step(dve.bn_stats(stats[:], x_raw[:]))
                chain.wait()
                stand_alone(dve, passed_dve)
                dve.bn_aggr(mean_var[:], stats[:]).then_inc(var_ready, 1)

            def norm_apply(t):
                dve.wait_ge(rstd_ready, t + 1)
                dve.tensor_scalar(x_hat[:], x_raw[:], mean_var[:, 0:1], rstd[:, 0:1], ALU.subtract, ALU.mult
                                  ).then_inc(x_hat_ready, 1)

            def low_xt(t):
                dve.wait_ge(xt_hi, t + 1)
                dve.tensor_tensor(x_t[1][:].rearrange("p c n -> p (c n)"), tr[0][:],
                                  x_t[0][:].rearrange("p c n -> p (c n)").bitcast(F32), ALU.subtract
                                  ).then_inc(xt_lo, 1)

            def copy_q_rows(t):
                dve.wait_ge(q_full, t + 1)
                dve.tensor_copy(q_sb[:], tr[1][:]).then_inc(q_copied, 1)

            def copy_q(t):
                dve.wait_ge(qt_full, t + 1)
                for a in (2, 3):
                    rows = slice(32 * a, 32 * a + 32)
                    last = dve.tensor_copy(q_diag[rows, :, rows],
                                           tr[0][rows, :].rearrange("p (n i) -> p n i", i=SEQ))
                last.then_inc(q_diag_ready, 1)

            def finish_heads(t, par):
                q = 2 * t + par
                dve.wait_ge(exp_done, 2 * q + 2)
                chain.step(dve.reciprocal(r_denom[:], denom[:].rearrange("p b g -> p (b g)")))
                chain.step(dve.tensor_tensor(
                    last_part[:], probs[:, :, :, MAIN].rearrange("p b g -> p (b g)").unsqueeze(2).to_broadcast([P, 8, HD]),
                    v_last_all[:, bass.ds(2 * q, 2), :].rearrange("p b (g d) -> p (b g) d", g=4), ALU.mult))
                chain.wait()
                dve.wait_ge(pv_full, 2 * q + 2)
                for b in range(2):
                    for a in range(4):
                        rows = slice(32 * a, 32 * a + 32)
                        part = dve.tensor_tensor(
                            heads[rows, 4 * b:4 * b + 4, :],
                            out_bank[b][rows, :].rearrange("p (g n) -> p g n", g=4)[:, :, rows],
                            last_part[rows, 4 * b:4 * b + 4, :], ALU.add)
                part.then_inc(pv_read, 1)
                dve.wait_ge(pv_read, q + 1)
                chain.step(dve.tensor_tensor(heads[:], heads[:], r_denom[:].unsqueeze(2).to_broadcast([P, 8, HD]), ALU.mult))
                chain.wait()
                wait(dve, heads_out[par], 16 * t)
                dve.transpose(heads_t[par][:], heads[:].rearrange("p n d -> p (n d)")).then_inc(heads_ready, 1)

            dve.memset(stats[:], 0.0).then_inc(s_read, 1)
            dve.memset(mean_var[:], 0.0).then_inc(s_read, 1)
            dve.wait_ge(s_read, 2)
            for n, (raw, parts) in enumerate(((wk_raw, wk_s), (last_raw, last_s), (wv_raw, wv_s), (wq_raw, wq_s))):
                dve.wait_ge(w_hi, n + 1)
                cols = NB if n == 1 else D
                dve.tensor_tensor(parts[1][:, :, 0:cols], raw[:], parts[0][:, :, 0:cols].bitcast(F32), ALU.subtract
                                  ).then_inc(w_lo, 1)
                if n == 1:
                    norm_stats(0)
            norm_apply(0)
            dve.wait_ge(last_k_full, 1)
            dve.tensor_copy(k_last[:], proj[0][:].rearrange("p (g n) -> p g n", g=4)[:, :, 0:NB]
                            ).then_inc(last_k_done, 1)
            dve.wait_ge(last_k_done, 1)
            low_xt(0)
            copy_k(0, 0, 0)
            copy_q_rows(0)
            copy_k(0, 0, 1)
            last_key(0, 0)
            dve.wait_ge(diag_zero, 1)
            copy_q(0)
            copy_v(0, 0, 0)
            copy_v(0, 0, 1)
            dve.wait_ge(vlast_in, 64)

            def even_pair(t, more):
                mask_max(t, 0)
                copy_k(t, 1, 0)
                if more:
                    norm_stats(t + 1)
                copy_k(t, 1, 1)
                last_key(t, 1)
                copy_pt(t, 0, 0)
                copy_pt(t, 0, 1)
                if more:
                    norm_apply(t + 1)
                copy_v(t, 1, 0)
                copy_v(t, 1, 1)
                finish_heads(t, 0)

            chain.enter(0, 7)
            with dve.Fori(0, TILES - 1) as t:
                chain.base = chain.before + 7 * t
                even_pair(t, True)
                mask_max(t, 1)
                low_xt(t + 1)
                copy_k(t + 1, 0, 0)
                copy_q_rows(t + 1)
                copy_k(t + 1, 0, 1)
                last_key(t + 1, 0)
                copy_q(t + 1)
                copy_pt(t, 1, 0)
                copy_pt(t, 1, 1)
                copy_v(t + 1, 0, 0)
                copy_v(t + 1, 0, 1)
                finish_heads(t, 1)
            chain.leave(TILES - 1)
            even_pair(TILES - 1, False)
            mask_max(TILES - 1, 1)
            copy_pt(TILES - 1, 1, 0)
            copy_pt(TILES - 1, 1, 1)
            finish_heads(TILES - 1, 1)

        @block.tensor
        def _(pe):
            def keys(t, par, js):
                q = 2 * t + par
                pe.wait_ge(ctx_ready, q + 1)
                for j in js:
                    for bank in range(2):
                        g = 2 * j + bank
                        if j == 0:
                            wait(pe, v_done[bank], 2 * q)
                        else:
                            pe.wait_ge(k_done[bank], 2 * q + 1)
                        for c in range(CC):
                            last = product(pe, proj[bank][:], [w[:, c, g * P:(g + 1) * P] for w in wk_s],
                                           [s[:, c, :] for s in ctx_s[par]], c == 0, c == CC - 1)
                        last.then_inc(k_full[bank], 1)

            def values(t, par):
                q = 2 * t + par
                for b in range(2):
                    for bank in range(2):
                        if b == 0:
                            pe.wait_ge(k_done[bank], 2 * q + 2)
                        else:
                            pe.wait_ge(v_done[bank], 2 * q + 1)
                        at = slice(MAIN * b + P * bank, MAIN * b + P * bank + P)
                        for c in range(CC):
                            last = product(pe, proj[bank][:], [s[:, c, at] for s in ctx_s[par]],
                                           [w[:, c, :] for w in wv_s], c == 0, c == CC - 1)
                        last.then_inc(v_full[bank], 1)

            def scores(t, par):
                q = 2 * t + par
                for bank in range(2):
                    pe.wait_ge(k_done[bank], 2 * q + 2)
                pe.wait_ge(k_last_ready, q + 1)
                pe.wait_ge(q_diag_ready, 2 * t + 2)
                for b in range(2):
                    for g in range(KC):
                        pe.wait_ge(s_read, 8 * q + 4 * b + g + 1)
                        pe.matmul(score_bank[g % 2][:, 0:KEYS], q_diag[:, 4 * g + 2 * par + b, :],
                                  k_t[par][:, g, b, 0:KEYS], start=True, stop=True).then_inc(s_full, 1)

            def transpose_x(t):
                pe.wait_ge(x_hat_ready, t + 1)
                wait(pe, pt_done[0], 4 * t - 2)
                for c in range(KC):
                    last = pe.transpose(tr[0][:, c * P:(c + 1) * P], x_hat[:, c * P:(c + 1) * P], ident[:])
                last.then_inc(xt_full, 1)

            def queries(t):
                pe.wait_ge(xt_lo, t + 1)
                wait(pe, pt_done[1], 4 * t - 2)
                for c in range(KC):
                    last = product(pe, tr[1][:], [s[:, c, :] for s in x_t], [w[:, c, :] for w in wq_s],
                                   c == 0, c == KC - 1)
                last.then_inc(q_full, 1)

            def transpose_q(t):
                pe.wait_ge(q_copied, t + 1)
                for g in range(KC):
                    last = pe.transpose(tr[0][:, g * P:(g + 1) * P], q_sb[:, g * P:(g + 1) * P], ident[:])
                last.then_inc(qt_full, 1)

            def transpose_probs(t, par):
                q = 2 * t + par
                for b in range(2):
                    pe.wait_ge(exp_done, 2 * q + b + 1)
                    for c in range(2):
                        wait(pe, pt_done[c], 2 * q + b)
                        for g in range(KC):
                            last = pe.transpose(tr[c][:, g * P:(g + 1) * P], probs[:, b, g, c * P:(c + 1) * P], ident[:])
                        last.then_inc(pt_full[c], 1)

            def attend(t, par):
                q = 2 * t + par
                for bank in range(2):
                    pe.wait_ge(v_done[bank], 2 * q + 2)
                wait(pe, pv_read, q)
                for b in range(2):
                    for c in range(2):
                        pe.wait_ge(pt_done[c], 2 * q + b + 1)
                    for g in range(KC):
                        for c in range(2):
                            last = pe.matmul(out_bank[b][:, g * P:(g + 1) * P], probs_t[:, b, c, g, :],
                                             v_sb[par][:, b, c, g * P:(g + 1) * P], start=c == 0, stop=c == 1)
                    last.then_inc(pv_full, 1)

            pe.wait_ge(ident_ready, 1)
            pe.wait_ge(w_lo, 2)
            for g in range(KC):
                for c in range(CC):
                    last = product(pe, proj[0][:, g * P:(g + 1) * P], [w[:, c, g * P:(g + 1) * P] for w in wk_s],
                                   [s[:, c, :] for s in last_s], c == 0, c == CC - 1)
            last.then_inc(last_k_full, 1)
            pe.wait_ge(w_lo, 3)
            for c in range(CC):
                last = product(pe, proj[1][:], [s[:, c, :] for s in last_s], [w[:, c, :] for w in wv_s],
                               c == 0, c == CC - 1)
            last.then_inc(last_v_full, 1)
            transpose_x(0)
            pe.wait_ge(last_k_done, 1)
            pe.wait_ge(last_v_done, 1)
            keys(0, 0, (0,))
            pe.wait_ge(w_lo, 4)
            queries(0)
            keys(0, 0, (1,))
            transpose_q(0)
            values(0, 0)

            def even_pair(t):
                scores(t, 0)
                keys(t, 1, (0, 1))
                transpose_probs(t, 0)
                values(t, 1)
                attend(t, 0)

            with pe.Fori(0, TILES - 1) as t:
                even_pair(t)
                scores(t, 1)
                transpose_x(t + 1)
                keys(t + 1, 0, (0,))
                queries(t + 1)
                keys(t + 1, 0, (1,))
                transpose_q(t + 1)
                pe.wait_ge(q_diag_ready, 2 * t + 4)
                transpose_probs(t, 1)
                values(t + 1, 0)
                attend(t, 1)
            even_pair(TILES - 1)
            scores(TILES - 1, 1)
            transpose_probs(TILES - 1, 1)
            attend(TILES - 1, 1)


def rest_of_layer(nc, banks, ident, x, heads_dram, units, gate, n1, n2, bo, out):
    x_halves = x.rearrange("(h t p) d -> h p t d", h=HALVES, p=P)
    out_halves = out.rearrange("(h t p) d -> h p t d", h=HALVES, p=P)
    heads_halves = heads_dram.rearrange("(h q) p n -> h p q n", h=HALVES)
    with ExitStack() as stack:
        def sb(name, shape, dt=F32):
            return stack.enter_context(nc.sbuf_tensor(name, shape, dt))

        def sem(name):
            return stack.enter_context(nc.semaphore(name))

        def split_pair(name, shape):
            return sb(name + "_hi", shape, F32R), sb(name + "_lo", shape, F32R)

        proj = [banks["proj0"], banks["proj1"]]
        tr = [banks["tr0"], banks["tr1"]]
        score_bank = [banks["s0"], banks["s1"]]
        out_bank = [banks["o0"], banks["o1"]]
        down_bank = score_bank + out_bank
        gate_bank, gate_t_bank = score_bank

        unit_raw = [sb(f"unit_raw{i}", [P, 2, D]) for i in range(2)]
        unit_s = [split_pair(f"unit{i}", [P, KC, D]) for i in range(RING)]
        res = sb("res", [P, HT, D])
        y = sb("y", [P, HT, D])
        heads_s = split_pair("heads_s", [P, KC, HALF])
        xt_s = split_pair("xt_s", [P, KC, HALF])
        x_hat = [sb(f"c_x_hat{i}", [P, D]) for i in range(2)]
        q_t = [sb(f"q_t{i}", [P, HALF]) for i in range(2)]
        k_diag = [sb(f"k_diag{i}", [P, 16, P]) for i in range(2)]
        v_tok = sb("v_tok", [P, HT, D])
        masked = sb("masked", [P, 16, SEQ])
        pr = sb("pr", [P, 16, SEQ])
        pt_diag = [sb(f"pt_diag{i}", [P, 16, P]) for i in range(2)]
        causal = sb("causal", [P, SEQ])
        act_buf = [sb(f"act_buf{i}", [P, HALF]) for i in range(2)]
        h_s = split_pair("h_s", [P, 8, HALF])
        gate_raw = sb("gate_raw", [P, KC, NE])
        gate_s = split_pair("gate_s", [P, KC, P])
        logits = sb("logits", [NE, HALF])
        n1_all, n2_all, bo_all = sb("n1_all", [P, D]), sb("n2_all", [P, D]), sb("bo_all", [P, D])
        minus_half = sb("c_minus_half", [P, 1])
        stats = sb("c_stats", [P, HT, 6])
        mean_var = sb("c_mean_var", [P, HT, 2])
        square_sum = sb("square_sum", [P, HT])
        root_in = sb("root_in", [P, 2, HT])
        rstd = sb("c_rstd", [P, 2, HT])
        row_max = sb("c_row_max", [P, 16])
        den = sb("c_den", [P, 16])
        r_den = sb("c_r_den", [P, 16])
        top = sb("top", [P, HT, NE])
        g_small = sb("g_small", [P, 5, HT])
        weight = sb("weight", [P, HT])

        passed_pool, passed_dve, passed_pe = sem("c_passed_pool"), sem("c_passed_dve"), sem("c_passed_pe")
        passed_sp = sem("c_passed_sp")
        const_in, gate_in = sem("const_in"), sem("gate_in")
        const_ready, gate_ready = sem("const_ready"), sem("gate_ready")
        unit_in = [sem(f"unit_in{i}") for i in range(2)]
        unit_ready, down_half = sem("unit_ready"), sem("down_half")
        x_in, heads_in = sem("c_x_in"), sem("c_heads_in")
        pool_step, dve_step = sem("c_pool_step"), sem("c_dve_step")
        p_full = [sem(f"p_full{i}") for i in range(2)]
        p_free = [sem(f"p_free{i}") for i in range(2)]
        t_full = [sem(f"t_full{i}") for i in range(2)]
        t_hi, x_hat_ready = sem("t_hi"), sem("c_x_hat_ready")
        t_free = [sem(f"t_free{i}") for i in range(2)]
        heads_hi, heads_lo = sem("heads_hi"), sem("heads_lo")
        sc_full = [sem(f"sc_full{i}") for i in range(2)]
        at_full = [sem(f"at_full{i}") for i in range(2)]
        shifted, exp_ready, pt_ready = sem("shifted"), sem("exp_ready"), sem("pt_ready")
        var_ready, rstd_ready = sem("c_var_ready"), sem("c_rstd_ready")
        y_ready, square_ready, rms_ready = sem("y_ready"), sem("square_ready"), sem("rms_ready")
        gate_full, logits_ready, gate_t_full = sem("gate_full"), sem("logits_ready"), sem("gate_t_full")
        top_ready, top_exp, weight_ready = sem("top_ready"), sem("top_exp"), sem("weight_ready")
        tanh_ready, silu_ready, h_hi, h_lo = sem("tanh_ready"), sem("silu_ready"), sem("h_hi"), sem("h_lo")
        down_full, down_read, final, stored = sem("down_full"), sem("down_read"), sem("final"), sem("stored")

        def proj_full(n, h):
            return p_full[n % 2], USES * h + n // 2 + 1

        def proj_free(n, h):
            return p_free[n % 2], FREES * h + n // 2

        def unit_used(u, h):
            last_use = {0: 3, 1: 7, 2: 14, 3: 15, 4: 19, 5: 23, 6: 30, 7: 31, 8: 35, 9: 39, 10: 43, 13: 47, 14: 51}
            if u in last_use:
                return proj_full(last_use[u], h)
            if u in (11, 15):
                return down_half, 2 * h + (1 if u == 11 else 2)
            return down_full, 8 * h + (4 if u == 12 else 8)

        block = stack.enter_context(nc.Block())

        @block.sync
        def _(sp):
            def load_unit(h, u):
                for v in range(2):
                    wait(sp, unit_ready, 2 * NU * h + (2 * u + v - 1 if u else 0))
                    sp.dma_start(unit_raw[v][:], units[u, :, 2 * v:2 * v + 2, :]).then_inc(unit_in[v], 16)

            sp.dma_start(gate_raw[:], gate).then_inc(gate_in, 16)
            for row, vector in ((n1_all, n1), (n2_all, n2), (bo_all, bo)):
                sp.dma_start(row[:], vector.unsqueeze(0).to_broadcast([P, D])).then_inc(const_in, 16)
            with sp.Fori(0, HALVES) as h:
                load_unit(h, 0)
                sp.wait_ge(stored, 64 * h)
                stand_alone(sp, passed_sp)
                sp.dma_start(y[:].rearrange("p t d -> p (t d)").rearrange("p (q n) -> p q n", q=HPAIRS),
                             heads_halves[bass.ds(h, 1)].rearrange("o p q n -> (o p) q n")).then_inc(heads_in, 16)
                sp.wait_ge(final, 4 * h)
                stand_alone(sp, passed_sp)
                sp.dma_start(res[:], x_halves[bass.ds(h, 1)].rearrange("o p t d -> (o p) t d")).then_inc(x_in, 16)
                for u in range(1, NU):
                    load_unit(h, u)

        @block.gpsimd
        def _(pool):
            chain = Chain(pool, pool_step)

            def split_unit(h, u):
                hi, lo = unit_s[u % RING]
                if u >= RING:
                    used, count = unit_used(u - RING, h)
                else:
                    used, count = ((down_half, 2 * h), (down_full, 8 * h), (p_full[1], USES * h))[u]
                pool.wait_ge(used, count)
                for v in range(2):
                    pool.wait_ge(unit_in[v], 16 * (NU * h + u + 1))
                    stand_alone(pool, passed_pool)
                    at = slice(2 * v, 2 * v + 2)
                    chain.step(pool.tensor_scalar(hi[:, at, :], unit_raw[v][:], 1.0, None, ALU.mult))
                    chain.wait()
                    pool.tensor_tensor(lo[:, at, :], unit_raw[v][:], hi[:, at, :].bitcast(F32), ALU.subtract
                                       ).then_inc(unit_ready, 1)

            def root_var(h, stage, t):
                pool.wait_ge(var_ready, 8 * h + 4 * stage + t + 1)
                stand_alone(pool, passed_pool)
                chain.step(pool.tensor_scalar(root_in[:, 0, t:t + 1], mean_var[:, t, 1:2], LN_EPS, None, ALU.add))
                chain.wait()
                pool.tensor_tensor(rstd[:, 0, t:t + 1], root_in[:, 0, t:t + 1], minus_half[:], ALU.pow
                                   ).then_inc(rstd_ready, 1)

            def root_square(h, stage, t):
                pool.wait_ge(square_ready, 8 * h + 4 * (stage - 1) + t + 1)
                stand_alone(pool, passed_pool)
                chain.step(pool.tensor_scalar(root_in[:, 1, t:t + 1], square_sum[:, t:t + 1], 1.0 / D, RMS_EPS,
                                              ALU.mult, ALU.add))
                chain.wait()
                pool.tensor_tensor(rstd[:, 1, t:t + 1], root_in[:, 1, t:t + 1], minus_half[:], ALU.pow
                                   ).then_inc(rms_ready, 1)

            chain.step(pool.memset(minus_half[:], -0.5))
            for part in gate_s:
                pool.memset(part[:].bitcast(F32), 0.0).then_inc(const_ready, 1)
            for i in range(2):
                pool.memset(k_diag[i][:], 0.0).then_inc(const_ready, 1)
            chain.step(pool.memset(causal[:], 0.0))
            chain.wait()
            for b in range(4):
                rows = slice(32 * b, 32 * b + 32)
                pool.affine_select(out=causal[rows, :], in_=causal[rows, :], compare_op=ALU.is_ge, fill=-BIG,
                                   base=0, pattern=[[-1, SEQ]], channel_multiplier=1).then_inc(const_ready, 1)
                pool.wait_ge(const_ready, 5 + b)
            for i in range(2):
                pool.memset(pt_diag[i][:], 0.0).then_inc(const_ready, 1)
            per = 2 * NU + 16
            chain.enter(0, per)
            with pool.Fori(0, HALVES) as h:
                chain.base = chain.before + per * h
                split_unit(h, 0)
                split_unit(h, 1)
                for t in range(HT):
                    root_var(h, 0, t)
                for u in range(2, 6):
                    split_unit(h, u)
                root_var(h, 1, 0)
                root_var(h, 1, 1)
                root_square(h, 1, 0)
                root_var(h, 1, 2)
                root_square(h, 1, 1)
                root_var(h, 1, 3)
                root_square(h, 1, 2)
                root_square(h, 1, 3)
                for u in range(6, 10):
                    split_unit(h, u)
                for t in range(HT):
                    root_square(h, 2, t)
                for u in range(10, NU):
                    split_unit(h, u)
            chain.leave(HALVES)

        @block.scalar
        def _(act):
            def high_xt(h, stage, t):
                n = 4 * stage + t
                act.wait_ge(t_full[n % 2], 6 * h + n // 2 + 1)
                act.activation(xt_s[0][:, :, t * P:(t + 1) * P],
                               tr[n % 2][:].rearrange("p (c n) -> p c n", c=KC), ACT.Copy).then_inc(t_hi, 1)

            def copy_v(h, layer, t):
                n = USE_V[layer] + t
                act.wait_ge(*proj_full(n, h))
                act.activation(v_tok[:, t, :], proj[n % 2][:], ACT.Copy).then_inc(p_free[n % 2], 1)

            def copy_kq(h, layer, m):
                n = USE_KQ[layer] + 2 * m
                act.wait_ge(*proj_full(n, h))
                for a in range(4):
                    rows = slice(32 * a, 32 * a + 32)
                    last = act.activation(k_diag[m % 2][rows, :, rows],
                                          proj[0][rows, :].rearrange("p (n j) -> p n j", j=SEQ), ACT.Copy)
                last.then_inc(p_free[0], 1)
                act.wait_ge(*proj_full(n + 1, h))
                act.activation(q_t[m % 2][:], proj[1][:], ACT.Copy).then_inc(p_free[1], 1)

            def exp(h, layer, m):
                act.wait_ge(shifted, 8 * h + 4 * layer + m + 1)
                act.activation(pr[:], pr[:], ACT.Exp, scale=SCALE).then_inc(exp_ready, 1)

            def high_heads(h, layer, m):
                n = 4 * layer + m
                act.wait_ge(at_full[n % 2], 4 * h + n // 2 + 1)
                act.activation(heads_s[0][:, m, :], out_bank[n % 2][:], ACT.Copy).then_inc(heads_hi, 1)

            def square(h, stage, t):
                if stage == 1:
                    act.wait_ge(y_ready, 4 * h + t + 1)
                else:
                    act.wait_ge(p_free[t % 2], FREES * h + (USE_WO[2] + t) // 2 + 1)
                act.wait_ge(square_ready, 8 * h + 4 * (stage - 1) + t)
                act.activation(act_buf[0][:], y[:, t, :], ACT.Square, accum_out=square_sum[:, t:t + 1]
                               ).then_inc(square_ready, 1)

            def attention(h, layer):
                for m in range(KC):
                    copy_kq(h, layer, m)
                    if m >= 1:
                        exp(h, layer, m - 1)
                    if m >= 2:
                        high_heads(h, layer, m - 2)
                exp(h, layer, 3)
                high_heads(h, layer, 2)
                high_heads(h, layer, 3)

            act.wait_ge(gate_in, 16)
            act.wait_ge(const_ready, 2)
            act.activation(gate_s[0][:, :, 0:NE], gate_raw[:], ACT.Copy).then_inc(gate_ready, 1)
            act.wait_ge(const_ready, 4)
            with act.Fori(0, HALVES) as h:
                act.wait_ge(heads_in, 16 * h + 16)
                act.activation(heads_s[0][:].rearrange("p g (n i) -> p g n i", i=SEQ),
                               y[:].rearrange("p t d -> p (t d)").rearrange("p (n g i) -> p g n i", g=4, i=SEQ),
                               ACT.Copy).then_inc(heads_hi, 1)
                for t in (0, 1, 2):
                    high_xt(h, 0, t)
                copy_v(h, 0, 0)
                copy_v(h, 0, 1)
                high_xt(h, 0, 3)
                copy_v(h, 0, 2)
                copy_v(h, 0, 3)
                attention(h, 0)
                square(h, 1, 0)
                square(h, 1, 1)
                high_xt(h, 1, 0)
                square(h, 1, 2)
                high_xt(h, 1, 1)
                copy_v(h, 1, 0)
                square(h, 1, 3)
                high_xt(h, 1, 2)
                copy_v(h, 1, 1)
                high_xt(h, 1, 3)
                copy_v(h, 1, 2)
                copy_v(h, 1, 3)
                attention(h, 1)
                square(h, 2, 0)
                square(h, 2, 1)
                high_xt(h, 2, 0)
                square(h, 2, 2)
                high_xt(h, 2, 1)
                square(h, 2, 3)
                high_xt(h, 2, 2)
                high_xt(h, 2, 3)
                act.wait_ge(gate_full, h + 1)
                act.activation(logits[:], gate_bank[0:NE, :], ACT.Copy).then_inc(logits_ready, 1)
                for f in range(2):
                    for j in range(9):
                        if j < 8:
                            n = USE_UP[f] + j
                            act.wait_ge(*proj_full(n, h))
                            if j >= 2:
                                act.wait_ge(h_lo, 16 * h + 8 * f + j - 1)
                            act.activation(act_buf[j % 2][:], proj[n % 2][:], ACT.Tanh, scale=0.5
                                           ).then_inc(tanh_ready, 1)
                        if j:
                            act.wait_ge(silu_ready, 16 * h + 8 * f + j)
                            act.activation(h_s[0][:, j - 1, :], act_buf[(j - 1) % 2][:], ACT.Copy, scale=0.5
                                           ).then_inc(h_hi, 1)
                        if f == 0 and j == 2:
                            act.wait_ge(top_ready, h + 1)
                            act.activation(top[:], top[:], ACT.Exp).then_inc(top_exp, 1)
                for t in range(HT):
                    act.wait_ge(final, 4 * h + t + 1)
                    act.dma_start(out_halves[bass.ds(h, 1), :, t, :].rearrange("o p d -> (o p) d"), y[:, t, :]
                                  ).then_inc(stored, 16)
            act.wait_ge(stored, 64 * HALVES)

        @block.vector
        def _(dve):
            chain = Chain(dve, dve_step)

            def low_xt(h, stage, t):
                n = 4 * stage + t
                at = slice(t * P, (t + 1) * P)
                dve.wait_ge(t_hi, 12 * h + n + 1)
                dve.tensor_tensor(xt_s[1][:, :, at], tr[n % 2][:].rearrange("p (c n) -> p c n", c=KC),
                                  xt_s[0][:, :, at].bitcast(F32), ALU.subtract).then_inc(t_free[n % 2], 1)

            def low_heads(h, layer, m):
                n = 4 * layer + m
                dve.wait_ge(heads_hi, 9 * h + 1 + n + 1)
                dve.tensor_tensor(heads_s[1][:, m, :], out_bank[n % 2][:], heads_s[0][:, m, :].bitcast(F32),
                                  ALU.subtract).then_inc(heads_lo, 1)

            def add_res(h, stage, t):
                n = USE_WO[stage] + t
                row = y[:, t, :] if stage == 2 else res[:, t, :]
                dve.wait_ge(*proj_full(n, h))
                dve.tensor_tensor(row, proj[n % 2][:], row, ALU.add).then_inc(p_free[n % 2], 1)
                if stage < 2:
                    dve.wait_ge(p_free[n % 2], FREES * h + n // 2 + 1)
                    chain.step(dve.bn_stats(stats[:, t, :], row))
                    chain.wait()
                    stand_alone(dve, passed_dve)
                    dve.bn_aggr(mean_var[:, t, :], stats[:, t, :]).then_inc(var_ready, 1)

            def layer_norm(h, stage, t):
                dve.wait_ge(rstd_ready, 8 * h + 4 * stage + t + 1)
                if stage == 0:
                    dve.tensor_scalar(x_hat[t % 2][:], res[:, t, :], mean_var[:, t, 0:1], rstd[:, 0, t:t + 1],
                                      ALU.subtract, ALU.mult).then_inc(x_hat_ready, 1)
                    chain.step(dve.tensor_tensor(res[:, t, :], res[:, t, :], bo_all[:], ALU.add))
                else:
                    dve.tensor_scalar(y[:, t, :], res[:, t, :], mean_var[:, t, 0:1], rstd[:, 0, t:t + 1],
                                      ALU.subtract, ALU.mult).then_inc(y_ready, 1)

            def rms_norm(h, stage, t):
                dve.wait_ge(rms_ready, 8 * h + 4 * (stage - 1) + t + 1)
                dve.scalar_tensor_tensor(x_hat[t % 2][:], y[:, t, :], rstd[:, 1, t:t + 1],
                                         (n1_all if stage == 1 else n2_all)[:], ALU.mult, ALU.mult
                                         ).then_inc(x_hat_ready, 1)

            def softmax(h, layer, m):
                n = 4 * layer + m
                bank = score_bank[n % 2][:].rearrange("p (n j) -> p n j", j=SEQ)
                dve.wait_ge(sc_full[n % 2], 4 * h + n // 2 + 1)
                if layer == 1:
                    chain.step(dve.tensor_tensor(masked[:], bank, causal[:].unsqueeze(1).to_broadcast([P, 16, SEQ]), ALU.add))
                    chain.wait()
                    bank = masked[:]
                chain.step(dve.tensor_reduce(row_max[:], bank, AX.X, ALU.max))
                chain.wait()
                dve.tensor_tensor(pr[:], bank, row_max[:].unsqueeze(2).to_broadcast([P, 16, SEQ]), ALU.subtract
                                  ).then_inc(shifted, 1)

            def softmax_end(h, layer, m):
                n = 4 * layer + m
                dve.wait_ge(exp_ready, 8 * h + n + 1)
                chain.step(dve.tensor_reduce(den[:], pr[:], AX.X, ALU.add))
                chain.wait()
                if layer == 0:
                    chain.step(dve.tensor_scalar(den[:], den[:], DEN_EPS, None, ALU.add))
                    chain.wait()
                chain.step(dve.reciprocal(r_den[:], den[:]))
                chain.wait()
                chain.step(dve.tensor_tensor(pr[:], pr[:], r_den[:].unsqueeze(2).to_broadcast([P, 16, SEQ]), ALU.mult))
                chain.wait()
                for b in range(4):
                    rows = slice(32 * b, 32 * b + 32)
                    last = dve.transpose(pt_diag[m % 2][rows, :, rows], pr[rows])
                last.then_inc(pt_ready, 1)

            def attention(h, layer):
                for m in range(KC):
                    softmax(h, layer, m)
                    softmax_end(h, layer, m)
                    if m:
                        low_heads(h, layer, m - 1)
                low_heads(h, layer, 3)

            def gate_top(h):
                dve.wait_ge(gate_t_full, h + 1)
                stand_alone(dve, passed_dve)
                for t in range(HT):
                    chain.step(dve.max(top[:, t, :], gate_t_bank[:, t * NE:(t + 1) * NE]))
                chain.wait()
                chain.step(dve.tensor_copy(g_small[:, 0, :], top[:, :, 0]))
                chain.wait()
                dve.tensor_tensor(top[:], top[:], g_small[:, 0, :].unsqueeze(2).to_broadcast([P, HT, NE]),
                                  ALU.subtract).then_inc(top_ready, 1)

            def gate_weight(h):
                dve.wait_ge(top_exp, h + 1)
                chain.step(dve.tensor_reduce(g_small[:, 1, :], top[:], AX.X, ALU.add))
                chain.step(dve.tensor_tensor(g_small[:, 2, :], top[:, :, 0], top[:, :, 1], ALU.add))
                chain.wait()
                chain.step(dve.reciprocal(g_small[:, 3, :], g_small[:, 1, :]))
                chain.wait()
                chain.step(dve.tensor_tensor(g_small[:, 2, :], g_small[:, 2, :], g_small[:, 3, :], ALU.mult))
                chain.wait()
                chain.step(dve.tensor_scalar(g_small[:, 4, :], g_small[:, 2, :], TOPK_EPS, None, ALU.add))
                chain.wait()
                chain.step(dve.reciprocal(g_small[:, 3, :], g_small[:, 4, :]))
                chain.wait()
                dve.tensor_tensor(weight[:], g_small[:, 2, :], g_small[:, 3, :], ALU.mult).then_inc(weight_ready, 1)

            def silu(h, f, j):
                k = 8 * f + j
                dve.wait_ge(tanh_ready, 16 * h + k + 1)
                n = USE_UP[f] + j
                dve.scalar_tensor_tensor(act_buf[j % 2][:], act_buf[j % 2][:], 1.0, proj[n % 2][:], ALU.add, ALU.mult
                                         ).then_inc(silu_ready, 1)

            def low_h(h, f, j):
                k = 8 * f + j
                dve.wait_ge(h_hi, 16 * h + k + 1)
                dve.scalar_tensor_tensor(h_s[1][:, j, :], act_buf[j % 2][:], 0.5, h_s[0][:, j, :].bitcast(F32),
                                         ALU.mult, ALU.subtract).then_inc(h_lo, 1)

            def add_down(h, f, t):
                dve.wait_ge(down_full, 8 * h + 4 * f + t + 1)
                dve.scalar_tensor_tensor(y[:, t, :], down_bank[t][:], weight[:, t:t + 1], y[:, t, :],
                                         ALU.mult, ALU.add).then_inc(down_read, 1)

            dve.wait_ge(const_in, 48)
            dve.wait_ge(gate_ready, 1)
            dve.tensor_tensor(gate_s[1][:, :, 0:NE], gate_raw[:], gate_s[0][:, :, 0:NE].bitcast(F32), ALU.subtract
                              ).then_inc(gate_ready, 1)
            dve.wait_ge(const_ready, 10)
            per = 63
            chain.enter(0, per)
            with dve.Fori(0, HALVES) as h:
                chain.base = chain.before + per * h
                dve.wait_ge(heads_hi, 9 * h + 1)
                dve.tensor_tensor(heads_s[1][:].rearrange("p g (n i) -> p g n i", i=SEQ),
                                  y[:].rearrange("p t d -> p (t d)").rearrange("p (n g i) -> p g n i", g=4, i=SEQ),
                                  heads_s[0][:].rearrange("p g (n i) -> p g n i", i=SEQ).bitcast(F32),
                                  ALU.subtract).then_inc(heads_lo, 1)
                dve.wait_ge(x_in, 16 * h + 16)
                for t in range(HT):
                    add_res(h, 0, t)
                    if t >= 1:
                        layer_norm(h, 0, t - 1)
                    if t >= 2:
                        low_xt(h, 0, t - 2)
                layer_norm(h, 0, 3)
                low_xt(h, 0, 2)
                low_xt(h, 0, 3)
                attention(h, 0)
                chain.wait()
                add_res(h, 1, 0)
                add_res(h, 1, 1)
                layer_norm(h, 1, 0)
                add_res(h, 1, 2)
                layer_norm(h, 1, 1)
                rms_norm(h, 1, 0)
                add_res(h, 1, 3)
                layer_norm(h, 1, 2)
                rms_norm(h, 1, 1)
                low_xt(h, 1, 0)
                layer_norm(h, 1, 3)
                rms_norm(h, 1, 2)
                low_xt(h, 1, 1)
                rms_norm(h, 1, 3)
                low_xt(h, 1, 2)
                low_xt(h, 1, 3)
                attention(h, 1)
                add_res(h, 2, 0)
                for t in range(HT):
                    if t < 3:
                        add_res(h, 2, t + 1)
                    rms_norm(h, 2, t)
                    if t >= 1:
                        low_xt(h, 2, t - 1)
                low_xt(h, 2, 3)
                gate_top(h)
                for f in range(2):
                    for j in range(9):
                        if j < 8:
                            silu(h, f, j)
                        if j:
                            low_h(h, f, j - 1)
                        if f == 0 and j == 2:
                            gate_weight(h)
                            dve.wait_ge(weight_ready, h + 1)
                    for t in range(HT):
                        add_down(h, f, t)
                        if f == 1:
                            dve.wait_ge(down_read, 8 * h + 4 * f + t + 1)
                            dve.tensor_tensor(y[:, t, :], y[:, t, :], res[:, t, :], ALU.add).then_inc(final, 1)
            chain.leave(HALVES)

        @block.tensor
        def _(pe):
            def project(h, stage, t):
                n = USE_WO[stage] + t
                w = unit_s[(0, 4, 8)[stage] % RING]
                if t == 0:
                    pe.wait_ge(heads_lo, 9 * h + (1, 5, 9)[stage])
                    pe.wait_ge(unit_ready, 2 * NU * h + 2 * (0, 4, 8)[stage] + 2)
                    if stage == 0:
                        pe.wait_ge(silu_ready, 16 * h)
                pe.wait_ge(*proj_free(n, h))
                for c in range(KC):
                    last = product(pe, proj[n % 2][:], [s[:, c, t * P:(t + 1) * P] for s in heads_s],
                                   [s[:, c, :] for s in w], c == 0, c == KC - 1)
                last.then_inc(p_full[n % 2], 1)

            def transpose_x(h, stage, t):
                n = 4 * stage + t
                pe.wait_ge(x_hat_ready, 12 * h + n + 1)
                pe.wait_ge(t_free[n % 2], 6 * h + n // 2)
                for c in range(KC):
                    last = pe.transpose(tr[n % 2][:, c * P:(c + 1) * P], x_hat[n % 2][:, c * P:(c + 1) * P], ident[:])
                last.then_inc(t_full[n % 2], 1)

            def values(h, layer, t):
                n = USE_V[layer] + t
                u = (1, 5)[layer]
                if t == 0:
                    pe.wait_ge(unit_ready, 2 * NU * h + 2 * u + 2)
                pe.wait_ge(t_free[t % 2], 6 * h + (4 * layer + t) // 2 + 1)
                pe.wait_ge(*proj_free(n, h))
                for c in range(KC):
                    last = product(pe, proj[n % 2][:], [s[:, c, t * P:(t + 1) * P] for s in xt_s],
                                   [s[:, c, :] for s in unit_s[u % RING]], c == 0, c == KC - 1)
                last.then_inc(p_full[n % 2], 1)

            def features(h, u, n, m):
                if m == 0:
                    pe.wait_ge(unit_ready, 2 * NU * h + 2 * u + 2)
                k = n - USE_UP[0]
                if k < 2:
                    pe.wait_ge(*proj_free(n, h))
                else:
                    pe.wait_ge(silu_ready, 16 * h + k - 1)
                for c in range(KC):
                    last = product(pe, proj[n % 2][:], [s[:, c, m * P:(m + 1) * P] for s in unit_s[u % RING]],
                                   [s[:, c, :] for s in xt_s], c == 0, c == KC - 1)
                last.then_inc(p_full[n % 2], 1)

            def keys_queries(h, layer, m):
                u, n = (2, 6)[layer], USE_KQ[layer] + 2 * m
                features(h, u, n, m)
                features(h, u + 1, n + 1, m)

            def scores(h, layer, m):
                n = 4 * layer + m
                k = (USE_KQ[layer] + 2 * m) // 2
                pe.wait_ge(p_free[0], FREES * h + k + 1)
                pe.wait_ge(p_free[1], FREES * h + k + 1)
                if n < 2:
                    pe.wait_ge(down_read, 8 * h)
                else:
                    pe.wait_ge(shifted, 8 * h + n - 1)
                for t in range(HT):
                    for b in range(4):
                        rows = slice(32 * b, 32 * b + 32)
                        last = pe.matmul(score_bank[n % 2][rows, t * P:(t + 1) * P],
                                         q_t[m % 2][:, t * P + 32 * b:t * P + 32 * b + 32],
                                         k_diag[m % 2][:, 4 * t + b, :], start=True, stop=True)
                last.then_inc(sc_full[n % 2], 1)

            def attend(h, layer, m):
                n = 4 * layer + m
                pe.wait_ge(pt_ready, 8 * h + n + 1)
                if n < 2:
                    pe.wait_ge(down_read, 8 * h)
                else:
                    pe.wait_ge(heads_lo, 9 * h + n)
                for t in range(HT):
                    for a in range(4):
                        rows = slice(32 * a, 32 * a + 32)
                        last = pe.matmul(out_bank[n % 2][rows, t * P:(t + 1) * P],
                                         v_tok[:, t, m * P + 32 * a:m * P + 32 * a + 32],
                                         pt_diag[m % 2][:, 4 * t + a, :], start=True, stop=True)
                last.then_inc(at_full[n % 2], 1)

            def attention(h, layer):
                keys_queries(h, layer, 0)
                keys_queries(h, layer, 1)
                scores(h, layer, 0)
                keys_queries(h, layer, 2)
                scores(h, layer, 1)
                attend(h, layer, 0)
                keys_queries(h, layer, 3)
                scores(h, layer, 2)
                attend(h, layer, 1)
                scores(h, layer, 3)
                attend(h, layer, 2)
                attend(h, layer, 3)

            def gate_logits(h):
                for bank in range(2):
                    pe.wait_ge(t_free[bank], 6 * h + 6)
                pe.wait_ge(shifted, 8 * h + 8)
                for c in range(KC):
                    last = product(pe, gate_bank[:], [s[:, c, :] for s in gate_s], [s[:, c, :] for s in xt_s],
                                   c == 0, c == KC - 1)
                last.then_inc(gate_full, 1)

            def gate_transpose(h):
                pe.wait_ge(logits_ready, h + 1)
                stand_alone(pe, passed_pe)
                for t in range(HT):
                    last = pe.transpose(gate_t_bank[:, t * NE:(t + 1) * NE], logits[:, t * P:(t + 1) * P],
                                        ident[0:NE, 0:NE])
                last.then_inc(gate_t_full, 1)

            def down(h, f):
                for d in range(2):
                    u = (11, 15)[f] + d
                    pe.wait_ge(unit_ready, 2 * NU * h + 2 * u + 2)
                    pe.wait_ge(h_lo, 16 * h + 8 * f + 4 * d + 4)
                    for t in range(HT):
                        if d == 0 and f == 0:
                            if t < 2:
                                pe.wait_ge(top_ready, h + 1)
                            else:
                                pe.wait_ge(heads_lo, 9 * h + 9)
                        elif d == 0:
                            pe.wait_ge(down_read, 8 * h + t + 1)
                        for c in range(KC):
                            last = product(pe, down_bank[t][:], [s[:, 4 * d + c, t * P:(t + 1) * P] for s in h_s],
                                           [s[:, c, :] for s in unit_s[u % RING]],
                                           d == 0 and c == 0, d == 1 and c == KC - 1)
                        if d == 1:
                            last.then_inc(down_full, 1)
                        elif t == HT - 1:
                            last.then_inc(down_half, 1)

            pe.wait_ge(gate_ready, 2)
            with pe.Fori(0, HALVES) as h:
                project(h, 0, 0)
                project(h, 0, 1)
                transpose_x(h, 0, 0)
                project(h, 0, 2)
                transpose_x(h, 0, 1)
                project(h, 0, 3)
                transpose_x(h, 0, 2)
                values(h, 0, 0)
                values(h, 0, 1)
                transpose_x(h, 0, 3)
                values(h, 0, 2)
                values(h, 0, 3)
                attention(h, 0)
                for t in range(HT):
                    project(h, 1, t)
                transpose_x(h, 1, 0)
                transpose_x(h, 1, 1)
                values(h, 1, 0)
                transpose_x(h, 1, 2)
                values(h, 1, 1)
                transpose_x(h, 1, 3)
                values(h, 1, 2)
                values(h, 1, 3)
                attention(h, 1)
                project(h, 2, 0)
                project(h, 2, 1)
                transpose_x(h, 2, 0)
                project(h, 2, 2)
                transpose_x(h, 2, 1)
                project(h, 2, 3)
                transpose_x(h, 2, 2)
                transpose_x(h, 2, 3)
                gate_logits(h)
                for f in range(2):
                    for j in range(8):
                        features(h, (9, 13)[f] + j // 4, USE_UP[f] + j, j % 4)
                        if f == 0 and j == 0:
                            gate_transpose(h)
                    down(h, f)


_INPUTS = ["x", "ctx_main", "ctx_last", "mask", "wq", "wk", "wv", "units", "gate", "n1", "n2", "bo"]


def kernel(**inputs):
    import numpy as np
    import concourse.bacc as _bacc
    from concourse.bass_utils import run_bass_kernel_spmd as _run

    a = {k: np.asarray(v) for k, v in inputs.items()}

    def by_rows(w):
        return np.ascontiguousarray(w.reshape(-1, P, w.shape[1]).transpose(1, 0, 2))

    ctx = a["ctx_768"]
    qkv, up, down = a["L0_ffn_qkv_w"], a["L0_ffn_up_w"], a["L0_ffn_down_w"]
    mats = {"x_wo": a["L0_xattn_Wo"], "a_v": a["L0_attn_Wv"].T, "a_k": a["L0_attn_Wk"].T,
            "a_q": a["L0_attn_Wq"].T, "a_wo": a["L0_attn_Wo"].T,
            "f_q": qkv[0:D].T, "f_k": qkv[D:2 * D].T, "f_v": qkv[2 * D:3 * D].T, "f_wo": a["L0_ffn_o_w"].T}
    for j in range(4):
        mats[f"up{j}"] = up[D * j:D * (j + 1)].T
        mats[f"down{j}"] = down[:, D * j:D * (j + 1)].T
    arrays = {
        "x": a["x"].reshape(NB * SEQ, D),
        "ctx_main": ctx[:, 0:MAIN].reshape(PAIRS, 2, MAIN, CC, P).transpose(0, 4, 3, 1, 2).reshape(PAIRS, P, CC, 2 * MAIN),
        "ctx_last": ctx[:, MAIN].reshape(NB, CC, P).transpose(2, 1, 0),
        "mask": a["mask_BxS2_bf1"].view(np.uint8),
        "wq": by_rows(a["L0_xattn_Wq"]),
        "wk": by_rows(a["L0_xattn_Wk"]),
        "wv": by_rows(a["L0_xattn_Wv"]),
        "units": np.stack([by_rows(mats[n]) for n in UNITS]),
        "gate": by_rows(a["L0_ffn_gate_w"].T),
        "n1": a["L0_ffn_n1_w"], "n2": a["L0_ffn_n2_w"], "bo": a["L0_attn_bo"],
    }
    nc = _bacc.Bacc("TRN2", target_bir_lowering=False, num_devices=1)
    named, args = {}, []
    for name in _INPUTS:
        named[f"in_{name}"] = np.ascontiguousarray(arrays[name])
        args.append(nc.dram_tensor(f"in_{name}", named[f"in_{name}"].shape,
                                   mybir.dt.from_np(named[f"in_{name}"].dtype), kind="ExternalInput").ap())
    args.append(nc.dram_tensor("out", (NB * SEQ, D), F32, kind="ExternalOutput").ap())
    build(nc, *args)
    got = _run(nc, [named], core_ids=[0])
    return got.results[0]["out"].reshape(NB, SEQ, D)
```

```python
from contextlib import ExitStack

import concourse.bass as bass
from concourse import mybir

F32 = mybir.dt.float32
F32R = mybir.dt.float32r
U8 = mybir.dt.uint8
ALU = mybir.AluOpType
ACT = mybir.ActivationFunctionType
AX = mybir.AxisListType

P = 128
D = 512
KC = D // P
CC = 3
HD = 32
SEQ = 32
NB = 32
KEYS = 257
MAIN = KEYS - 1
PAIRS = NB // 2
TILES = NB * SEQ // P
HALVES = 2
HT = TILES // HALVES
HALF = HT * P
HPAIRS = PAIRS // HALVES
NE = 8
SCALE = float(HD) ** -0.5
BIG = 1.0e38
LN_EPS = 1e-5
RMS_EPS = 1e-6
DEN_EPS = 1e-8
TOPK_EPS = 1e-9

CREDIT = 1

UNITS = ["x_wo", "a_v", "a_k", "a_q", "a_wo", "f_v", "f_k", "f_q", "f_wo",
         "up0", "up1", "down0", "down1", "up2", "up3", "down2", "down3"]
NU = len(UNITS)
RING = 3

USE_WO = (0, 16, 32)
USE_V = (4, 20)
USE_KQ = (8, 24)
USE_UP = (36, 44)
USES = 52 // 2
FREES = 36 // 2


class Chain:

    def __init__(self, eng, sem):
        self.eng, self.sem, self.base, self.n = eng, sem, 0, 0

    def step(self, ins):
        ins.then_inc(self.sem, 1)
        self.n += 1

    def wait(self):
        self.eng.wait_ge(self.sem, self.base + self.n)

    def enter(self, i, per):
        self.before, self.per = self.base + self.n, per
        self.base, self.n = self.before + per * i, 0

    def leave(self, count):
        assert self.n == self.per, self.n
        self.base, self.n = self.before + self.per * count, 0


def wait(eng, sem, value):
    if not isinstance(value, int) or value > 0:
        eng.wait_ge(sem, value)


def stand_alone(eng, passed):
    eng.sem_inc(passed, 1)


def product(pe, out, left, right, first, last):
    pe.matmul(out, left[0], right[0], start=first, stop=False)
    pe.matmul(out, left[0], right[1], start=False, stop=False)
    return pe.matmul(out, left[1], right[0], start=False, stop=last)


class Shared:

    def __init__(self, nc, stack):
        self.raw = stack.enter_context(nc.sbuf_tensor("raw", [P, KC, D], F32))
        self.heads_raw = stack.enter_context(nc.sbuf_tensor("heads_raw", [P, KC, HALF], F32R))
        self.unit_in = [stack.enter_context(nc.semaphore(f"unit_in{i}")) for i in range(2)]
        self.heads_in = stack.enter_context(nc.semaphore("c_heads_in"))


def load_heads(sp, shared, heads_dram, h):
    sp.dma_start(shared.heads_raw[:].bitcast(F32).rearrange("p t d -> p (t d)").rearrange("p (q n) -> p q n", q=HPAIRS),
                 heads_dram.rearrange("(h q) p n -> h p q n", h=HALVES)[bass.ds(h, 1)]
                 .rearrange("o p q n -> (o p) q n")).then_inc(shared.heads_in, 16)


def build(nc, x, ctx_main, ctx_last, mask, wq, wk, wv, units, gate, n1, n2, bo, out):
    heads_dram = nc.dram_tensor("heads_scratch", (PAIRS, P, 256), F32, kind="Internal").ap()
    vlast_dram = nc.dram_tensor("vlast_scratch", (NB, 4, P), F32, kind="Internal").ap()
    with ExitStack() as stack:
        banks = {}
        for name in ("proj0", "proj1", "tr0", "tr1", "s0", "s1", "o0", "o1"):
            banks[name] = stack.enter_context(nc.psum_tensor(name, [P, 512], F32))
        ident = stack.enter_context(nc.sbuf_tensor("ident", [P, P], F32))
        shared = Shared(nc, stack)
        cross_attention(nc, banks, ident, shared, x, ctx_main, ctx_last, mask, wq, wk, wv,
                        heads_dram, vlast_dram, units)
        rest_of_layer(nc, banks, ident, shared, x, heads_dram, units, gate, n1, n2, bo, out)


def cross_attention(nc, banks, ident, shared, x, ctx_main, ctx_last, mask, wq, wk, wv,
                    heads_dram, vlast_dram, units):
    x_tiles = x.rearrange("(t p) d -> t p d", p=P)
    mask_pairs = mask.rearrange("(q b) j -> q b j", b=2)
    with ExitStack() as stack:
        def sb(name, shape, dt=F32):
            return stack.enter_context(nc.sbuf_tensor(name, shape, dt))

        def sem(name):
            return stack.enter_context(nc.semaphore(name))

        def split_pair(name, shape):
            return sb(name + "_hi", shape, F32R), sb(name + "_lo", shape, F32R)

        proj = [banks["proj0"], banks["proj1"]]
        tr = [banks["tr0"], banks["tr1"]]
        score_bank = [banks["s0"], banks["s1"]]
        out_bank = [banks["o0"], banks["o1"]]

        wk_raw, wv_raw, wq_raw = sb("wk_raw", [P, CC, D]), sb("wv_raw", [P, CC, D]), shared.raw
        wk_s, wv_s, wq_s = split_pair("wk", [P, CC, D]), split_pair("wv", [P, CC, D]), split_pair("wq", [P, KC, D])
        last_raw = sb("ctx_last_raw", [P, CC, NB])
        last_s = split_pair("ctx_last", [P, CC, P])
        k_last = sb("k_last", [P, KC, NB])
        v_last = sb("v_last", [NB, 4, 4, HD])
        v_last_all = sb("v_last_all", [P, NB, P])
        ctx_raw = [sb(f"ctx_raw{i}", [P, CC, 512]) for i in range(2)]
        ctx_s = [split_pair(f"ctx{i}", [P, CC, 512]) for i in range(2)]
        mask_raw = [sb(f"mask_raw{i}", [P, 2, KEYS], U8) for i in range(2)]
        mask_bias = [sb(f"mask_bias{i}", [P, 2, KEYS]) for i in range(2)]
        k_t = [sb(f"k_t{i}", [P, KC, 2, 258]) for i in range(2)]
        v_sb = [sb(f"v_sb{i}", [P, 2, 2, D]) for i in range(2)]
        probs = sb("probs", [P, 2, KC, KEYS])
        probs_t = sb("probs_t", [P, 2, 2, KC, P])
        x_raw = sb("x_raw", [P, D])
        x_hat = sb("x_hat", [P, D])
        x_t = split_pair("x_t", [P, KC, P])
        q_sb = sb("q_sb", [P, D])
        q_diag = sb("q_diag", [P, 4 * 4, P])
        stats = sb("stats", [P, 6])
        mean_var = sb("mean_var", [P, 2])
        var_eps = sb("var_eps", [P, 1])
        rstd = sb("rstd", [P, 1])
        minus_half = sb("minus_half", [P, 1])
        row_max = sb("row_max", [P, 2, KC])
        exp_bias = sb("exp_bias", [P, 2, KC])
        denom = sb("denom", [P, 2, KC])
        r_denom = sb("r_denom", [P, 8])
        last_part = sb("last_part", [P, 8, HD])
        heads = sb("heads", [P, 8, HD])
        heads_t = [sb(f"heads_t{i}", [P, 8 * SEQ]) for i in range(2)]

        passed_pool, passed_dve, passed_sp = sem("passed_pool"), sem("passed_dve"), sem("passed_sp")
        w_in = [sem(f"w_in{i}") for i in range(3)]
        w_hi, w_lo = sem("w_hi"), sem("w_lo")
        last_in, last_zero = sem("last_in"), sem("last_zero")
        last_k_full, last_v_full, last_k_done, last_v_done = (
            sem("last_k_full"), sem("last_v_full"), sem("last_k_done"), sem("last_v_done"))
        vlast_out, vlast_in = sem("vlast_out"), sem("vlast_in")
        ctx_in = [sem(f"ctx_in{i}") for i in range(2)]
        mask_in = [sem(f"mask_in{i}") for i in range(2)]
        x_in = sem("x_in")
        ctx_ready, mask_ready, k_last_ready = sem("ctx_ready"), sem("mask_ready"), sem("k_last_ready")
        ident_ready, diag_zero, pool_step, dve_step = sem("ident_ready"), sem("diag_zero"), sem("pool_step"), sem("dve_step")
        var_ready, rstd_ready, x_hat_ready = sem("var_ready"), sem("rstd_ready"), sem("x_hat_ready")
        xt_full, xt_hi, xt_lo = sem("xt_full"), sem("xt_hi"), sem("xt_lo")
        q_full, q_copied, qt_full, q_diag_ready = sem("q_full"), sem("q_copied"), sem("qt_full"), sem("q_diag_ready")
        k_full = [sem(f"k_full{i}") for i in range(2)]
        k_done = [sem(f"k_done{i}") for i in range(2)]
        v_full = [sem(f"v_full{i}") for i in range(2)]
        v_done = [sem(f"v_done{i}") for i in range(2)]
        s_full, s_read = sem("s_full"), sem("s_read")
        bias_ready, exp_done = sem("bias_ready"), sem("exp_done")
        pt_full = [sem(f"pt_full{i}") for i in range(2)]
        pt_done = [sem(f"pt_done{i}") for i in range(2)]
        pv_full, pv_read, heads_ready = sem("pv_full"), sem("pv_read"), sem("heads_ready")
        heads_out = [sem(f"heads_out{i}") for i in range(2)]

        block = stack.enter_context(nc.Block())

        @block.sync
        def _(sp):
            def load_pair(t, par):
                q = 2 * t + par
                sp.dma_start(ctx_raw[par][:], ctx_main[bass.ds(q, 1)].rearrange("o p c n -> (o p) c n")
                             ).then_inc(ctx_in[par], 16)

            def load_mask(t, par):
                q = 2 * t + par
                sp.dma_start(mask_raw[par][:],
                             mask_pairs[bass.ds(q, 1)].rearrange("o b j -> (o b) j").unsqueeze(0)
                             .to_broadcast([P, 2, KEYS])).then_inc(mask_in[par], 16)

            def store_heads(t, par):
                q = 2 * t + par
                sp.wait_ge(heads_ready, q + 1)
                stand_alone(sp, passed_sp)
                sp.dma_start(heads_dram[bass.ds(q, 1)].rearrange("o p n -> (o p) n"), heads_t[par][:]
                             ).then_inc(heads_out[par], 16)

            sp.dma_start(last_raw[:], ctx_last).then_inc(last_in, 16)
            sp.dma_start(wk_raw[:], wk).then_inc(w_in[0], 16)
            load_pair(0, 0)
            sp.dma_start(x_raw[:], x_tiles[0]).then_inc(x_in, 16)
            sp.dma_start(wv_raw[:], wv).then_inc(w_in[1], 16)
            sp.dma_start(wq_raw[:], wq).then_inc(w_in[2], 16)
            load_mask(0, 0)
            load_mask(0, 1)
            load_pair(0, 1)
            sp.wait_ge(last_v_done, 1)
            sp.dma_start(vlast_dram.rearrange("b a n -> b (a n)"),
                         v_last[:].rearrange("b a g d -> b (a g d)")).then_inc(vlast_out, 16)
            sp.wait_ge(vlast_out, 16)
            for a in range(4):
                sp.dma_start(v_last_all[32 * a:32 * a + 32],
                             vlast_dram[:, a, :].unsqueeze(0).to_broadcast([SEQ, NB, P])
                             ).then_inc(vlast_in, 16)
            sp.wait_ge(w_lo, 4)
            for v in range(2):
                sp.dma_start(shared.raw[:, 2 * v:2 * v + 2, :], units[0, :, 2 * v:2 * v + 2, :]
                             ).then_inc(shared.unit_in[v], 16)
            with sp.Fori(0, TILES - 1) as t:
                sp.wait_ge(x_hat_ready, t + 1)
                stand_alone(sp, passed_sp)
                sp.dma_start(x_raw[:], x_tiles[bass.ds(t + 1, 1)].rearrange("o p d -> (o p) d")
                             ).then_inc(x_in, 16)
                for par in range(2):
                    sp.wait_ge(ctx_ready, 2 * t + par + 1)
                    stand_alone(sp, passed_sp)
                    load_pair(t + 1, par)
                    sp.wait_ge(mask_ready, 2 * t + par + 1)
                    stand_alone(sp, passed_sp)
                    load_mask(t + 1, par)
                    store_heads(t, par)
            for par in range(2):
                sp.wait_ge(heads_out[par], 16 * TILES // HALVES + CREDIT)
            load_heads(sp, shared, heads_dram, 0)
            for par in range(2):
                store_heads(TILES - 1, par)
            for par in range(2):
                sp.wait_ge(heads_out[par], 16 * TILES + CREDIT)

        @block.gpsimd
        def _(pool):
            chain = Chain(pool, pool_step)

            pool.sem_inc(v_full[1], CREDIT)

            def split_ctx(t, par):
                q = 2 * t + par
                wait(pool, s_read, 8 * q - 6)
                pool.wait_ge(mask_in[par], 16 * t + 16)
                stand_alone(pool, passed_pool)
                pool.tensor_scalar(mask_bias[par][:], mask_raw[par][:], BIG, -BIG, ALU.mult, ALU.add
                                   ).then_inc(mask_ready, 1)
                wait(pool, v_full[1], 2 * q - 2 + CREDIT)
                pool.wait_ge(ctx_in[par], 16 * t + 16)
                hi, lo = ctx_s[par]
                stand_alone(pool, passed_pool)
                chain.step(pool.tensor_scalar(hi[:], ctx_raw[par][:], 1.0, None, ALU.mult))
                chain.wait()
                pool.tensor_tensor(lo[:], ctx_raw[par][:], hi[:].bitcast(F32), ALU.subtract
                                   ).then_inc(ctx_ready, 1)

            def root(t):
                pool.wait_ge(var_ready, t + 1)
                stand_alone(pool, passed_pool)
                chain.step(pool.tensor_scalar(var_eps[:], mean_var[:, 1:2], LN_EPS, None, ALU.add))
                chain.wait()
                pool.tensor_tensor(rstd[:], var_eps[:], minus_half[:], ALU.pow).then_inc(rstd_ready, 1)

            for part in last_s:
                pool.memset(part[:].bitcast(F32), 0.0).then_inc(last_zero, 1)
            chain.step(pool.memset(minus_half[:], -0.5))
            chain.step(pool.memset(ident[:], 0.0))
            chain.wait()
            pool.affine_select(out=ident[:], in_=ident[:], compare_op=ALU.not_equal, fill=1.0, base=0,
                               pattern=[[-1, P]], channel_multiplier=1).then_inc(ident_ready, 1)
            split_ctx(0, 0)
            root(0)
            pool.memset(q_diag[:], 0.0).then_inc(diag_zero, 1)
            chain.enter(0, 3)
            with pool.Fori(0, TILES - 1) as t:
                chain.base = chain.before + 3 * t
                split_ctx(t, 1)
                root(t + 1)
                split_ctx(t + 1, 0)
            chain.leave(TILES - 1)
            split_ctx(TILES - 1, 1)

        @block.scalar
        def _(act):
            def copy_k(t, par, j):
                q = 2 * t + par
                act.wait_ge(k_full[0], 2 * q + j + 1)
                act.activation(k_t[par][:, 2 * j, :, 0:MAIN],
                               proj[0][:].rearrange("p (b n) -> p b n", b=2), ACT.Copy).then_inc(k_done[0], 1)

            def copy_v(t, par, j):
                q = 2 * t + par
                act.wait_ge(v_full[0], 2 * q + j + 1)
                act.activation(v_sb[par][:, j, 0, :], proj[0][:], ACT.Copy).then_inc(v_done[0], 1)

            def exps(t, par, b):
                q = 2 * t + par
                act.wait_ge(bias_ready, 2 * q + b + 1)
                for g in range(KC):
                    last = act.activation(probs[:, b, g, :], probs[:, b, g, :], ACT.Exp,
                                          bias=exp_bias[:, b, g:g + 1], scale=SCALE,
                                          accum_out=denom[:, b, g:g + 1])
                last.then_inc(exp_done, 1)

            def copy_pt(t, par, b):
                q = 2 * t + par
                act.wait_ge(pt_full[0], 2 * q + b + 1)
                act.activation(probs_t[:, b, 0].rearrange("p g n -> p (g n)"), tr[0][:], ACT.Copy
                               ).then_inc(pt_done[0], 1)

            def copy_xt(t):
                act.wait_ge(xt_full, t + 1)
                act.activation(x_t[0][:].rearrange("p c n -> p (c n)"), tr[0][:], ACT.Copy).then_inc(xt_hi, 1)

            def copy_q(t):
                act.wait_ge(qt_full, t + 1)
                for a in (0, 1):
                    rows = slice(32 * a, 32 * a + 32)
                    last = act.activation(q_diag[rows, :, rows],
                                          tr[0][rows, :].rearrange("p (n i) -> p n i", i=SEQ), ACT.Copy)
                last.then_inc(q_diag_ready, 1)

            for n, (raw, parts) in enumerate(((wk_raw, wk_s), (wv_raw, wv_s), (wq_raw, wq_s))):
                act.wait_ge(w_in[n], 16)
                act.activation(parts[0][:], raw[:], ACT.Copy).then_inc(w_hi, 1)
                if n == 0:
                    act.wait_ge(last_in, 16)
                    act.wait_ge(last_zero, 2)
                    act.activation(last_s[0][:, :, 0:NB], last_raw[:], ACT.Copy).then_inc(w_hi, 1)
            act.wait_ge(last_v_full, 1)
            act.activation(v_last[:], proj[1][0:NB, :].rearrange("p (g a d) -> p a g d", g=4, a=4), ACT.Copy
                           ).then_inc(last_v_done, 1)
            copy_xt(0)
            copy_k(0, 0, 0)
            copy_k(0, 0, 1)
            act.wait_ge(diag_zero, 1)
            copy_q(0)
            copy_v(0, 0, 0)
            copy_v(0, 0, 1)

            def even_pair(t):
                exps(t, 0, 0)
                copy_k(t, 1, 0)
                exps(t, 0, 1)
                copy_k(t, 1, 1)
                copy_pt(t, 0, 0)
                copy_pt(t, 0, 1)
                copy_v(t, 1, 0)
                copy_v(t, 1, 1)

            with act.Fori(0, TILES - 1) as t:
                even_pair(t)
                exps(t, 1, 0)
                copy_xt(t + 1)
                copy_k(t + 1, 0, 0)
                exps(t, 1, 1)
                copy_k(t + 1, 0, 1)
                copy_q(t + 1)
                copy_pt(t, 1, 0)
                copy_pt(t, 1, 1)
                copy_v(t + 1, 0, 0)
                copy_v(t + 1, 0, 1)
            even_pair(TILES - 1)
            exps(TILES - 1, 1, 0)
            exps(TILES - 1, 1, 1)
            copy_pt(TILES - 1, 1, 0)
            copy_pt(TILES - 1, 1, 1)

        @block.vector
        def _(dve):
            chain = Chain(dve, dve_step)

            def copy_k(t, par, j):
                q = 2 * t + par
                dve.wait_ge(k_full[1], 2 * q + j + 1)
                dve.tensor_copy(k_t[par][:, 2 * j + 1, :, 0:MAIN],
                                proj[1][:].rearrange("p (b n) -> p b n", b=2)).then_inc(k_done[1], 1)

            def last_key(t, par):
                q = 2 * t + par
                dve.tensor_scalar(k_t[par][:, :, :, MAIN], k_last[:, :, bass.ds(2 * q, 2)], 1.0, None, ALU.mult
                                  ).then_inc(k_last_ready, 1)

            def copy_v(t, par, j):
                q = 2 * t + par
                dve.wait_ge(v_full[1], 2 * q + j + 1 + CREDIT)
                dve.tensor_copy(v_sb[par][:, j, 1, :], proj[1][:]).then_inc(v_done[1], 1)

            def mask_max(t, par):
                q = 2 * t + par
                dve.wait_ge(mask_ready, q + 1)
                for b in range(2):
                    for g in range(KC):
                        dve.wait_ge(s_full, 8 * q + 4 * b + g + 1)
                        stand_alone(dve, passed_dve)
                        dve.tensor_tensor_reduce(
                            out=probs[:, b, g, :], in0=score_bank[g % 2][:, 0:KEYS], in1=mask_bias[par][:, b, :],
                            scale=1.0, scalar=-3.0e38, op0=ALU.add, op1=ALU.max,
                            accum_out=row_max[:, b, g:g + 1]).then_inc(s_read, 1)
                    dve.wait_ge(s_read, 8 * q + 4 * b + 6)
                    dve.tensor_scalar(exp_bias[:, b, :], row_max[:, b, :], -SCALE, None, ALU.mult
                                      ).then_inc(bias_ready, 1)

            def copy_pt(t, par, b):
                q = 2 * t + par
                dve.wait_ge(pt_full[1], 2 * q + b + 1)
                dve.tensor_copy(probs_t[:, b, 1].rearrange("p g n -> p (g n)"), tr[1][:]).then_inc(pt_done[1], 1)

            def norm_stats(t):
                dve.wait_ge(x_in, 16 * t + 16)
                chain.step(dve.bn_stats(stats[:], x_raw[:]))
                chain.wait()
                stand_alone(dve, passed_dve)
                dve.bn_aggr(mean_var[:], stats[:]).then_inc(var_ready, 1)

            def norm_apply(t):
                dve.wait_ge(rstd_ready, t + 1)
                dve.tensor_scalar(x_hat[:], x_raw[:], mean_var[:, 0:1], rstd[:, 0:1], ALU.subtract, ALU.mult
                                  ).then_inc(x_hat_ready, 1)

            def low_xt(t):
                dve.wait_ge(xt_hi, t + 1)
                dve.tensor_tensor(x_t[1][:].rearrange("p c n -> p (c n)"), tr[0][:],
                                  x_t[0][:].rearrange("p c n -> p (c n)").bitcast(F32), ALU.subtract
                                  ).then_inc(xt_lo, 1)

            def copy_q_rows(t):
                dve.wait_ge(q_full, t + 1)
                dve.tensor_copy(q_sb[:], tr[1][:]).then_inc(q_copied, 1)

            def copy_q(t):
                dve.wait_ge(qt_full, t + 1)
                for a in (2, 3):
                    rows = slice(32 * a, 32 * a + 32)
                    last = dve.tensor_copy(q_diag[rows, :, rows],
                                           tr[0][rows, :].rearrange("p (n i) -> p n i", i=SEQ))
                last.then_inc(q_diag_ready, 1)

            def finish_heads(t, par):
                q = 2 * t + par
                dve.wait_ge(exp_done, 2 * q + 2)
                chain.step(dve.reciprocal(r_denom[:], denom[:].rearrange("p b g -> p (b g)")))
                chain.step(dve.tensor_tensor(
                    last_part[:], probs[:, :, :, MAIN].rearrange("p b g -> p (b g)").unsqueeze(2).to_broadcast([P, 8, HD]),
                    v_last_all[:, bass.ds(2 * q, 2), :].rearrange("p b (g d) -> p (b g) d", g=4), ALU.mult))
                chain.wait()
                dve.wait_ge(pv_full, 2 * q + 2)
                for b in range(2):
                    for a in range(4):
                        rows = slice(32 * a, 32 * a + 32)
                        part = dve.tensor_tensor(
                            heads[rows, 4 * b:4 * b + 4, :],
                            out_bank[b][rows, :].rearrange("p (g n) -> p g n", g=4)[:, :, rows],
                            last_part[rows, 4 * b:4 * b + 4, :], ALU.add)
                part.then_inc(pv_read, 1)
                dve.wait_ge(pv_read, q + 1 + CREDIT)
                chain.step(dve.tensor_tensor(heads[:], heads[:], r_denom[:].unsqueeze(2).to_broadcast([P, 8, HD]), ALU.mult))
                chain.wait()
                dve.wait_ge(heads_out[par], 16 * t + CREDIT)
                dve.transpose(heads_t[par][:], heads[:].rearrange("p n d -> p (n d)")).then_inc(heads_ready, 1)

            for par in range(2):
                dve.sem_inc(heads_out[par], CREDIT)
            dve.memset(stats[:], 0.0).then_inc(s_read, 1)
            dve.memset(mean_var[:], 0.0).then_inc(s_read, 1)
            dve.wait_ge(s_read, 2)
            for n, (raw, parts) in enumerate(((wk_raw, wk_s), (last_raw, last_s), (wv_raw, wv_s), (wq_raw, wq_s))):
                dve.wait_ge(w_hi, n + 1)
                cols = NB if n == 1 else D
                dve.tensor_tensor(parts[1][:, :, 0:cols], raw[:], parts[0][:, :, 0:cols].bitcast(F32), ALU.subtract
                                  ).then_inc(w_lo, 1)
                if n == 1:
                    norm_stats(0)
            norm_apply(0)
            dve.wait_ge(last_k_full, 1)
            dve.tensor_copy(k_last[:], proj[0][:].rearrange("p (g n) -> p g n", g=4)[:, :, 0:NB]
                            ).then_inc(last_k_done, 1)
            dve.wait_ge(last_k_done, 1)
            low_xt(0)
            copy_k(0, 0, 0)
            copy_q_rows(0)
            copy_k(0, 0, 1)
            last_key(0, 0)
            dve.wait_ge(diag_zero, 1)
            copy_q(0)
            copy_v(0, 0, 0)
            copy_v(0, 0, 1)
            dve.wait_ge(vlast_in, 64)

            def even_pair(t, more):
                mask_max(t, 0)
                copy_k(t, 1, 0)
                if more:
                    norm_stats(t + 1)
                copy_k(t, 1, 1)
                last_key(t, 1)
                copy_pt(t, 0, 0)
                copy_pt(t, 0, 1)
                if more:
                    norm_apply(t + 1)
                copy_v(t, 1, 0)
                finish_heads(t, 0)
                copy_v(t, 1, 1)

            chain.enter(0, 7)
            with dve.Fori(0, TILES - 1) as t:
                chain.base = chain.before + 7 * t
                even_pair(t, True)
                mask_max(t, 1)
                low_xt(t + 1)
                copy_k(t + 1, 0, 0)
                copy_q_rows(t + 1)
                copy_k(t + 1, 0, 1)
                last_key(t + 1, 0)
                copy_q(t + 1)
                copy_pt(t, 1, 0)
                copy_pt(t, 1, 1)
                copy_v(t + 1, 0, 0)
                finish_heads(t, 1)
                copy_v(t + 1, 0, 1)
            chain.leave(TILES - 1)
            even_pair(TILES - 1, False)
            mask_max(TILES - 1, 1)
            copy_pt(TILES - 1, 1, 0)
            copy_pt(TILES - 1, 1, 1)
            finish_heads(TILES - 1, 1)

        @block.tensor
        def _(pe):
            def keys(t, par, js):
                q = 2 * t + par
                pe.wait_ge(ctx_ready, q + 1)
                for j in js:
                    for bank in range(2):
                        g = 2 * j + bank
                        if j == 0:
                            wait(pe, v_done[bank], 2 * q)
                        else:
                            pe.wait_ge(k_done[bank], 2 * q + 1)
                        for c in range(CC):
                            last = product(pe, proj[bank][:], [w[:, c, g * P:(g + 1) * P] for w in wk_s],
                                           [s[:, c, :] for s in ctx_s[par]], c == 0, c == CC - 1)
                        last.then_inc(k_full[bank], 1)

            def values(t, par, bs=(0, 1)):
                q = 2 * t + par
                for b in bs:
                    for bank in range(2):
                        if b == 0:
                            pe.wait_ge(k_done[bank], 2 * q + 2)
                        else:
                            pe.wait_ge(v_done[bank], 2 * q + 1)
                        at = slice(MAIN * b + P * bank, MAIN * b + P * bank + P)
                        for c in range(CC):
                            last = product(pe, proj[bank][:], [s[:, c, at] for s in ctx_s[par]],
                                           [w[:, c, :] for w in wv_s], c == 0, c == CC - 1)
                        last.then_inc(v_full[bank], 1)

            def scores(t, par):
                q = 2 * t + par
                for bank in range(2):
                    pe.wait_ge(k_done[bank], 2 * q + 2)
                pe.wait_ge(k_last_ready, q + 1)
                pe.wait_ge(q_diag_ready, 2 * t + 2)
                for b in range(2):
                    for g in range(KC):
                        pe.wait_ge(s_read, 8 * q + 4 * b + g + 1)
                        pe.matmul(score_bank[g % 2][:, 0:KEYS], q_diag[:, 4 * g + 2 * par + b, :],
                                  k_t[par][:, g, b, 0:KEYS], start=True, stop=True).then_inc(s_full, 1)

            def transpose_x(t):
                pe.wait_ge(x_hat_ready, t + 1)
                wait(pe, pt_done[0], 4 * t - 2 + CREDIT)
                for c in range(KC):
                    last = pe.transpose(tr[0][:, c * P:(c + 1) * P], x_hat[:, c * P:(c + 1) * P], ident[:])
                last.then_inc(xt_full, 1)

            def queries(t):
                pe.wait_ge(xt_lo, t + 1)
                wait(pe, pt_done[1], 4 * t - 2 + CREDIT)
                for c in range(KC):
                    last = product(pe, tr[1][:], [s[:, c, :] for s in x_t], [w[:, c, :] for w in wq_s],
                                   c == 0, c == KC - 1)
                last.then_inc(q_full, 1)

            def transpose_q(t):
                pe.wait_ge(q_copied, t + 1)
                for g in range(KC):
                    last = pe.transpose(tr[0][:, g * P:(g + 1) * P], q_sb[:, g * P:(g + 1) * P], ident[:])
                last.then_inc(qt_full, 1)

            def transpose_probs(t, par):
                q = 2 * t + par
                for b in range(2):
                    pe.wait_ge(exp_done, 2 * q + b + 1)
                    for c in range(2):
                        pe.wait_ge(pt_done[c], 2 * q + b + CREDIT)
                        for g in range(KC):
                            last = pe.transpose(tr[c][:, g * P:(g + 1) * P], probs[:, b, g, c * P:(c + 1) * P], ident[:])
                        last.then_inc(pt_full[c], 1)

            def attend(t, par):
                q = 2 * t + par
                for bank in range(2):
                    pe.wait_ge(v_done[bank], 2 * q + 2)
                pe.wait_ge(pv_read, q + CREDIT)
                for b in range(2):
                    for c in range(2):
                        pe.wait_ge(pt_done[c], 2 * q + b + 1 + CREDIT)
                    for g in range(KC):
                        for c in range(2):
                            last = pe.matmul(out_bank[b][:, g * P:(g + 1) * P], probs_t[:, b, c, g, :],
                                             v_sb[par][:, b, c, g * P:(g + 1) * P], start=c == 0, stop=c == 1)
                    last.then_inc(pv_full, 1)

            for free in (pt_done[0], pt_done[1], pv_read):
                pe.sem_inc(free, CREDIT)
            pe.wait_ge(ident_ready, 1)
            pe.wait_ge(w_lo, 2)
            for g in range(KC):
                for c in range(CC):
                    last = product(pe, proj[0][:, g * P:(g + 1) * P], [w[:, c, g * P:(g + 1) * P] for w in wk_s],
                                   [s[:, c, :] for s in last_s], c == 0, c == CC - 1)
            last.then_inc(last_k_full, 1)
            pe.wait_ge(w_lo, 3)
            for c in range(CC):
                last = product(pe, proj[1][:], [s[:, c, :] for s in last_s], [w[:, c, :] for w in wv_s],
                               c == 0, c == CC - 1)
            last.then_inc(last_v_full, 1)
            transpose_x(0)
            pe.wait_ge(last_k_done, 1)
            pe.wait_ge(last_v_done, 1)
            keys(0, 0, (0,))
            pe.wait_ge(w_lo, 4)
            queries(0)
            keys(0, 0, (1,))
            transpose_q(0)
            values(0, 0)

            def even_pair(t):
                scores(t, 0)
                keys(t, 1, (0, 1))
                transpose_probs(t, 0)
                values(t, 1, (0,))
                attend(t, 0)
                values(t, 1, (1,))

            with pe.Fori(0, TILES - 1) as t:
                even_pair(t)
                scores(t, 1)
                transpose_x(t + 1)
                keys(t + 1, 0, (0,))
                queries(t + 1)
                keys(t + 1, 0, (1,))
                transpose_q(t + 1)
                pe.wait_ge(q_diag_ready, 2 * t + 4)
                transpose_probs(t, 1)
                values(t + 1, 0, (0,))
                attend(t, 1)
                values(t + 1, 0, (1,))
            even_pair(TILES - 1)
            scores(TILES - 1, 1)
            transpose_probs(TILES - 1, 1)
            attend(TILES - 1, 1)


def rest_of_layer(nc, banks, ident, shared, x, heads_dram, units, gate, n1, n2, bo, out):
    x_halves = x.rearrange("(h t p) d -> h p t d", h=HALVES, p=P)
    out_halves = out.rearrange("(h t p) d -> h p t d", h=HALVES, p=P)
    with ExitStack() as stack:
        def sb(name, shape, dt=F32):
            return stack.enter_context(nc.sbuf_tensor(name, shape, dt))

        def sem(name):
            return stack.enter_context(nc.semaphore(name))

        def split_pair(name, shape):
            return sb(name + "_hi", shape, F32R), sb(name + "_lo", shape, F32R)

        proj = [banks["proj0"], banks["proj1"]]
        tr = [banks["tr0"], banks["tr1"]]
        score_bank = [banks["s0"], banks["s1"]]
        out_bank = [banks["o0"], banks["o1"]]
        down_bank = score_bank + out_bank
        gate_bank, gate_t_bank = score_bank

        unit_raw = [shared.raw[:, 2 * i:2 * i + 2, :] for i in range(2)]
        unit_s = [split_pair(f"unit{i}", [P, KC, D]) for i in range(RING)]
        res = sb("res", [P, HT, D])
        y = sb("y", [P, HT, D])
        heads_s = split_pair("heads_s", [P, KC, HALF])
        xt_s = sb("xt_s_hi", [P, KC, HALF], F32R), shared.heads_raw
        x_hat = [sb(f"c_x_hat{i}", [P, D]) for i in range(2)]
        q_t = [sb(f"q_t{i}", [P, HALF]) for i in range(2)]
        k_diag = [sb(f"k_diag{i}", [P, 16, P]) for i in range(2)]
        v_tok = sb("v_tok", [P, HT, D])
        masked = sb("masked", [P, 16, SEQ])
        pr = sb("pr", [P, 16, SEQ])
        pt_diag = [sb(f"pt_diag{i}", [P, 16, P]) for i in range(2)]
        causal = sb("causal", [P, SEQ])
        act_buf = [sb(f"act_buf{i}", [P, HALF]) for i in range(2)]
        h_s = split_pair("h_s", [P, 8, HALF])
        gate_raw = sb("gate_raw", [P, KC, NE])
        gate_s = split_pair("gate_s", [P, KC, P])
        logits = sb("logits", [NE, HALF])
        n1_all, n2_all, bo_all = sb("n1_all", [P, D]), sb("n2_all", [P, D]), sb("bo_all", [P, D])
        minus_half = sb("c_minus_half", [P, 1])
        stats = sb("c_stats", [P, HT, 6])
        mean_var = sb("c_mean_var", [P, HT, 2])
        square_sum = sb("square_sum", [P, HT])
        root_in = sb("root_in", [P, 2, HT])
        rstd = sb("c_rstd", [P, 2, HT])
        row_max = sb("c_row_max", [P, 16])
        den = sb("c_den", [P, 16])
        r_den = sb("c_r_den", [P, 16])
        top = sb("top", [P, HT, NE])
        g_small = sb("g_small", [P, 5, HT])
        weight = sb("weight", [P, HT])

        passed_pool, passed_dve, passed_pe = sem("c_passed_pool"), sem("c_passed_dve"), sem("c_passed_pe")
        passed_sp = sem("c_passed_sp")
        const_in, gate_in = sem("const_in"), sem("gate_in")
        const_ready, kdiag_ready, gate_ready = sem("const_ready"), sem("kdiag_ready"), sem("gate_ready")
        unit_in, heads_in = shared.unit_in, shared.heads_in
        unit_hi, unit_ready, down_half = sem("unit_hi"), sem("unit_ready"), sem("down_half")
        x_in = [sem(f"c_x_in{i}") for i in range(HT)]
        pool_step, dve_step = sem("c_pool_step"), sem("c_dve_step")
        p_full = [sem(f"p_full{i}") for i in range(2)]
        p_free = [sem(f"p_free{i}") for i in range(2)]
        t_full = [sem(f"t_full{i}") for i in range(2)]
        t_hi, x_hat_ready = sem("t_hi"), sem("c_x_hat_ready")
        t_free = [sem(f"t_free{i}") for i in range(2)]
        heads_hi, heads_lo = sem("heads_hi"), sem("heads_lo")
        sc_full = [sem(f"sc_full{i}") for i in range(2)]
        at_full = [sem(f"at_full{i}") for i in range(2)]
        shifted, exp_ready, pt_ready = sem("shifted"), sem("exp_ready"), sem("pt_ready")
        var_ready, rstd_ready = sem("c_var_ready"), sem("c_rstd_ready")
        y_ready, square_ready, rms_ready = sem("y_ready"), sem("square_ready"), sem("rms_ready")
        gate_full, logits_ready, gate_t_full = sem("gate_full"), sem("logits_ready"), sem("gate_t_full")
        top_ready, top_exp, weight_ready = sem("top_ready"), sem("top_exp"), sem("weight_ready")
        tanh_ready, silu_ready, h_hi, h_lo = sem("tanh_ready"), sem("silu_ready"), sem("h_hi"), sem("h_lo")
        down_full, down_read, final, stored = sem("down_full"), sem("down_read"), sem("final"), sem("stored")

        def proj_full(n, h):
            return p_full[n % 2], USES * h + n // 2 + 1 + CREDIT

        def proj_free(n, h):
            return p_free[n % 2], FREES * h + n // 2 + CREDIT

        def unit_used(u, h):
            if u < 0:
                return ((down_half, 2 * h + CREDIT), (down_full, 8 * h + CREDIT), (p_full[1], USES * h + CREDIT))[u + RING]
            last_use = {0: 3, 1: 7, 2: 14, 3: 15, 4: 19, 5: 23, 6: 30, 7: 31, 8: 35, 9: 39, 10: 43, 13: 47, 14: 51}
            if u in last_use:
                return proj_full(last_use[u], h)
            if u in (11, 15):
                return down_half, 2 * h + (1 if u == 11 else 2) + CREDIT
            return down_full, 8 * h + (4 if u == 12 else 8) + CREDIT

        heads_raw = shared.heads_raw[:].bitcast(F32).rearrange("p t d -> p (t d)")
        block = stack.enter_context(nc.Block())

        @block.sync
        def _(sp):
            def load_unit(h, u):
                for v in range(2):
                    wait(sp, unit_ready, 2 * (NU * h + u) + v - 1)
                    sp.dma_start(unit_raw[v], units[u, :, 2 * v:2 * v + 2, :]).then_inc(unit_in[v], 16)

            def half(h):
                for u in range(1, NU):
                    load_unit(h, u)

            def store(h, t):
                sp.wait_ge(final, 4 * h + t + 1)
                stand_alone(sp, passed_sp)
                sp.dma_start(out_halves[bass.ds(h, 1), :, t, :].rearrange("o p d -> (o p) d"), y[:, t, :]
                             ).then_inc(stored, 16)

            def load_x(h, t):
                sp.dma_start(res[:, t, :], x_halves[bass.ds(h, 1), :, t, :].rearrange("o p d -> (o p) d")
                             ).then_inc(x_in[t], 16)

            for t in range(HT):
                load_x(0, t)
            sp.dma_start(gate_raw[:], gate).then_inc(gate_in, 16)
            for row, vector in ((n1_all, n1), (n2_all, n2), (bo_all, bo)):
                sp.dma_start(row[:], vector.unsqueeze(0).to_broadcast([P, D])).then_inc(const_in, 16)
            with sp.Fori(0, HALVES - 1) as h:
                half(h)
                load_unit(h + 1, 0)
                sp.wait_ge(p_full[1], USES * (h + 1) + CREDIT)
                stand_alone(sp, passed_sp)
                load_heads(sp, shared, heads_dram, h + 1)
                for t in range(HT):
                    store(h, t)
                    load_x(h + 1, t)
            half(HALVES - 1)
            for t in range(HT):
                store(HALVES - 1, t)
            sp.wait_ge(stored, 16 * HT * HALVES + CREDIT)

        @block.gpsimd
        def _(pool):
            chain = Chain(pool, pool_step)

            def low_unit(h, u, vs=(0, 1)):
                hi, lo = unit_s[u % RING]
                for v in vs:
                    pool.wait_ge(unit_hi, 2 * (NU * h + u) + v + 1)
                    stand_alone(pool, passed_pool)
                    at = slice(2 * v, 2 * v + 2)
                    pool.tensor_tensor(lo[:, at, :], unit_raw[v], hi[:, at, :].bitcast(F32), ALU.subtract
                                       ).then_inc(unit_ready, 1)

            def root_var(h, stage, t):
                pool.wait_ge(var_ready, 8 * h + 4 * stage + t + 1)
                stand_alone(pool, passed_pool)
                chain.step(pool.tensor_scalar(root_in[:, 0, t:t + 1], mean_var[:, t, 1:2], LN_EPS, None, ALU.add))
                chain.wait()
                pool.tensor_tensor(rstd[:, 0, t:t + 1], root_in[:, 0, t:t + 1], minus_half[:], ALU.pow
                                   ).then_inc(rstd_ready, 1)

            def root_square(h, stage, t):
                pool.wait_ge(square_ready, 8 * h + 4 * (stage - 1) + t + 1 + CREDIT)
                stand_alone(pool, passed_pool)
                chain.step(pool.tensor_scalar(root_in[:, 1, t:t + 1], square_sum[:, t:t + 1], 1.0 / D, RMS_EPS,
                                              ALU.mult, ALU.add))
                chain.wait()
                pool.tensor_tensor(rstd[:, 1, t:t + 1], root_in[:, 1, t:t + 1], minus_half[:], ALU.pow
                                   ).then_inc(rms_ready, 1)

            chain.step(pool.memset(minus_half[:], -0.5))
            for part in gate_s:
                pool.memset(part[:].bitcast(F32), 0.0).then_inc(const_ready, 1)
            chain.step(pool.memset(causal[:], 0.0))
            chain.wait()
            for b in range(4):
                rows = slice(32 * b, 32 * b + 32)
                pool.affine_select(out=causal[rows, :], in_=causal[rows, :], compare_op=ALU.is_ge, fill=-BIG,
                                   base=0, pattern=[[-1, SEQ]], channel_multiplier=1).then_inc(const_ready, 1)
                pool.wait_ge(const_ready, 3 + b)
            per = 16
            chain.enter(0, per)
            with pool.Fori(0, HALVES) as h:
                chain.base = chain.before + per * h
                low_unit(h, 0)
                low_unit(h, 1)
                root_var(h, 0, 0)
                root_var(h, 0, 1)
                low_unit(h, 2)
                root_var(h, 0, 2)
                root_var(h, 0, 3)
                for u in range(3, 6):
                    low_unit(h, u)
                root_var(h, 1, 0)
                low_unit(h, 6, (0,))
                root_var(h, 1, 1)
                root_square(h, 1, 0)
                low_unit(h, 6, (1,))
                root_var(h, 1, 2)
                root_square(h, 1, 1)
                root_var(h, 1, 3)
                root_square(h, 1, 2)
                root_square(h, 1, 3)
                for u in range(7, 10):
                    low_unit(h, u)
                for t in range(HT):
                    root_square(h, 2, t)
                for u in range(10, NU):
                    low_unit(h, u)
            chain.leave(HALVES)

        @block.scalar
        def _(act):
            def high_unit(h, u):
                act.wait_ge(*unit_used(u - RING, h))
                for v in range(2):
                    act.wait_ge(unit_in[v], 16 * (NU * h + u + 1))
                    act.activation(unit_s[u % RING][0][:, 2 * v:2 * v + 2, :], unit_raw[v], ACT.Copy
                                   ).then_inc(unit_hi, 1)

            def high_xt(h, stage, t):
                n = 4 * stage + t
                act.wait_ge(t_full[n % 2], 6 * h + n // 2 + 1)
                act.activation(xt_s[0][:, :, t * P:(t + 1) * P],
                               tr[n % 2][:].rearrange("p (c n) -> p c n", c=KC), ACT.Copy).then_inc(t_hi, 1)

            def copy_v(h, layer, t):
                n = USE_V[layer] + t
                act.wait_ge(*proj_full(n, h))
                act.activation(v_tok[:, t, :], proj[n % 2][:], ACT.Copy).then_inc(p_free[n % 2], 1)

            def copy_kq(h, layer, m):
                n = USE_KQ[layer] + 2 * m
                act.wait_ge(*proj_full(n, h))
                for a in range(4):
                    rows = slice(32 * a, 32 * a + 32)
                    last = act.activation(k_diag[m % 2][rows, :, rows],
                                          proj[0][rows, :].rearrange("p (n j) -> p n j", j=SEQ), ACT.Copy)
                last.then_inc(p_free[0], 1)
                act.wait_ge(*proj_full(n + 1, h))
                act.activation(q_t[m % 2][:], proj[1][:], ACT.Copy).then_inc(p_free[1], 1)

            def exp(h, layer, m):
                act.wait_ge(shifted, 8 * h + 4 * layer + m + 1)
                act.activation(pr[:], pr[:], ACT.Exp, scale=SCALE).then_inc(exp_ready, 1)

            def high_heads(h, layer, m):
                n = 4 * layer + m
                act.wait_ge(at_full[n % 2], 4 * h + n // 2 + 1)
                act.activation(heads_s[0][:, m, :], out_bank[n % 2][:], ACT.Copy).then_inc(heads_hi, 1)

            def square(h, stage, t):
                if stage == 1:
                    act.wait_ge(y_ready, 4 * h + t + 1)
                else:
                    act.wait_ge(p_free[t % 2], FREES * h + (USE_WO[2] + t) // 2 + 1 + CREDIT)
                act.wait_ge(square_ready, 8 * h + 4 * (stage - 1) + t + CREDIT)
                act.activation(act_buf[0][:], y[:, t, :], ACT.Square, accum_out=square_sum[:, t:t + 1]
                               ).then_inc(square_ready, 1)

            def attention(h, layer):
                for m in range(KC):
                    copy_kq(h, layer, m)
                    if m >= 1:
                        exp(h, layer, m - 1)
                    if m >= 2:
                        high_heads(h, layer, m - 2)
                high_unit(h, (5, 9)[layer])
                exp(h, layer, 3)
                high_heads(h, layer, 2)
                high_heads(h, layer, 3)
                high_unit(h, (6, 10)[layer])

            act.wait_ge(gate_in, 16)
            act.wait_ge(const_ready, 2)
            act.activation(gate_s[0][:, :, 0:NE], gate_raw[:], ACT.Copy).then_inc(gate_ready, 1)
            with act.Fori(0, HALVES) as h:
                high_unit(h, 0)
                act.wait_ge(heads_in, 16 * h + 16)
                act.activation(heads_s[0][:].rearrange("p g (n i) -> p g n i", i=SEQ),
                               heads_raw.rearrange("p (n g i) -> p g n i", g=4, i=SEQ),
                               ACT.Copy).then_inc(heads_hi, 1)
                high_unit(h, 1)
                high_xt(h, 0, 0)
                high_xt(h, 0, 1)
                high_unit(h, 2)
                high_xt(h, 0, 2)
                copy_v(h, 0, 0)
                high_unit(h, 3)
                copy_v(h, 0, 1)
                high_xt(h, 0, 3)
                copy_v(h, 0, 2)
                copy_v(h, 0, 3)
                high_unit(h, 4)
                act.wait_ge(kdiag_ready, 2)
                attention(h, 0)
                square(h, 1, 0)
                square(h, 1, 1)
                high_xt(h, 1, 0)
                square(h, 1, 2)
                high_xt(h, 1, 1)
                copy_v(h, 1, 0)
                square(h, 1, 3)
                high_xt(h, 1, 2)
                high_unit(h, 7)
                copy_v(h, 1, 1)
                high_xt(h, 1, 3)
                copy_v(h, 1, 2)
                copy_v(h, 1, 3)
                high_unit(h, 8)
                attention(h, 1)
                square(h, 2, 0)
                square(h, 2, 1)
                high_xt(h, 2, 0)
                square(h, 2, 2)
                high_xt(h, 2, 1)
                square(h, 2, 3)
                high_xt(h, 2, 2)
                high_xt(h, 2, 3)
                act.wait_ge(gate_full, h + 1)
                act.activation(logits[:], gate_bank[0:NE, :], ACT.Copy).then_inc(logits_ready, 1)
                high_unit(h, 11)
                for f in range(2):
                    for j in range(9):
                        if j < 8:
                            n = USE_UP[f] + j
                            act.wait_ge(*proj_full(n, h))
                            if j >= 2:
                                act.wait_ge(h_lo, 16 * h + 8 * f + j - 1)
                            act.activation(act_buf[j % 2][:], proj[n % 2][:], ACT.Tanh, scale=0.5
                                           ).then_inc(tanh_ready, 1)
                        if j:
                            act.wait_ge(silu_ready, 16 * h + 8 * f + j + CREDIT)
                            act.activation(h_s[0][:, j - 1, :], act_buf[(j - 1) % 2][:], ACT.Copy, scale=0.5
                                           ).then_inc(h_hi, 1)
                        if f == 0 and j == 2:
                            act.wait_ge(top_ready, h + 1)
                            act.activation(top[:], top[:], ACT.Exp).then_inc(top_exp, 1)
                        if j == 4:
                            high_unit(h, (12, 16)[f])
                    if f == 0:
                        for u in (13, 14, 15):
                            high_unit(h, u)

        @block.vector
        def _(dve):
            chain = Chain(dve, dve_step)

            def low_xt(h, stage, t):
                n = 4 * stage + t
                at = slice(t * P, (t + 1) * P)
                dve.wait_ge(t_hi, 12 * h + n + 1)
                dve.tensor_tensor(xt_s[1][:, :, at], tr[n % 2][:].rearrange("p (c n) -> p c n", c=KC),
                                  xt_s[0][:, :, at].bitcast(F32), ALU.subtract).then_inc(t_free[n % 2], 1)

            def low_raw_heads(h, t):
                dve.wait_ge(heads_hi, 9 * h + 1)
                at = slice(t * P, (t + 1) * P)
                dve.tensor_tensor(heads_s[1][:, :, at].rearrange("p g (n i) -> p g n i", i=SEQ),
                                  heads_raw.rearrange("p (n g i) -> p g n i", g=4, i=SEQ)[:, :, 4 * t:4 * t + 4],
                                  heads_s[0][:, :, at].rearrange("p g (n i) -> p g n i", i=SEQ).bitcast(F32),
                                  ALU.subtract).then_inc(heads_lo, 1)

            def low_heads(h, layer, m):
                n = 4 * layer + m
                dve.wait_ge(heads_hi, 9 * h + 1 + n + 1)
                dve.tensor_tensor(heads_s[1][:, m, :], out_bank[n % 2][:], heads_s[0][:, m, :].bitcast(F32),
                                  ALU.subtract).then_inc(heads_lo, 1)

            def add_res(h, stage, t):
                n = USE_WO[stage] + t
                row = y[:, t, :] if stage == 2 else res[:, t, :]
                dve.wait_ge(*proj_full(n, h))
                if stage == 0:
                    dve.wait_ge(x_in[t], 16 * h + 16)
                dve.tensor_tensor(row, proj[n % 2][:], row, ALU.add).then_inc(p_free[n % 2], 1)
                if stage < 2:
                    dve.wait_ge(p_free[n % 2], FREES * h + n // 2 + 1 + CREDIT)
                    chain.step(dve.bn_stats(stats[:, t, :], row))
                    chain.wait()
                    stand_alone(dve, passed_dve)
                    dve.bn_aggr(mean_var[:, t, :], stats[:, t, :]).then_inc(var_ready, 1)

            def layer_norm(h, stage, t):
                dve.wait_ge(rstd_ready, 8 * h + 4 * stage + t + 1)
                if stage == 0:
                    dve.tensor_scalar(x_hat[t % 2][:], res[:, t, :], mean_var[:, t, 0:1], rstd[:, 0, t:t + 1],
                                      ALU.subtract, ALU.mult).then_inc(x_hat_ready, 1)
                    chain.step(dve.tensor_tensor(res[:, t, :], res[:, t, :], bo_all[:], ALU.add))
                else:
                    dve.tensor_scalar(y[:, t, :], res[:, t, :], mean_var[:, t, 0:1], rstd[:, 0, t:t + 1],
                                      ALU.subtract, ALU.mult).then_inc(y_ready, 1)

            def rms_norm(h, stage, t):
                dve.wait_ge(rms_ready, 8 * h + 4 * (stage - 1) + t + 1)
                dve.scalar_tensor_tensor(x_hat[t % 2][:], y[:, t, :], rstd[:, 1, t:t + 1],
                                         (n1_all if stage == 1 else n2_all)[:], ALU.mult, ALU.mult
                                         ).then_inc(x_hat_ready, 1)

            def softmax(h, layer, m):
                n = 4 * layer + m
                bank = score_bank[n % 2][:].rearrange("p (n j) -> p n j", j=SEQ)
                dve.wait_ge(sc_full[n % 2], 4 * h + n // 2 + 1)
                if layer == 1:
                    chain.step(dve.tensor_tensor(masked[:], bank, causal[:].unsqueeze(1).to_broadcast([P, 16, SEQ]), ALU.add))
                    chain.wait()
                    bank = masked[:]
                chain.step(dve.tensor_reduce(row_max[:], bank, AX.X, ALU.max))
                chain.wait()
                dve.tensor_tensor(pr[:], bank, row_max[:].unsqueeze(2).to_broadcast([P, 16, SEQ]), ALU.subtract
                                  ).then_inc(shifted, 1)

            def softmax_end(h, layer, m):
                n = 4 * layer + m
                dve.wait_ge(exp_ready, 8 * h + n + 1)
                chain.step(dve.tensor_reduce(den[:], pr[:], AX.X, ALU.add))
                chain.wait()
                if layer == 0:
                    chain.step(dve.tensor_scalar(den[:], den[:], DEN_EPS, None, ALU.add))
                    chain.wait()
                chain.step(dve.reciprocal(r_den[:], den[:]))
                chain.wait()
                chain.step(dve.tensor_tensor(pr[:], pr[:], r_den[:].unsqueeze(2).to_broadcast([P, 16, SEQ]), ALU.mult))
                chain.wait()
                for b in range(4):
                    rows = slice(32 * b, 32 * b + 32)
                    last = dve.transpose(pt_diag[m % 2][rows, :, rows], pr[rows])
                last.then_inc(pt_ready, 1)

            def attention(h, layer):
                for m in range(KC):
                    softmax(h, layer, m)
                    softmax_end(h, layer, m)
                    if m:
                        low_heads(h, layer, m - 1)
                low_heads(h, layer, 3)

            def gate_top(h):
                dve.wait_ge(gate_t_full, h + 1)
                stand_alone(dve, passed_dve)
                for t in range(HT):
                    chain.step(dve.max(top[:, t, :], gate_t_bank[:, t * NE:(t + 1) * NE]))
                chain.wait()
                chain.step(dve.tensor_copy(g_small[:, 0, :], top[:, :, 0]))
                chain.wait()
                dve.tensor_tensor(top[:], top[:], g_small[:, 0, :].unsqueeze(2).to_broadcast([P, HT, NE]),
                                  ALU.subtract).then_inc(top_ready, 1)

            def gate_weight(h):
                dve.wait_ge(top_exp, h + 1)
                chain.step(dve.tensor_reduce(g_small[:, 1, :], top[:], AX.X, ALU.add))
                chain.step(dve.tensor_tensor(g_small[:, 2, :], top[:, :, 0], top[:, :, 1], ALU.add))
                chain.wait()
                chain.step(dve.reciprocal(g_small[:, 3, :], g_small[:, 1, :]))
                chain.wait()
                chain.step(dve.tensor_tensor(g_small[:, 2, :], g_small[:, 2, :], g_small[:, 3, :], ALU.mult))
                chain.wait()
                chain.step(dve.tensor_scalar(g_small[:, 4, :], g_small[:, 2, :], TOPK_EPS, None, ALU.add))
                chain.wait()
                chain.step(dve.reciprocal(g_small[:, 3, :], g_small[:, 4, :]))
                chain.wait()
                dve.tensor_tensor(weight[:], g_small[:, 2, :], g_small[:, 3, :], ALU.mult).then_inc(weight_ready, 1)

            def silu(h, f, j):
                k = 8 * f + j
                dve.wait_ge(tanh_ready, 16 * h + k + 1)
                n = USE_UP[f] + j
                dve.scalar_tensor_tensor(act_buf[j % 2][:], act_buf[j % 2][:], 1.0, proj[n % 2][:], ALU.add, ALU.mult
                                         ).then_inc(silu_ready, 1)

            def low_h(h, f, j):
                k = 8 * f + j
                dve.wait_ge(h_hi, 16 * h + k + 1)
                dve.scalar_tensor_tensor(h_s[1][:, j, :], act_buf[j % 2][:], 0.5, h_s[0][:, j, :].bitcast(F32),
                                         ALU.mult, ALU.subtract).then_inc(h_lo, 1)

            def add_down(h, f, t):
                dve.wait_ge(down_full, 8 * h + 4 * f + t + 1 + CREDIT)
                dve.scalar_tensor_tensor(y[:, t, :], down_bank[t][:], weight[:, t:t + 1], y[:, t, :],
                                         ALU.mult, ALU.add).then_inc(down_read, 1)

            dve.wait_ge(const_in, 48)
            dve.wait_ge(gate_ready, 1)
            dve.tensor_tensor(gate_s[1][:, :, 0:NE], gate_raw[:], gate_s[0][:, :, 0:NE].bitcast(F32), ALU.subtract
                              ).then_inc(gate_ready, 1)
            for i in range(2):
                dve.memset(k_diag[i][:], 0.0).then_inc(kdiag_ready, 1)
                chain.step(dve.memset(pt_diag[i][:], 0.0))
            per = 63
            chain.enter(0, per)
            with dve.Fori(0, HALVES) as h:
                chain.base = chain.before + per * h
                low_raw_heads(h, 0)
                low_raw_heads(h, 1)
                for t in range(HT):
                    add_res(h, 0, t)
                    if t < 2:
                        low_raw_heads(h, t + 2)
                    if t >= 1:
                        layer_norm(h, 0, t - 1)
                    if t >= 2:
                        low_xt(h, 0, t - 2)
                layer_norm(h, 0, 3)
                low_xt(h, 0, 2)
                low_xt(h, 0, 3)
                dve.wait_ge(const_ready, 6)
                attention(h, 0)
                chain.wait()
                add_res(h, 1, 0)
                add_res(h, 1, 1)
                dve.wait_ge(stored, 16 * HT * h + CREDIT)
                layer_norm(h, 1, 0)
                add_res(h, 1, 2)
                layer_norm(h, 1, 1)
                rms_norm(h, 1, 0)
                add_res(h, 1, 3)
                layer_norm(h, 1, 2)
                rms_norm(h, 1, 1)
                low_xt(h, 1, 0)
                layer_norm(h, 1, 3)
                rms_norm(h, 1, 2)
                low_xt(h, 1, 1)
                rms_norm(h, 1, 3)
                low_xt(h, 1, 2)
                low_xt(h, 1, 3)
                attention(h, 1)
                add_res(h, 2, 0)
                for t in range(HT):
                    if t < 3:
                        add_res(h, 2, t + 1)
                    rms_norm(h, 2, t)
                    if t >= 1:
                        low_xt(h, 2, t - 1)
                low_xt(h, 2, 3)
                gate_top(h)
                for f in range(2):
                    for j in range(9):
                        if j < 8:
                            silu(h, f, j)
                        if j:
                            low_h(h, f, j - 1)
                        if f == 0 and j == 2:
                            gate_weight(h)
                            dve.wait_ge(weight_ready, h + 1)
                    for t in range(HT):
                        add_down(h, f, t)
                        if f == 1:
                            dve.wait_ge(down_read, 8 * h + 4 * f + t + 1 + CREDIT)
                            dve.tensor_tensor(y[:, t, :], y[:, t, :], res[:, t, :], ALU.add).then_inc(final, 1)
            chain.leave(HALVES)

        @block.tensor
        def _(pe):
            def project(h, stage, t):
                n = USE_WO[stage] + t
                w = unit_s[(0, 4, 8)[stage] % RING]
                if t == 0:
                    if stage:
                        pe.wait_ge(heads_lo, 12 * h + (8, 12)[stage - 1])
                    pe.wait_ge(unit_ready, 2 * NU * h + 2 * (0, 4, 8)[stage] + 2)
                    if stage == 0:
                        pe.wait_ge(silu_ready, 16 * h + CREDIT)
                if stage == 0:
                    pe.wait_ge(heads_lo, 12 * h + t + 1)
                pe.wait_ge(*proj_free(n, h))
                for c in range(KC):
                    last = product(pe, proj[n % 2][:], [s[:, c, t * P:(t + 1) * P] for s in heads_s],
                                   [s[:, c, :] for s in w], c == 0, c == KC - 1)
                last.then_inc(p_full[n % 2], 1)

            def transpose_x(h, stage, t):
                n = 4 * stage + t
                pe.wait_ge(x_hat_ready, 12 * h + n + 1)
                pe.wait_ge(t_free[n % 2], 6 * h + n // 2 + CREDIT)
                for c in range(KC):
                    last = pe.transpose(tr[n % 2][:, c * P:(c + 1) * P], x_hat[n % 2][:, c * P:(c + 1) * P], ident[:])
                last.then_inc(t_full[n % 2], 1)

            def values(h, layer, t):
                n = USE_V[layer] + t
                u = (1, 5)[layer]
                if t == 0:
                    pe.wait_ge(unit_ready, 2 * NU * h + 2 * u + 2)
                pe.wait_ge(t_free[t % 2], 6 * h + (4 * layer + t) // 2 + 1 + CREDIT)
                pe.wait_ge(*proj_free(n, h))
                for c in range(KC):
                    last = product(pe, proj[n % 2][:], [s[:, c, t * P:(t + 1) * P] for s in xt_s],
                                   [s[:, c, :] for s in unit_s[u % RING]], c == 0, c == KC - 1)
                last.then_inc(p_full[n % 2], 1)

            def features(h, u, n, m):
                if m == 0:
                    pe.wait_ge(unit_ready, 2 * NU * h + 2 * u + 2)
                k = n - USE_UP[0]
                if k < 2:
                    pe.wait_ge(*proj_free(n, h))
                else:
                    pe.wait_ge(silu_ready, 16 * h + k - 1 + CREDIT)
                for c in range(KC):
                    last = product(pe, proj[n % 2][:], [s[:, c, m * P:(m + 1) * P] for s in unit_s[u % RING]],
                                   [s[:, c, :] for s in xt_s], c == 0, c == KC - 1)
                last.then_inc(p_full[n % 2], 1)

            def keys_queries(h, layer, m):
                u, n = (2, 6)[layer], USE_KQ[layer] + 2 * m
                features(h, u, n, m)
                features(h, u + 1, n + 1, m)

            def scores(h, layer, m):
                n = 4 * layer + m
                k = (USE_KQ[layer] + 2 * m) // 2
                pe.wait_ge(p_free[0], FREES * h + k + 1 + CREDIT)
                pe.wait_ge(p_free[1], FREES * h + k + 1 + CREDIT)
                if n < 2:
                    pe.wait_ge(down_read, 8 * h + CREDIT)
                else:
                    pe.wait_ge(shifted, 8 * h + n - 1)
                for t in range(HT):
                    for b in range(4):
                        rows = slice(32 * b, 32 * b + 32)
                        last = pe.matmul(score_bank[n % 2][rows, t * P:(t + 1) * P],
                                         q_t[m % 2][:, t * P + 32 * b:t * P + 32 * b + 32],
                                         k_diag[m % 2][:, 4 * t + b, :], start=True, stop=True)
                last.then_inc(sc_full[n % 2], 1)

            def attend(h, layer, m):
                n = 4 * layer + m
                pe.wait_ge(pt_ready, 8 * h + n + 1)
                if n < 2:
                    pe.wait_ge(down_read, 8 * h + CREDIT)
                else:
                    pe.wait_ge(heads_lo, 12 * h + HT + n - 1)
                for t in range(HT):
                    for a in range(4):
                        rows = slice(32 * a, 32 * a + 32)
                        last = pe.matmul(out_bank[n % 2][rows, t * P:(t + 1) * P],
                                         v_tok[:, t, m * P + 32 * a:m * P + 32 * a + 32],
                                         pt_diag[m % 2][:, 4 * t + a, :], start=True, stop=True)
                last.then_inc(at_full[n % 2], 1)

            def attention(h, layer):
                keys_queries(h, layer, 0)
                keys_queries(h, layer, 1)
                scores(h, layer, 0)
                keys_queries(h, layer, 2)
                scores(h, layer, 1)
                attend(h, layer, 0)
                keys_queries(h, layer, 3)
                scores(h, layer, 2)
                attend(h, layer, 1)
                scores(h, layer, 3)
                attend(h, layer, 2)
                attend(h, layer, 3)

            def gate_logits(h):
                for bank in range(2):
                    pe.wait_ge(t_free[bank], 6 * h + 6 + CREDIT)
                pe.wait_ge(shifted, 8 * h + 8)
                for c in range(KC):
                    last = product(pe, gate_bank[:], [s[:, c, :] for s in gate_s], [s[:, c, :] for s in xt_s],
                                   c == 0, c == KC - 1)
                last.then_inc(gate_full, 1)

            def gate_transpose(h):
                pe.wait_ge(logits_ready, h + 1)
                stand_alone(pe, passed_pe)
                for t in range(HT):
                    last = pe.transpose(gate_t_bank[:, t * NE:(t + 1) * NE], logits[:, t * P:(t + 1) * P],
                                        ident[0:NE, 0:NE])
                last.then_inc(gate_t_full, 1)

            def down(h, f):
                for d in range(2):
                    u = (11, 15)[f] + d
                    pe.wait_ge(unit_ready, 2 * NU * h + 2 * u + 2)
                    pe.wait_ge(h_lo, 16 * h + 8 * f + 4 * d + 4)
                    for t in range(HT):
                        if d == 0 and f == 0:
                            if t < 2:
                                pe.wait_ge(top_ready, h + 1)
                            else:
                                pe.wait_ge(heads_lo, 12 * h + 12)
                        elif d == 0:
                            pe.wait_ge(down_read, 8 * h + t + 1 + CREDIT)
                        for c in range(KC):
                            last = product(pe, down_bank[t][:], [s[:, 4 * d + c, t * P:(t + 1) * P] for s in h_s],
                                           [s[:, c, :] for s in unit_s[u % RING]],
                                           d == 0 and c == 0, d == 1 and c == KC - 1)
                        if d == 1:
                            last.then_inc(down_full, 1)
                        elif t == HT - 1:
                            last.then_inc(down_half, 1)

            for free in p_full + p_free + t_free + [silu_ready, down_read, down_half, down_full, square_ready, stored]:
                pe.sem_inc(free, CREDIT)
            pe.wait_ge(gate_ready, 2)
            with pe.Fori(0, HALVES) as h:
                project(h, 0, 0)
                project(h, 0, 1)
                transpose_x(h, 0, 0)
                project(h, 0, 2)
                transpose_x(h, 0, 1)
                project(h, 0, 3)
                transpose_x(h, 0, 2)
                values(h, 0, 0)
                values(h, 0, 1)
                transpose_x(h, 0, 3)
                values(h, 0, 2)
                values(h, 0, 3)
                attention(h, 0)
                for t in range(HT):
                    project(h, 1, t)
                transpose_x(h, 1, 0)
                transpose_x(h, 1, 1)
                values(h, 1, 0)
                transpose_x(h, 1, 2)
                values(h, 1, 1)
                transpose_x(h, 1, 3)
                values(h, 1, 2)
                values(h, 1, 3)
                attention(h, 1)
                project(h, 2, 0)
                project(h, 2, 1)
                transpose_x(h, 2, 0)
                project(h, 2, 2)
                transpose_x(h, 2, 1)
                project(h, 2, 3)
                transpose_x(h, 2, 2)
                transpose_x(h, 2, 3)
                gate_logits(h)
                for f in range(2):
                    for j in range(8):
                        features(h, (9, 13)[f] + j // 4, USE_UP[f] + j, j % 4)
                        if f == 0 and j == 0:
                            gate_transpose(h)
                    down(h, f)


_INPUTS = ["x", "ctx_main", "ctx_last", "mask", "wq", "wk", "wv", "units", "gate", "n1", "n2", "bo"]


def kernel(**inputs):
    import numpy as np
    import concourse.bacc as _bacc
    from concourse.bass_utils import run_bass_kernel_spmd as _run

    a = {k: np.asarray(v) for k, v in inputs.items()}

    def by_rows(w):
        return np.ascontiguousarray(w.reshape(-1, P, w.shape[1]).transpose(1, 0, 2))

    ctx = a["ctx_768"]
    qkv, up, down = a["L0_ffn_qkv_w"], a["L0_ffn_up_w"], a["L0_ffn_down_w"]
    mats = {"x_wo": a["L0_xattn_Wo"], "a_v": a["L0_attn_Wv"].T, "a_k": a["L0_attn_Wk"].T,
            "a_q": a["L0_attn_Wq"].T, "a_wo": a["L0_attn_Wo"].T,
            "f_q": qkv[0:D].T, "f_k": qkv[D:2 * D].T, "f_v": qkv[2 * D:3 * D].T, "f_wo": a["L0_ffn_o_w"].T}
    for j in range(4):
        mats[f"up{j}"] = up[D * j:D * (j + 1)].T
        mats[f"down{j}"] = down[:, D * j:D * (j + 1)].T
    arrays = {
        "x": a["x"].reshape(NB * SEQ, D),
        "ctx_main": ctx[:, 0:MAIN].reshape(PAIRS, 2, MAIN, CC, P).transpose(0, 4, 3, 1, 2).reshape(PAIRS, P, CC, 2 * MAIN),
        "ctx_last": ctx[:, MAIN].reshape(NB, CC, P).transpose(2, 1, 0),
        "mask": a["mask_BxS2_bf1"].view(np.uint8),
        "wq": by_rows(a["L0_xattn_Wq"]),
        "wk": by_rows(a["L0_xattn_Wk"]),
        "wv": by_rows(a["L0_xattn_Wv"]),
        "units": np.stack([by_rows(mats[n]) for n in UNITS]),
        "gate": by_rows(a["L0_ffn_gate_w"].T),
        "n1": a["L0_ffn_n1_w"], "n2": a["L0_ffn_n2_w"], "bo": a["L0_attn_bo"],
    }
    nc = _bacc.Bacc("TRN2", target_bir_lowering=False, num_devices=1)
    named, args = {}, []
    for name in _INPUTS:
        named[f"in_{name}"] = np.ascontiguousarray(arrays[name])
        args.append(nc.dram_tensor(f"in_{name}", named[f"in_{name}"].shape,
                                   mybir.dt.from_np(named[f"in_{name}"].dtype), kind="ExternalInput").ap())
    args.append(nc.dram_tensor("out", (NB * SEQ, D), F32, kind="ExternalOutput").ap())
    build(nc, *args)
    got = _run(nc, [named], core_ids=[0])
    return got.results[0]["out"].reshape(NB, SEQ, D)
```

```python
from contextlib import ExitStack

import concourse.bass as bass
from concourse import mybir

F32 = mybir.dt.float32
F32R = mybir.dt.float32r
U8 = mybir.dt.uint8
ALU = mybir.AluOpType
ACT = mybir.ActivationFunctionType
AX = mybir.AxisListType

P = 128
D = 512
KC = D // P
CC = 3
HD = 32
SEQ = 32
NB = 32
KEYS = 257
MAIN = KEYS - 1
PAIRS = NB // 2
TILES = NB * SEQ // P
HALVES = 2
HT = TILES // HALVES
HALF = HT * P
HPAIRS = PAIRS // HALVES
NE = 8
SCALE = float(HD) ** -0.5
BIG = 1.0e38
LN_EPS = 1e-5
RMS_EPS = 1e-6
DEN_EPS = 1e-8
TOPK_EPS = 1e-9

CREDIT = 1

UNITS = ["x_wo", "a_v", "a_k", "a_q", "a_wo", "f_v", "f_k", "f_q", "f_wo",
         "up0", "up1", "down0", "down1", "up2", "up3", "down2", "down3"]
NU = len(UNITS)
RING = 3

USE_WO = (0, 16, 32)
USE_V = (4, 20)
USE_KQ = (8, 24)
USE_UP = (36, 44)
USES = 52 // 2
AT_USES = (3, 2)
FREES = 36 // 2


class Chain:

    def __init__(self, eng, sem):
        self.eng, self.sem, self.base, self.n = eng, sem, 0, 0

    def step(self, ins):
        ins.then_inc(self.sem, 1)
        self.n += 1

    def wait(self):
        self.eng.wait_ge(self.sem, self.base + self.n)

    def enter(self, i, per):
        self.before, self.per = self.base + self.n, per
        self.base, self.n = self.before + per * i, 0

    def leave(self, count):
        assert self.n == self.per, self.n
        self.base, self.n = self.before + self.per * count, 0


def wait(eng, sem, value):
    if not isinstance(value, int) or value > 0:
        eng.wait_ge(sem, value)


def stand_alone(eng, passed):
    eng.sem_inc(passed, 1)


def product(pe, out, left, right, first, last):
    pe.matmul(out, left[0], right[0], start=first, stop=False)
    pe.matmul(out, left[0], right[1], start=False, stop=False)
    return pe.matmul(out, left[1], right[0], start=False, stop=last)


class Shared:

    def __init__(self, nc, stack):
        self.raw = stack.enter_context(nc.sbuf_tensor("raw", [P, KC, D], F32))
        self.heads_raw = stack.enter_context(nc.sbuf_tensor("heads_raw", [P, KC, HALF], F32R))
        self.gate_raw = stack.enter_context(nc.sbuf_tensor("gate_raw", [P, KC, NE], F32))
        self.gate_s = [stack.enter_context(nc.sbuf_tensor(f"gate_{part}", [P, KC, P], F32R)) for part in ("hi", "lo")]
        self.rows = [stack.enter_context(nc.sbuf_tensor(name, [P, D], F32)) for name in ("n1_all", "n2_all", "bo_all")]
        self.causal = stack.enter_context(nc.sbuf_tensor("causal", [P, SEQ], F32))
        self.heads_out = [stack.enter_context(nc.semaphore(f"heads_out{i}")) for i in range(2)]
        self.const_in = stack.enter_context(nc.semaphore("const_in"))
        self.gate_step = stack.enter_context(nc.semaphore("gate_step"))
        self.causal_step = stack.enter_context(nc.semaphore("causal_step"))
        self.unit_in = [stack.enter_context(nc.semaphore(f"unit_in{i}")) for i in range(2)]
        self.heads_in = stack.enter_context(nc.semaphore("c_heads_in"))


def load_heads(sp, shared, heads_dram, h):
    sp.dma_start(shared.heads_raw[:].bitcast(F32).rearrange("p t d -> p (t d)").rearrange("p (q n) -> p q n", q=HPAIRS),
                 heads_dram.rearrange("(h q) p n -> h p q n", h=HALVES)[bass.ds(h, 1)]
                 .rearrange("o p q n -> (o p) q n")).then_inc(shared.heads_in, 16)


def build(nc, x, ctx_main, ctx_last, mask, wq, wk, wv, units, gate, n1, n2, bo, out):
    heads_dram = nc.dram_tensor("heads_scratch", (PAIRS, P, 256), F32, kind="Internal").ap()
    vlast_dram = nc.dram_tensor("vlast_scratch", (NB, 4, P), F32, kind="Internal").ap()
    with ExitStack() as stack:
        banks = {}
        for name in ("proj0", "proj1", "tr0", "tr1", "s0", "s1", "o0", "o1"):
            banks[name] = stack.enter_context(nc.psum_tensor(name, [P, 512], F32))
        ident = stack.enter_context(nc.sbuf_tensor("ident", [P, P], F32))
        shared = Shared(nc, stack)
        cross_attention(nc, banks, ident, shared, x, ctx_main, ctx_last, mask, wq, wk, wv,
                        heads_dram, vlast_dram, units, gate, n1, n2, bo)
        rest_of_layer(nc, banks, ident, shared, x, heads_dram, units, out)


def cross_attention(nc, banks, ident, shared, x, ctx_main, ctx_last, mask, wq, wk, wv,
                    heads_dram, vlast_dram, units, gate, n1, n2, bo):
    x_tiles = x.rearrange("(t p) d -> t p d", p=P)
    mask_pairs = mask.rearrange("(q b) j -> q b j", b=2)
    with ExitStack() as stack:
        def sb(name, shape, dt=F32):
            return stack.enter_context(nc.sbuf_tensor(name, shape, dt))

        def sem(name):
            return stack.enter_context(nc.semaphore(name))

        def split_pair(name, shape):
            return sb(name + "_hi", shape, F32R), sb(name + "_lo", shape, F32R)

        proj = [banks["proj0"], banks["proj1"]]
        tr = [banks["tr0"], banks["tr1"]]
        score_bank = [banks["s0"], banks["s1"], *tr]
        out_bank = [banks["o0"], banks["o1"]]

        wq_raw = shared.raw
        wk_s, wv_s, wq_s = split_pair("wk", [P, CC, D]), split_pair("wv", [P, CC, D]), split_pair("wq", [P, KC, D])
        last_raw = sb("ctx_last_raw", [P, CC, NB])
        last_s = split_pair("ctx_last", [P, CC, P])
        k_last = split_pair("k_last", [P, KC, NB])
        v_last_all = sb("v_last_all", [P, NB, P])
        ctx_raw = [sb(f"ctx_raw{i}", [P, CC, 512]) for i in range(2)]
        wk_raw = ctx_raw[1]
        ctx_s = [split_pair(f"ctx{i}", [P, CC, 512]) for i in range(2)]
        mask_raw = [sb(f"mask_raw{i}", [P, 2, KEYS], U8) for i in range(2)]
        mask_bias = [sb(f"mask_bias{i}", [P, 2, KEYS]) for i in range(2)]
        k_s = split_pair("k", [P, KC, 2, KEYS + 1])
        v_sb = [sb(f"v_sb{i}", [P, 2, 2, D]) for i in range(2)]
        probs = sb("probs", [P, 2, KC, KEYS])
        wv_raw = probs[:].rearrange("p b g n -> p (b g n)")[:, 0:CC * D].rearrange("p (c n) -> p c n", c=CC)
        v_last = probs[0:NB, 0, :, 0:P]
        probs_t = sb("probs_t", [P, 2, 2, KC, P])
        last_rows = probs_t[:, 0, 0].rearrange("p g n -> p (g n)")
        x_raw = sb("x_raw", [P, D])
        x_hat = sb("x_hat", [P, D])
        x_t = split_pair("x_t", [P, KC, P])
        q_sb = x_hat
        q_diag = split_pair("q_diag", [P, 16, P])
        stats = sb("stats", [P, 6])
        mean_var = sb("mean_var", [P, 2])
        var_eps = sb("var_eps", [P, 1])
        rstd = sb("rstd", [P, 1])
        minus_half = sb("minus_half", [P, 1])
        row_max = sb("row_max", [P, 2, KC])
        exp_bias = sb("exp_bias", [P, 2, KC])
        denom = sb("denom", [P, 2, KC])
        r_denom = sb("r_denom", [P, 8])
        last_part = sb("last_part", [P, 8, HD])
        heads = sb("heads", [P, 8, HD])
        heads_t = [sb(f"heads_t{i}", [P, 8 * SEQ]) for i in range(2)]

        passed_pool, passed_dve, passed_sp = sem("passed_pool"), sem("passed_dve"), sem("passed_sp")
        w_in = [sem(f"w_in{i}") for i in range(3)]
        w_hi, w_lo = sem("w_hi"), sem("w_lo")
        last_in, last_zero = sem("last_in"), sem("last_zero")
        first_hi, last_rows_full, last_rows_copied = sem("first_hi"), sem("last_rows_full"), sem("last_rows_copied")
        last_k_full, last_v_full, last_k_done, last_v_done = (
            sem("last_k_full"), sem("last_v_full"), sem("last_k_done"), sem("last_v_done"))
        vlast_out, vlast_in = sem("vlast_out"), sem("vlast_in")
        ctx_in = [sem(f"ctx_in{i}") for i in range(2)]
        mask_in = [sem(f"mask_in{i}") for i in range(2)]
        x_in = sem("x_in")
        ctx_ready, mask_ready, k_last_ready = sem("ctx_ready"), sem("mask_ready"), sem("k_last_ready")
        ident_ready, diag_zero, pool_step, dve_step = sem("ident_ready"), sem("diag_zero"), sem("pool_step"), sem("dve_step")
        var_ready, rstd_ready, x_hat_ready = sem("var_ready"), sem("rstd_ready"), sem("x_hat_ready")
        xt_full, xt_hi, xt_lo = sem("xt_full"), sem("xt_hi"), sem("xt_lo")
        q_full, q_copied, qt_full, q_diag_ready = sem("q_full"), sem("q_copied"), sem("qt_full"), sem("q_diag_ready")
        qt_copied, q_hi_ready, k_hi_ready = sem("qt_copied"), sem("q_hi_ready"), sem("k_hi_ready")
        k_full = [sem(f"k_full{i}") for i in range(2)]
        k_done = [sem(f"k_done{i}") for i in range(2)]
        v_full = [sem(f"v_full{i}") for i in range(2)]
        v_done = [sem(f"v_done{i}") for i in range(2)]
        s_full, s_read = sem("s_full"), sem("s_read")
        bias_ready, exp_done = sem("bias_ready"), sem("exp_done")
        pt_full = [sem(f"pt_full{i}") for i in range(2)]
        pt_done = [sem(f"pt_done{i}") for i in range(2)]
        pv_full, pv_read, heads_ready = sem("pv_full"), sem("pv_read"), sem("heads_ready")
        heads_out, gate_step, gate_s = shared.heads_out, shared.gate_step, shared.gate_s

        block = stack.enter_context(nc.Block())

        @block.sync
        def _(sp):
            def load_pair(t, par):
                q = 2 * t + par
                sp.dma_start(ctx_raw[par][:], ctx_main[bass.ds(q, 1)].rearrange("o p c n -> (o p) c n")
                             ).then_inc(ctx_in[par], 16)

            def load_mask(t, par):
                q = 2 * t + par
                sp.dma_start(mask_raw[par][:],
                             mask_pairs[bass.ds(q, 1)].rearrange("o b j -> (o b) j").unsqueeze(0)
                             .to_broadcast([P, 2, KEYS])).then_inc(mask_in[par], 16)

            def store_heads(t, par):
                q = 2 * t + par
                sp.wait_ge(heads_ready, q + 1)
                stand_alone(sp, passed_sp)
                sp.dma_start(heads_dram[bass.ds(q, 1)].rearrange("o p n -> (o p) n"), heads_t[par][:]
                             ).then_inc(heads_out[par], 16)

            sp.dma_start(last_raw[:], ctx_last).then_inc(last_in, 16)
            sp.dma_start(wk_raw[:], wk).then_inc(w_in[0], 16)
            load_mask(0, 0)
            load_pair(0, 0)
            sp.dma_start(x_raw[:], x_tiles[0]).then_inc(x_in, 16)
            sp.dma_start(wv_raw, wv).then_inc(w_in[1], 16)
            sp.dma_start(wq_raw[:], wq).then_inc(w_in[2], 16)
            load_mask(0, 1)
            sp.wait_ge(w_lo, 1)
            load_pair(0, 1)
            sp.wait_ge(last_v_done, 1)
            sp.dma_start(vlast_dram, v_last).then_inc(vlast_out, 16)
            sp.wait_ge(vlast_out, 16)
            for a in range(4):
                sp.dma_start(v_last_all[32 * a:32 * a + 32],
                             vlast_dram[:, a, :].unsqueeze(0).to_broadcast([SEQ, NB, P])
                             ).then_inc(vlast_in, 16)
            sp.dma_start(shared.gate_raw[:], gate).then_inc(shared.const_in, 16)
            for row, vector in zip(shared.rows, (n1, n2, bo)):
                sp.dma_start(row[:], vector.unsqueeze(0).to_broadcast([P, D])).then_inc(shared.const_in, 16)
            sp.wait_ge(w_lo, 4)
            for v in range(2):
                sp.dma_start(shared.raw[:, 2 * v:2 * v + 2, :], units[0, :, 2 * v:2 * v + 2, :]
                             ).then_inc(shared.unit_in[v], 16)
            with sp.Fori(0, TILES - 1) as t:
                sp.wait_ge(x_hat_ready, t + 1)
                stand_alone(sp, passed_sp)
                sp.dma_start(x_raw[:], x_tiles[bass.ds(t + 1, 1)].rearrange("o p d -> (o p) d")
                             ).then_inc(x_in, 16)
                for par in range(2):
                    sp.wait_ge(ctx_ready, 2 * t + par + 1)
                    stand_alone(sp, passed_sp)
                    load_pair(t + 1, par)
                    sp.wait_ge(mask_ready, 2 * t + par + 1)
                    stand_alone(sp, passed_sp)
                    load_mask(t + 1, par)
                    store_heads(t, par)
            for par in range(2):
                sp.wait_ge(heads_out[par], 16 * TILES // HALVES + CREDIT)
            load_heads(sp, shared, heads_dram, 0)
            for par in range(2):
                store_heads(TILES - 1, par)

        @block.gpsimd
        def _(pool):
            chain = Chain(pool, pool_step)

            pool.sem_inc(v_full[1], CREDIT)

            def bias_of_mask(t, par):
                q = 2 * t + par
                wait(pool, s_read, 8 * q - 8 + KC)
                pool.wait_ge(mask_in[par], 16 * t + 16)
                stand_alone(pool, passed_pool)
                pool.tensor_scalar(mask_bias[par][:], mask_raw[par][:], BIG, -BIG, ALU.mult, ALU.add
                                   ).then_inc(mask_ready, 1)

            def low_ctx(par):
                hi, lo = ctx_s[par]
                pool.tensor_tensor(lo[:], ctx_raw[par][:], hi[:].bitcast(F32), ALU.subtract
                                   ).then_inc(ctx_ready, 1)

            def split_ctx(t, par):
                q = 2 * t + par
                bias_of_mask(t, par)
                wait(pool, v_full[1], 2 * q - 2 + CREDIT)
                pool.wait_ge(ctx_in[par], 16 * t + 16)
                stand_alone(pool, passed_pool)
                chain.step(pool.tensor_scalar(ctx_s[par][0][:], ctx_raw[par][:], 1.0, None, ALU.mult))
                chain.wait()
                low_ctx(par)

            def root(t):
                pool.wait_ge(var_ready, t + 1)
                stand_alone(pool, passed_pool)
                chain.step(pool.tensor_scalar(var_eps[:], mean_var[:, 1:2], LN_EPS, None, ALU.add))
                chain.wait()
                pool.tensor_tensor(rstd[:], var_eps[:], minus_half[:], ALU.pow).then_inc(rstd_ready, 1)

            def low_q(t):
                pool.wait_ge(q_hi_ready, t + 1)
                stand_alone(pool, passed_pool)
                for a in range(4):
                    rows = slice(32 * a, 32 * a + 32)
                    pool.tensor_tensor(q_diag[1][rows, :, rows], q_sb[rows, :].rearrange("p (n i) -> p n i", i=SEQ),
                                       q_diag[0][rows, :, rows].bitcast(F32), ALU.subtract).then_inc(q_diag_ready, 1)
                    pool.wait_ge(q_diag_ready, 4 * t + a + 1)

            for part in last_s:
                pool.memset(part[:].bitcast(F32), 0.0).then_inc(last_zero, 1)
            chain.step(pool.memset(minus_half[:], -0.5))
            chain.step(pool.memset(ident[:], 0.0))
            chain.wait()
            pool.affine_select(out=ident[:], in_=ident[:], compare_op=ALU.not_equal, fill=1.0, base=0,
                               pattern=[[-1, P]], channel_multiplier=1).then_inc(ident_ready, 1)
            root(0)
            pool.wait_ge(first_hi, 1)
            low_ctx(0)
            bias_of_mask(0, 0)
            for part in q_diag:
                pool.memset(part[:].bitcast(F32), 0.0).then_inc(diag_zero, 1)
            for part in k_s:
                pool.memset(part[:, :, :, KEYS:].bitcast(F32), 0.0).then_inc(diag_zero, 1)
            for part in gate_s:
                pool.memset(part[:].bitcast(F32), 0.0).then_inc(gate_step, 1)
            pool.memset(shared.causal[:], 0.0).then_inc(shared.causal_step, 1)
            pool.wait_ge(shared.causal_step, 1)
            for b in range(4):
                rows = slice(32 * b, 32 * b + 32)
                pool.affine_select(out=shared.causal[rows, :], in_=shared.causal[rows, :], compare_op=ALU.is_ge,
                                   fill=-BIG, base=0, pattern=[[-1, SEQ]], channel_multiplier=1
                                   ).then_inc(shared.causal_step, 1)
                pool.wait_ge(shared.causal_step, b + 2)
            split_ctx(0, 1)
            low_q(0)
            with pool.Fori(0, TILES - 1) as t:
                chain.enter(t, 3)
                root(t + 1)
                split_ctx(t + 1, 0)
                split_ctx(t + 1, 1)
                low_q(t + 1)
            chain.leave(TILES - 1)

        @block.scalar
        def _(act):
            def high_k(t, par, j):
                q = 2 * t + par
                act.wait_ge(k_full[1], 2 * q + j + 1)
                act.activation(k_s[0][:, 2 * j + 1, :, 0:MAIN],
                               proj[1][:].rearrange("p (b n) -> p b n", b=2), ACT.Copy).then_inc(k_hi_ready, 1)

            def copy_v(t, par, j):
                q = 2 * t + par
                for bank in range(j + 1):
                    act.wait_ge(v_full[bank], 2 * q + j + 1 + CREDIT * bank)
                    act.activation(v_sb[par][:, j, bank, :], proj[bank][:], ACT.Copy).then_inc(v_done[bank], 1)

            def exps(t, par, b):
                q = 2 * t + par
                act.wait_ge(bias_ready, 2 * q + b + 1)
                for g in range(KC):
                    last = act.activation(probs[:, b, g, :], probs[:, b, g, :], ACT.Exp,
                                          bias=exp_bias[:, b, g:g + 1], scale=SCALE,
                                          accum_out=denom[:, b, g:g + 1])
                last.then_inc(exp_done, 1)

            def copy_pt(t, par, b):
                q = 2 * t + par
                act.wait_ge(pt_full[0], 2 * q + b + 1)
                act.activation(probs_t[:, b, 0].rearrange("p g n -> p (g n)"), tr[0][:], ACT.Copy
                               ).then_inc(pt_done[0], 1)

            def copy_xt(t):
                act.wait_ge(xt_full, t + 1)
                act.activation(x_t[0][:].rearrange("p c n -> p (c n)"), tr[0][:], ACT.Copy).then_inc(xt_hi, 1)

            def high_q(t):
                act.wait_ge(qt_full, t + 1)
                act.activation(q_sb[:], tr[0][:], ACT.Copy).then_inc(qt_copied, 1)
                act.wait_ge(qt_copied, t + 1)
                for a in range(4):
                    rows = slice(32 * a, 32 * a + 32)
                    last = act.activation(q_diag[0][rows, :, rows],
                                          q_sb[rows, :].rearrange("p (n i) -> p n i", i=SEQ), ACT.Copy)
                last.then_inc(q_hi_ready, 1)

            for n, (raw, parts) in enumerate(((wk_raw[:], wk_s), (wv_raw, wv_s), (wq_raw[:], wq_s))):
                act.wait_ge(w_in[n], 16)
                act.activation(parts[0][:], raw, ACT.Copy).then_inc(w_hi, 1)
                if n == 0:
                    act.wait_ge(last_in, 16)
                    act.wait_ge(last_zero, 2)
                    act.activation(last_s[0][:, :, 0:NB], last_raw[:], ACT.Copy).then_inc(w_hi, 1)
                    act.wait_ge(ctx_in[0], 16)
                    act.activation(ctx_s[0][0][:], ctx_raw[0][:], ACT.Copy).then_inc(first_hi, 1)
                if n == 1:
                    copy_xt(0)
            act.wait_ge(last_v_full, 1)
            act.activation(v_last.rearrange("p a (g d) -> p a g d", g=4),
                           score_bank[0][0:NB, :].rearrange("p (g a d) -> p a g d", g=4, a=4), ACT.Copy
                           ).then_inc(last_v_done, 1)
            high_k(0, 0, 0)
            high_k(0, 0, 1)
            act.wait_ge(diag_zero, 4)
            high_q(0)
            copy_v(0, 0, 0)
            copy_v(0, 0, 1)
            act.wait_ge(shared.const_in, 64)
            act.wait_ge(gate_step, 2)
            act.activation(gate_s[0][:, :, 0:NE], shared.gate_raw[:], ACT.Copy).then_inc(gate_step, 1)

            def even_pair(t):
                exps(t, 0, 0)
                exps(t, 0, 1)
                high_k(t, 1, 0)
                high_k(t, 1, 1)
                copy_pt(t, 0, 0)
                copy_pt(t, 0, 1)
                copy_v(t, 1, 0)
                copy_v(t, 1, 1)

            with act.Fori(0, TILES - 1) as t:
                even_pair(t)
                exps(t, 1, 0)
                exps(t, 1, 1)
                copy_xt(t + 1)
                high_k(t + 1, 0, 0)
                high_k(t + 1, 0, 1)
                high_q(t + 1)
                copy_pt(t, 1, 0)
                copy_pt(t, 1, 1)
                copy_v(t + 1, 0, 0)
                copy_v(t + 1, 0, 1)
            even_pair(TILES - 1)
            exps(TILES - 1, 1, 0)
            exps(TILES - 1, 1, 1)
            copy_pt(TILES - 1, 1, 0)
            copy_pt(TILES - 1, 1, 1)

        @block.vector
        def _(dve):
            chain = Chain(dve, dve_step)

            def split_k(t, par, j):
                q = 2 * t + par
                dve.wait_ge(k_full[0], 2 * q + j + 1)
                bank = proj[0][:].rearrange("p (b n) -> p b n", b=2)
                hi, lo = (s[:, 2 * j, :, 0:MAIN] for s in k_s)
                chain.step(dve.tensor_copy(hi, bank))
                chain.wait()
                dve.tensor_tensor(lo, bank, hi.bitcast(F32), ALU.subtract).then_inc(k_done[0], 1)

            def low_k(t, par, j):
                q = 2 * t + par
                dve.wait_ge(k_hi_ready, 2 * q + j + 1)
                hi, lo = (s[:, 2 * j + 1, :, 0:MAIN] for s in k_s)
                dve.tensor_tensor(lo, proj[1][:].rearrange("p (b n) -> p b n", b=2), hi.bitcast(F32), ALU.subtract
                                  ).then_inc(k_done[1], 1)

            def last_key(t, par):
                q = 2 * t + par
                for part, of_all in zip(k_s, k_last):
                    dve.tensor_scalar(part[:, :, :, MAIN], of_all[:, :, bass.ds(2 * q, 2)].bitcast(F32), 1.0, None,
                                      ALU.mult).then_inc(k_last_ready, 1)

            def copy_v(t, par):
                q = 2 * t + par
                dve.wait_ge(v_full[1], 2 * q + 1 + CREDIT)
                dve.tensor_copy(v_sb[par][:, 0, 1, :], proj[1][:]).then_inc(v_done[1], 1)

            def mask_max(t, par):
                q = 2 * t + par
                dve.wait_ge(mask_ready, q + 1)
                for b in range(2):
                    for g in range(KC):
                        dve.wait_ge(s_full, 8 * q + 4 * b + g + 1)
                        stand_alone(dve, passed_dve)
                        dve.tensor_tensor_reduce(
                            out=probs[:, b, g, :], in0=score_bank[g][:, 0:KEYS], in1=mask_bias[par][:, b, :],
                            scale=1.0, scalar=-3.0e38, op0=ALU.add, op1=ALU.max,
                            accum_out=row_max[:, b, g:g + 1]).then_inc(s_read, 1)
                    dve.wait_ge(s_read, 8 * q + 4 * b + 4 + KC)
                    dve.tensor_scalar(exp_bias[:, b, :], row_max[:, b, :], -SCALE, None, ALU.mult
                                      ).then_inc(bias_ready, 1)

            def copy_pt(t, par, b):
                q = 2 * t + par
                dve.wait_ge(pt_full[1], 2 * q + b + 1)
                dve.tensor_copy(probs_t[:, b, 1].rearrange("p g n -> p (g n)"), tr[1][:]).then_inc(pt_done[1], 1)

            def norm_stats(t):
                dve.wait_ge(x_in, 16 * t + 16)
                chain.step(dve.bn_stats(stats[:], x_raw[:]))
                chain.wait()
                stand_alone(dve, passed_dve)
                dve.bn_aggr(mean_var[:], stats[:]).then_inc(var_ready, 1)

            def norm_apply(t):
                dve.wait_ge(rstd_ready, t + 1)
                wait(dve, q_diag_ready, 4 * t)
                dve.tensor_scalar(x_hat[:], x_raw[:], mean_var[:, 0:1], rstd[:, 0:1], ALU.subtract, ALU.mult
                                  ).then_inc(x_hat_ready, 1)

            def low_xt(t):
                dve.wait_ge(xt_hi, t + 1)
                dve.tensor_tensor(x_t[1][:].rearrange("p c n -> p (c n)"), tr[0][:],
                                  x_t[0][:].rearrange("p c n -> p (c n)").bitcast(F32), ALU.subtract
                                  ).then_inc(xt_lo, 1)

            def copy_q_rows(t):
                dve.wait_ge(q_full, t + 1)
                dve.tensor_copy(q_sb[:], tr[1][:]).then_inc(q_copied, 1)

            def finish_heads(t, par):
                q = 2 * t + par
                dve.wait_ge(exp_done, 2 * q + 2)
                chain.step(dve.reciprocal(r_denom[:], denom[:].rearrange("p b g -> p (b g)")))
                chain.step(dve.tensor_tensor(
                    last_part[:], probs[:, :, :, MAIN].rearrange("p b g -> p (b g)").unsqueeze(2).to_broadcast([P, 8, HD]),
                    v_last_all[:, bass.ds(2 * q, 2), :].rearrange("p b (g d) -> p (b g) d", g=4), ALU.mult))
                chain.wait()
                dve.wait_ge(pv_full, 2 * q + 2)
                for b in range(2):
                    for a in range(4):
                        rows = slice(32 * a, 32 * a + 32)
                        part = dve.tensor_tensor(
                            heads[rows, 4 * b:4 * b + 4, :],
                            out_bank[b][rows, :].rearrange("p (g n) -> p g n", g=4)[:, :, rows],
                            last_part[rows, 4 * b:4 * b + 4, :], ALU.add)
                part.then_inc(pv_read, 1)
                dve.wait_ge(pv_read, q + 1 + CREDIT)
                chain.step(dve.tensor_tensor(heads[:], heads[:], r_denom[:].unsqueeze(2).to_broadcast([P, 8, HD]), ALU.mult))
                chain.wait()
                dve.wait_ge(heads_out[par], 16 * t + CREDIT)
                dve.transpose(heads_t[par][:], heads[:].rearrange("p n d -> p (n d)")).then_inc(heads_ready, 1)

            for par in range(2):
                dve.sem_inc(heads_out[par], CREDIT)
            dve.sem_inc(s_read, KC)
            for n, (raw, parts) in enumerate(((wk_raw[:], wk_s), (last_raw[:], last_s), (wv_raw, wv_s), (wq_raw[:], wq_s))):
                dve.wait_ge(w_hi, n + 1)
                cols = NB if n == 1 else D
                dve.tensor_tensor(parts[1][:, :, 0:cols], raw, parts[0][:, :, 0:cols].bitcast(F32), ALU.subtract
                                  ).then_inc(w_lo, 1)
                if n == 1:
                    norm_stats(0)
                    norm_apply(0)
                    dve.wait_ge(last_rows_full, 1)
                    dve.tensor_copy(last_rows, score_bank[0][:]).then_inc(last_rows_copied, 1)
                    dve.wait_ge(last_k_full, 1)
                    bank = score_bank[1][:].rearrange("p (g n) -> p g n", g=4)[:, :, 0:NB]
                    chain.step(dve.tensor_copy(k_last[0][:], bank))
                    chain.wait()
                    dve.tensor_tensor(k_last[1][:], bank, k_last[0][:].bitcast(F32), ALU.subtract
                                      ).then_inc(last_k_done, 1)
                    dve.wait_ge(last_k_done, 1)
                if n == 2:
                    low_xt(0)
            split_k(0, 0, 0)
            low_k(0, 0, 0)
            copy_q_rows(0)
            split_k(0, 0, 1)
            low_k(0, 0, 1)
            last_key(0, 0)
            dve.wait_ge(diag_zero, 4)
            copy_v(0, 0)
            dve.wait_ge(vlast_in, 64)
            dve.wait_ge(gate_step, 3)
            dve.tensor_tensor(gate_s[1][:, :, 0:NE], shared.gate_raw[:], gate_s[0][:, :, 0:NE].bitcast(F32), ALU.subtract
                              ).then_inc(gate_step, 1)

            def even_pair(t, more):
                mask_max(t, 0)
                split_k(t, 1, 0)
                low_k(t, 1, 0)
                if more:
                    norm_stats(t + 1)
                split_k(t, 1, 1)
                low_k(t, 1, 1)
                last_key(t, 1)
                copy_pt(t, 0, 0)
                copy_pt(t, 0, 1)
                if more:
                    norm_apply(t + 1)
                copy_v(t, 1)
                finish_heads(t, 0)

            with dve.Fori(0, TILES - 1) as t:
                chain.enter(t, 11)
                even_pair(t, True)
                mask_max(t, 1)
                split_k(t + 1, 0, 0)
                low_xt(t + 1)
                low_k(t + 1, 0, 0)
                split_k(t + 1, 0, 1)
                copy_q_rows(t + 1)
                low_k(t + 1, 0, 1)
                last_key(t + 1, 0)
                copy_pt(t, 1, 0)
                copy_pt(t, 1, 1)
                copy_v(t + 1, 0)
                finish_heads(t, 1)
            chain.leave(TILES - 1)
            even_pair(TILES - 1, False)
            mask_max(TILES - 1, 1)
            copy_pt(TILES - 1, 1, 0)
            copy_pt(TILES - 1, 1, 1)
            finish_heads(TILES - 1, 1)

        @block.tensor
        def _(pe):
            def keys(t, par, j, on=(0, 1)):
                q = 2 * t + par
                pe.wait_ge(ctx_ready, q + 1)
                for bank in on:
                    g = 2 * j + bank
                    if j == 0:
                        wait(pe, v_done[bank], 2 * q)
                    else:
                        pe.wait_ge(k_done[bank], 2 * q + 1)
                    for c in range(CC):
                        last = product(pe, proj[bank][:], [w[:, c, g * P:(g + 1) * P] for w in wk_s],
                                       [s[:, c, :] for s in ctx_s[par]], c == 0, c == CC - 1)
                    last.then_inc(k_full[bank], 1)

            def values(t, par, b, on=(0, 1)):
                q = 2 * t + par
                for bank in on:
                    if b == 0:
                        pe.wait_ge(k_done[bank], 2 * q + 2)
                    else:
                        pe.wait_ge(v_done[bank], 2 * q + 1)
                    at = slice(MAIN * b + P * bank, MAIN * b + P * bank + P)
                    for c in range(CC):
                        last = product(pe, proj[bank][:], [s[:, c, at] for s in ctx_s[par]],
                                       [w[:, c, :] for w in wv_s], c == 0, c == CC - 1)
                    last.then_inc(v_full[bank], 1)

            def scores(t, par):
                q = 2 * t + par
                for bank in range(2):
                    pe.wait_ge(k_done[bank], 2 * q + 2)
                pe.wait_ge(k_last_ready, 2 * q + 2)
                pe.wait_ge(q_diag_ready, 4 * t + 4)
                for b in range(2):
                    for g in range(KC):
                        pe.wait_ge(s_read, 8 * q + 4 * b + g + 1)
                        product(pe, score_bank[g][:, 0:KEYS + 1], [s[:, 4 * g + 2 * par + b, :] for s in q_diag],
                                [s[:, g, b, :] for s in k_s], True, True).then_inc(s_full, 1)

            def transpose_x(t):
                pe.wait_ge(x_hat_ready, t + 1)
                if not isinstance(t, int):
                    pe.wait_ge(s_read, 16 * t + KC - 1)
                for c in range(KC):
                    last = pe.transpose(tr[0][:, c * P:(c + 1) * P], x_hat[:, c * P:(c + 1) * P], ident[:])
                last.then_inc(xt_full, 1)

            def queries(t):
                pe.wait_ge(xt_lo, t + 1)
                if not isinstance(t, int):
                    pe.wait_ge(s_read, 16 * t + KC)
                for c in range(KC):
                    last = product(pe, tr[1][:], [s[:, c, :] for s in x_t], [w[:, c, :] for w in wq_s],
                                   c == 0, c == KC - 1)
                last.then_inc(q_full, 1)

            def transpose_q(t):
                pe.wait_ge(q_copied, t + 1)
                for g in range(KC):
                    last = pe.transpose(tr[0][:, g * P:(g + 1) * P], q_sb[:, g * P:(g + 1) * P], ident[:])
                last.then_inc(qt_full, 1)

            def transpose_probs(t, par, b):
                q = 2 * t + par
                if b == 0:
                    pe.wait_ge(s_read, 8 * q + 8 + KC)
                pe.wait_ge(exp_done, 2 * q + b + 1)
                for c in range(2):
                    pe.wait_ge(pt_done[c], 2 * q + b + CREDIT)
                    for g in range(KC):
                        last = pe.transpose(tr[c][:, g * P:(g + 1) * P], probs[:, b, g, c * P:(c + 1) * P], ident[:])
                    last.then_inc(pt_full[c], 1)

            def attend(t, par):
                q = 2 * t + par
                for bank in range(2):
                    pe.wait_ge(v_done[bank], 2 * q + 2)
                pe.wait_ge(pv_read, q + CREDIT)
                for b in range(2):
                    for c in range(2):
                        pe.wait_ge(pt_done[c], 2 * q + b + 1 + CREDIT)
                    for g in range(KC):
                        for c in range(2):
                            last = pe.matmul(out_bank[b][:, g * P:(g + 1) * P], probs_t[:, b, c, g, :],
                                             v_sb[par][:, b, c, g * P:(g + 1) * P], start=c == 0, stop=c == 1)
                    last.then_inc(pv_full, 1)

            for free in (pt_done[0], pt_done[1], pv_read):
                pe.sem_inc(free, CREDIT)
            pe.wait_ge(ident_ready, 1)
            pe.wait_ge(w_lo, 2)
            for c in range(CC):
                last = product(pe, score_bank[0][:], [s[:, c, :] for s in last_s], [w[:, c, :] for w in wk_s],
                               c == 0, c == CC - 1)
            last.then_inc(last_rows_full, 1)
            transpose_x(0)
            pe.wait_ge(last_rows_copied, 1)
            for g in range(KC):
                last = pe.transpose(score_bank[1][:, g * P:(g + 1) * P], last_rows[:, g * P:(g + 1) * P], ident[:])
            last.then_inc(last_k_full, 1)
            keys(0, 0, 0)
            pe.wait_ge(w_lo, 3)
            for c in range(CC):
                last = product(pe, score_bank[0][:], [s[:, c, :] for s in last_s], [w[:, c, :] for w in wv_s],
                               c == 0, c == CC - 1)
            last.then_inc(last_v_full, 1)
            pe.wait_ge(w_lo, 4)
            queries(0)
            keys(0, 0, 1)
            transpose_q(0)
            values(0, 0, 0)
            values(0, 0, 1)

            def even_pair(t):
                scores(t, 0)
                keys(t, 1, 0)
                keys(t, 1, 1)
                transpose_probs(t, 0, 0)
                values(t, 1, 0, (0,))
                transpose_probs(t, 0, 1)
                values(t, 1, 0, (1,))
                attend(t, 0)
                values(t, 1, 1)

            pe.wait_ge(last_k_done, 1)
            pe.wait_ge(last_v_done, 1)
            with pe.Fori(0, TILES - 1) as t:
                even_pair(t)
                scores(t, 1)
                keys(t + 1, 0, 0, (0,))
                transpose_x(t + 1)
                keys(t + 1, 0, 0, (1,))
                keys(t + 1, 0, 1, (0,))
                queries(t + 1)
                keys(t + 1, 0, 1, (1,))
                transpose_q(t + 1)
                values(t + 1, 0, 0, (0,))
                pe.wait_ge(qt_copied, t + 2)
                transpose_probs(t, 1, 0)
                values(t + 1, 0, 0, (1,))
                transpose_probs(t, 1, 1)
                attend(t, 1)
                values(t + 1, 0, 1)
            even_pair(TILES - 1)
            scores(TILES - 1, 1)
            for b in range(2):
                transpose_probs(TILES - 1, 1, b)
            attend(TILES - 1, 1)


def rest_of_layer(nc, banks, ident, shared, x, heads_dram, units, out):
    x_halves = x.rearrange("(h t p) d -> h p t d", h=HALVES, p=P)
    out_halves = out.rearrange("(h t p) d -> h p t d", h=HALVES, p=P)
    with ExitStack() as stack:
        def sb(name, shape, dt=F32):
            return stack.enter_context(nc.sbuf_tensor(name, shape, dt))

        def sem(name):
            return stack.enter_context(nc.semaphore(name))

        def split_pair(name, shape):
            return sb(name + "_hi", shape, F32R), sb(name + "_lo", shape, F32R)

        proj = [banks["proj0"], banks["proj1"]]
        tr = [banks["tr0"], banks["tr1"]]
        score_bank = [banks["s0"], banks["s1"]]
        out_bank = [banks["o0"], banks["o1"]]
        down_bank = score_bank + out_bank
        gate_bank, gate_t_bank = score_bank

        unit_raw = [shared.raw[:, 2 * i:2 * i + 2, :] for i in range(2)]
        unit_s = [split_pair(f"unit{i}", [P, KC, D]) for i in range(RING)]
        res = sb("res", [P, HT, D])
        y = sb("y", [P, HT, D])
        heads_s = split_pair("heads_s", [P, KC, HALF])
        xt_s = sb("xt_s_hi", [P, KC, HALF], F32R), shared.heads_raw
        x_hat = [sb(f"c_x_hat{i}", [P, D]) for i in range(2)]
        q_t = [sb(f"q_t{i}", [P, HALF]) for i in range(2)]
        k_diag = [sb(f"k_diag{i}", [P, 16, P]) for i in range(2)]
        v_tok = sb("v_tok", [P, HT, D])
        masked = sb("masked", [P, 16, SEQ])
        pr = sb("pr", [P, 16, SEQ])
        pt_diag = [sb(f"pt_diag{i}", [P, 16, P]) for i in range(2)]
        pr_t = sb("pr_t", [P, 16, SEQ])
        act_buf = [sb(f"act_buf{i}", [P, HALF]) for i in range(2)]
        h_s = split_pair("h_s", [P, 8, HALF])
        gate_s, causal = shared.gate_s, shared.causal
        logits = sb("logits", [NE, HALF])
        n1_all, n2_all, bo_all = shared.rows
        minus_half = sb("c_minus_half", [P, 1])
        stats = sb("c_stats", [P, HT, 6])
        mean_var = sb("c_mean_var", [P, HT, 2])
        square_sum = sb("square_sum", [P, HT])
        root_in = sb("root_in", [P, 2, HT])
        rstd = sb("c_rstd", [P, 2, HT])
        row_max = sb("c_row_max", [P, 16])
        den = sb("c_den", [P, 16])
        r_den = sb("c_r_den", [P, 16])
        top = sb("top", [P, HT, NE])
        g_small = sb("g_small", [P, 5, HT])
        weight = sb("weight", [P, HT])

        passed_pool, passed_dve, passed_pe = sem("c_passed_pool"), sem("c_passed_dve"), sem("c_passed_pe")
        passed_sp = sem("c_passed_sp")
        diag_ready = sem("diag_ready")
        unit_in, heads_in = shared.unit_in, shared.heads_in
        unit_hi, unit_ready, down_half = sem("unit_hi"), sem("unit_ready"), sem("down_half")
        x_in = [sem(f"c_x_in{i}") for i in range(HT)]
        pool_step, dve_step = sem("c_pool_step"), sem("c_dve_step")
        p_full = [sem(f"p_full{i}") for i in range(2)]
        p_free = [sem(f"p_free{i}") for i in range(2)]
        t_full = [sem(f"t_full{i}") for i in range(2)]
        t_hi, x_hat_ready = sem("t_hi"), sem("c_x_hat_ready")
        t_free = [sem(f"t_free{i}") for i in range(2)]
        heads_hi, heads_whole = sem("heads_hi"), sem("heads_whole")
        heads_lo, heads_lo_pool = sem("heads_lo"), sem("heads_lo_pool")
        sc_full = [sem(f"sc_full{i}") for i in range(2)]
        at_full = [sem(f"at_full{i}") for i in range(2)]
        shifted, exp_ready, transposed = sem("shifted"), sem("exp_ready"), sem("transposed")
        pt_low, pt_high = sem("pt_low"), sem("pt_high")
        var_ready, rstd_ready = sem("c_var_ready"), sem("c_rstd_ready")
        y_ready, square_ready, rms_ready = sem("y_ready"), sem("square_ready"), sem("rms_ready")
        gate_full, logits_ready, gate_t_full = sem("gate_full"), sem("logits_ready"), sem("gate_t_full")
        top_ready, top_exp, weight_ready = sem("top_ready"), sem("top_exp"), sem("weight_ready")
        tanh_ready, silu_ready, h_hi, h_lo = sem("tanh_ready"), sem("silu_ready"), sem("h_hi"), sem("h_lo")
        down_full, down_read, final, stored = sem("down_full"), sem("down_read"), sem("final"), sem("stored")

        def proj_full(n, h):
            return p_full[n % 2], USES * h + n // 2 + 1 + CREDIT

        def proj_free(n, h):
            return p_free[n % 2], FREES * h + n // 2 + CREDIT

        def unit_used(u, h):
            if u < 0:
                return ((down_half, 2 * h + CREDIT), (down_full, 8 * h + CREDIT), (p_full[1], USES * h + CREDIT))[u + RING]
            last_use = {0: 3, 1: 7, 2: 14, 3: 15, 4: 19, 5: 23, 6: 30, 7: 31, 8: 35, 9: 39, 10: 43, 13: 47, 14: 51}
            if u in last_use:
                return proj_full(last_use[u], h)
            if u in (11, 15):
                return down_half, 2 * h + (1 if u == 11 else 2) + CREDIT
            return down_full, 8 * h + (4 if u == 12 else 8) + CREDIT

        halves = (slice(0, HALF // 2), slice(HALF // 2, HALF))
        heads_raw = shared.heads_raw[:].bitcast(F32).rearrange("p t d -> p (t d)")

        def low_part(h, layer, m, part=1):
            if m == 2:
                return heads_lo_pool, 2 * h + layer + 1
            return heads_lo, 12 * h + HT + 4 * layer + (m + 1 if m < 2 else 3 + part)

        def at_bank(m, part):
            return 0 if part == 1 else m % 2

        block = stack.enter_context(nc.Block())

        @block.sync
        def _(sp):
            def load_unit(h, u):
                for v in range(2):
                    wait(sp, unit_ready, 2 * (NU * h + u) + v - 1)
                    sp.dma_start(unit_raw[v], units[u, :, 2 * v:2 * v + 2, :]).then_inc(unit_in[v], 16)

            def later_units(h):
                for u in range(2, NU):
                    load_unit(h, u)

            def store(h, t):
                sp.wait_ge(final, 4 * h + t + 1)
                stand_alone(sp, passed_sp)
                sp.dma_start(out_halves[bass.ds(h, 1), :, t, :].rearrange("o p d -> (o p) d"), y[:, t, :]
                             ).then_inc(stored, 16)

            def load_x(h, t):
                sp.dma_start(res[:, t, :], x_halves[bass.ds(h, 1), :, t, :].rearrange("o p d -> (o p) d")
                             ).then_inc(x_in[t], 16)

            for t in range(HT):
                load_x(0, t)
            load_unit(0, 1)
            with sp.Fori(0, HALVES - 1) as h:
                later_units(h)
                load_unit(h + 1, 0)
                sp.wait_ge(p_full[1], USES * (h + 1) + CREDIT)
                for par in range(2):
                    sp.wait_ge(shared.heads_out[par], 16 * TILES + CREDIT)
                load_heads(sp, shared, heads_dram, h + 1)
                load_unit(h + 1, 1)
                for t in range(HT):
                    store(h, t)
                    load_x(h + 1, t)
            later_units(HALVES - 1)
            for t in range(HT):
                store(HALVES - 1, t)
            sp.wait_ge(stored, 16 * HT * HALVES + CREDIT)

        @block.gpsimd
        def _(pool):
            chain = Chain(pool, pool_step)

            def low_unit(h, u, vs=(0, 1)):
                hi, lo = unit_s[u % RING]
                for v in vs:
                    pool.wait_ge(unit_hi, 2 * (NU * h + u) + v + 1)
                    stand_alone(pool, passed_pool)
                    at = slice(2 * v, 2 * v + 2)
                    pool.tensor_tensor(lo[:, at, :], unit_raw[v], hi[:, at, :].bitcast(F32), ALU.subtract
                                       ).then_inc(unit_ready, 1)

            def low_heads(h, layer):
                pool.wait_ge(heads_whole, 2 * h + layer + 1)
                stand_alone(pool, passed_pool)
                pool.tensor_tensor(heads_s[1][:, 2, :], act_buf[1][:], heads_s[0][:, 2, :].bitcast(F32),
                                   ALU.subtract).then_inc(heads_lo_pool, 1)

            def root_var(h, stage, t):
                pool.wait_ge(var_ready, 8 * h + 4 * stage + t + 1)
                stand_alone(pool, passed_pool)
                chain.step(pool.tensor_scalar(root_in[:, 0, t:t + 1], mean_var[:, t, 1:2], LN_EPS, None, ALU.add))
                chain.wait()
                pool.tensor_tensor(rstd[:, 0, t:t + 1], root_in[:, 0, t:t + 1], minus_half[:], ALU.pow
                                   ).then_inc(rstd_ready, 1)

            def root_square(h, stage, t):
                pool.wait_ge(square_ready, 8 * h + 4 * (stage - 1) + t + 1 + CREDIT)
                stand_alone(pool, passed_pool)
                chain.step(pool.tensor_scalar(root_in[:, 1, t:t + 1], square_sum[:, t:t + 1], 1.0 / D, RMS_EPS,
                                              ALU.mult, ALU.add))
                chain.wait()
                pool.tensor_tensor(rstd[:, 1, t:t + 1], root_in[:, 1, t:t + 1], minus_half[:], ALU.pow
                                   ).then_inc(rms_ready, 1)

            chain.step(pool.memset(minus_half[:], -0.5))
            for i in range(2):
                pool.memset(k_diag[i][:], 0.0).then_inc(diag_ready, 1)
            with pool.Fori(0, HALVES) as h:
                chain.enter(h, 16)
                low_unit(h, 0)
                low_unit(h, 1, (0,))
                root_var(h, 0, 0)
                low_unit(h, 1, (1,))
                root_var(h, 0, 1)
                root_var(h, 0, 2)
                low_unit(h, 2, (0,))
                root_var(h, 0, 3)
                low_unit(h, 2, (1,))
                for u in range(3, 6):
                    low_unit(h, u)
                low_heads(h, 0)
                low_unit(h, 6, (0,))
                root_var(h, 1, 0)
                root_var(h, 1, 1)
                root_square(h, 1, 0)
                root_var(h, 1, 2)
                root_square(h, 1, 1)
                root_square(h, 1, 2)
                low_unit(h, 6, (1,))
                root_var(h, 1, 3)
                root_square(h, 1, 3)
                for u in range(7, 10):
                    low_unit(h, u)
                low_heads(h, 1)
                low_unit(h, 10, (0,))
                for t in range(HT):
                    root_square(h, 2, t)
                    if t == 2:
                        low_unit(h, 10, (1,))
                for u in range(11, NU):
                    low_unit(h, u)
            chain.leave(HALVES)

        @block.scalar
        def _(act):
            def high_unit(h, u, vs=(0, 1)):
                if vs[0] == 0:
                    act.wait_ge(*unit_used(u - RING, h))
                for v in vs:
                    act.wait_ge(unit_in[v], 16 * (NU * h + u + 1))
                    act.activation(unit_s[u % RING][0][:, 2 * v:2 * v + 2, :], unit_raw[v], ACT.Copy
                                   ).then_inc(unit_hi, 1)

            def high_xt(h, stage, t):
                n = 4 * stage + t
                act.wait_ge(t_full[n % 2], 6 * h + n // 2 + 1)
                act.activation(xt_s[0][:, :, t * P:(t + 1) * P],
                               tr[n % 2][:].rearrange("p (c n) -> p c n", c=KC), ACT.Copy).then_inc(t_hi, 1)

            def copy_v(h, layer, t):
                n = USE_V[layer] + t
                act.wait_ge(*proj_full(n, h))
                act.activation(v_tok[:, t, :], proj[n % 2][:], ACT.Copy).then_inc(p_free[n % 2], 1)

            def copy_k(h, layer, m):
                act.wait_ge(*proj_full(USE_KQ[layer] + 2 * m, h))
                for a in range(4):
                    rows = slice(32 * a, 32 * a + 32)
                    last = act.activation(k_diag[m % 2][rows, :, rows],
                                          proj[0][rows, :].rearrange("p (n j) -> p n j", j=SEQ), ACT.Copy)
                last.then_inc(p_free[0], 1)

            def copy_q(h, layer, m):
                act.wait_ge(*proj_full(USE_KQ[layer] + 2 * m + 1, h))
                act.activation(q_t[m % 2][:], proj[1][:], ACT.Copy).then_inc(p_free[1], 1)

            def copy_pt(h, layer, m):
                act.wait_ge(transposed, 8 * h + 4 * layer + m + 1)
                for b in (0, 1):
                    rows = slice(32 * b, 32 * b + 32)
                    last = act.activation(pt_diag[m % 2][rows, :, rows], pr_t[rows], ACT.Copy)
                last.then_inc(pt_low, 1)

            def exp(h, layer, m):
                act.wait_ge(shifted, 8 * h + 4 * layer + m + 1)
                act.activation(pr[:], pr[:], ACT.Exp, scale=SCALE).then_inc(exp_ready, 1)

            def high_heads(h, layer, m, part=None):
                at = slice(0, HALF) if part is None else halves[part]
                bank = at_bank(m, part)
                act.wait_ge(at_full[bank], AT_USES[bank] * (2 * h + layer) + (3 if part == 1 else m // 2 + 1))
                act.activation(heads_s[0][:, m, at], out_bank[bank][:, at], ACT.Copy).then_inc(heads_hi, 1)

            def square(h, stage, t):
                if stage == 1:
                    act.wait_ge(y_ready, 4 * h + t + 1)
                else:
                    act.wait_ge(p_free[t % 2], FREES * h + (USE_WO[2] + t) // 2 + 1 + CREDIT)
                act.wait_ge(square_ready, 8 * h + 4 * (stage - 1) + t + CREDIT)
                act.activation(act_buf[0][:], y[:, t, :], ACT.Square, accum_out=square_sum[:, t:t + 1]
                               ).then_inc(square_ready, 1)

            def attention(h, layer):
                ahead = (5, 9)[layer]
                for m in range(KC):
                    copy_k(h, layer, m)
                    if m == 3:
                        high_unit(h, ahead, (0,))
                    if m >= 1:
                        exp(h, layer, m - 1)
                    copy_q(h, layer, m)
                    if m == 0:
                        high_unit(h, (4, 8)[layer])
                    if m == 3:
                        high_unit(h, ahead, (1,))
                    if m >= 2:
                        high_heads(h, layer, m - 2)
                    if m >= 1:
                        copy_pt(h, layer, m - 1)
                exp(h, layer, 3)
                high_heads(h, layer, 2)
                act.activation(act_buf[1][:], out_bank[0][:], ACT.Copy).then_inc(heads_whole, 1)
                copy_pt(h, layer, 3)
                high_unit(h, ahead + 1, (0,))
                high_heads(h, layer, 3, 0)
                high_heads(h, layer, 3, 1)
                high_unit(h, ahead + 1, (1,))

            with act.Fori(0, HALVES) as h:
                high_unit(h, 0)
                act.wait_ge(heads_in, 16 * h + 16)
                act.activation(heads_s[0][:].rearrange("p g (n i) -> p g n i", i=SEQ),
                               heads_raw.rearrange("p (n g i) -> p g n i", g=4, i=SEQ),
                               ACT.Copy).then_inc(heads_hi, 1)
                high_unit(h, 1)
                high_xt(h, 0, 0)
                high_xt(h, 0, 1)
                high_unit(h, 2)
                copy_v(h, 0, 0)
                high_xt(h, 0, 2)
                copy_v(h, 0, 1)
                high_xt(h, 0, 3)
                high_unit(h, 3, (0,))
                copy_v(h, 0, 2)
                high_unit(h, 3, (1,))
                copy_v(h, 0, 3)
                act.wait_ge(diag_ready, 4)
                attention(h, 0)
                square(h, 1, 0)
                square(h, 1, 1)
                square(h, 1, 2)
                high_xt(h, 1, 0)
                high_xt(h, 1, 1)
                copy_v(h, 1, 0)
                square(h, 1, 3)
                high_xt(h, 1, 2)
                high_unit(h, 7)
                copy_v(h, 1, 1)
                high_xt(h, 1, 3)
                copy_v(h, 1, 2)
                copy_v(h, 1, 3)
                attention(h, 1)
                square(h, 2, 0)
                square(h, 2, 1)
                high_xt(h, 2, 0)
                square(h, 2, 2)
                high_xt(h, 2, 1)
                square(h, 2, 3)
                high_xt(h, 2, 2)
                high_xt(h, 2, 3)
                for f in range(2):
                    for j in range(9):
                        if j < 8:
                            n = USE_UP[f] + j
                            act.wait_ge(*proj_full(n, h))
                            if j >= 2:
                                act.wait_ge(h_lo, 16 * h + 8 * f + j - 1)
                            act.activation(act_buf[j % 2][:], proj[n % 2][:], ACT.Tanh, scale=0.5
                                           ).then_inc(tanh_ready, 1)
                        if f == 0 and j == 0:
                            act.wait_ge(gate_full, h + 1)
                            act.activation(logits[:], gate_bank[0:NE, :], ACT.Copy).then_inc(logits_ready, 1)
                        if j:
                            act.wait_ge(silu_ready, 16 * h + 8 * f + j + CREDIT)
                            act.activation(h_s[0][:, j - 1, :], act_buf[(j - 1) % 2][:], ACT.Copy, scale=0.5
                                           ).then_inc(h_hi, 1)
                        if f == 0 and j == 2:
                            act.wait_ge(top_ready, h + 1)
                            act.activation(top[:], top[:], ACT.Exp).then_inc(top_exp, 1)
                        if f == 0 and j == 1:
                            high_unit(h, 11)
                        if j == 4:
                            high_unit(h, (12, 16)[f])
                    if f == 0:
                        for u in (13, 14, 15):
                            high_unit(h, u)

        @block.vector
        def _(dve):
            chain = Chain(dve, dve_step)

            def low_xt(h, stage, t):
                n = 4 * stage + t
                at = slice(t * P, (t + 1) * P)
                dve.wait_ge(t_hi, 12 * h + n + 1)
                dve.tensor_tensor(xt_s[1][:, :, at], tr[n % 2][:].rearrange("p (c n) -> p c n", c=KC),
                                  xt_s[0][:, :, at].bitcast(F32), ALU.subtract).then_inc(t_free[n % 2], 1)

            def low_raw_heads(h, t):
                dve.wait_ge(heads_hi, 11 * h + 1)
                at = slice(t * P, (t + 1) * P)
                dve.tensor_tensor(heads_s[1][:, :, at].rearrange("p g (n i) -> p g n i", i=SEQ),
                                  heads_raw.rearrange("p (n g i) -> p g n i", g=4, i=SEQ)[:, :, 4 * t:4 * t + 4],
                                  heads_s[0][:, :, at].rearrange("p g (n i) -> p g n i", i=SEQ).bitcast(F32),
                                  ALU.subtract).then_inc(heads_lo, 1)

            def low_heads(h, layer, m, part=None):
                count, at = (m + 1, slice(0, HALF)) if part is None else (4 + part, halves[part])
                dve.wait_ge(heads_hi, 11 * h + 1 + 5 * layer + count)
                dve.tensor_tensor(heads_s[1][:, m, at], out_bank[at_bank(m, part)][:, at], heads_s[0][:, m, at].bitcast(F32),
                                  ALU.subtract).then_inc(heads_lo, 1)

            def add_res(h, stage, t):
                n = USE_WO[stage] + t
                row = y[:, t, :] if stage == 2 else res[:, t, :]
                dve.wait_ge(*proj_full(n, h))
                if stage == 0:
                    dve.wait_ge(x_in[t], 16 * h + 16)
                dve.tensor_tensor(row, proj[n % 2][:], row, ALU.add).then_inc(p_free[n % 2], 1)
                if stage < 2:
                    dve.wait_ge(p_free[n % 2], FREES * h + n // 2 + 1 + CREDIT)
                    chain.step(dve.bn_stats(stats[:, t, :], row))
                    chain.wait()
                    stand_alone(dve, passed_dve)
                    dve.bn_aggr(mean_var[:, t, :], stats[:, t, :]).then_inc(var_ready, 1)

            def x_hat_free(h, stage, t):
                if t >= 2:
                    dve.wait_ge(t_full[t % 2], 6 * h + (4 * stage + t) // 2)

            def layer_norm(h, stage, t):
                dve.wait_ge(rstd_ready, 8 * h + 4 * stage + t + 1)
                if stage == 0:
                    x_hat_free(h, 0, t)
                    dve.tensor_scalar(x_hat[t % 2][:], res[:, t, :], mean_var[:, t, 0:1], rstd[:, 0, t:t + 1],
                                      ALU.subtract, ALU.mult).then_inc(x_hat_ready, 1)
                else:
                    dve.tensor_scalar(y[:, t, :], res[:, t, :], mean_var[:, t, 0:1], rstd[:, 0, t:t + 1],
                                      ALU.subtract, ALU.mult).then_inc(y_ready, 1)

            def rms_norm(h, stage, t):
                dve.wait_ge(rms_ready, 8 * h + 4 * (stage - 1) + t + 1)
                x_hat_free(h, stage, t)
                dve.scalar_tensor_tensor(x_hat[t % 2][:], y[:, t, :], rstd[:, 1, t:t + 1],
                                         (n1_all if stage == 1 else n2_all)[:], ALU.mult, ALU.mult
                                         ).then_inc(x_hat_ready, 1)

            def softmax(h, layer, m):
                n = 4 * layer + m
                bank = score_bank[n % 2][:].rearrange("p (n j) -> p n j", j=SEQ)
                dve.wait_ge(sc_full[n % 2], 4 * h + n // 2 + 1)
                if layer == 1:
                    chain.step(dve.tensor_tensor(masked[:], bank, causal[:].unsqueeze(1).to_broadcast([P, 16, SEQ]),
                                                 ALU.add))
                    chain.wait()
                    bank = masked[:]
                chain.step(dve.tensor_reduce(row_max[:], bank, AX.X, ALU.max))
                chain.wait()
                dve.tensor_tensor(pr[:], bank, row_max[:].unsqueeze(2).to_broadcast([P, 16, SEQ]), ALU.subtract
                                  ).then_inc(shifted, 1)

            def softmax_end(h, layer, m):
                n = 4 * layer + m
                dve.wait_ge(exp_ready, 8 * h + n + 1)
                chain.step(dve.tensor_reduce(den[:], pr[:], AX.X, ALU.add))
                chain.wait()
                if layer == 0:
                    chain.step(dve.tensor_scalar(den[:], den[:], DEN_EPS, None, ALU.add))
                    chain.wait()
                chain.step(dve.reciprocal(r_den[:], den[:]))
                chain.wait()
                chain.step(dve.tensor_tensor(pr[:], pr[:], r_den[:].unsqueeze(2).to_broadcast([P, 16, SEQ]), ALU.mult))
                chain.wait()
                dve.wait_ge(pt_low, 8 * h + n + CREDIT)
                dve.transpose(pr_t[:], pr[:]).then_inc(transposed, 1)
                dve.wait_ge(transposed, 8 * h + n + 1)
                for b in (2, 3):
                    rows = slice(32 * b, 32 * b + 32)
                    last = dve.tensor_copy(pt_diag[m % 2][rows, :, rows], pr_t[rows])
                last.then_inc(pt_high, 1)

            def attention(h, layer):
                if layer == 0:
                    for t in range(HT):
                        chain.step(dve.tensor_tensor(res[:, t, :], res[:, t, :], bo_all[:], ALU.add))
                for m in range(KC):
                    softmax(h, layer, m)
                    if m == 3:
                        low_heads(h, layer, 1)
                    softmax_end(h, layer, m)
                    if m == 1:
                        low_heads(h, layer, 0)
                low_heads(h, layer, 3, 0)
                low_heads(h, layer, 3, 1)

            def gate_top(h):
                dve.wait_ge(gate_t_full, h + 1)
                stand_alone(dve, passed_dve)
                for t in range(HT):
                    chain.step(dve.max(top[:, t, :], gate_t_bank[:, t * NE:(t + 1) * NE]))
                chain.wait()
                chain.step(dve.tensor_copy(g_small[:, 0, :], top[:, :, 0]))
                chain.wait()
                dve.tensor_tensor(top[:], top[:], g_small[:, 0, :].unsqueeze(2).to_broadcast([P, HT, NE]),
                                  ALU.subtract).then_inc(top_ready, 1)

            def gate_weight(h):
                dve.wait_ge(top_exp, h + 1)
                chain.step(dve.tensor_reduce(g_small[:, 1, :], top[:], AX.X, ALU.add))
                chain.step(dve.tensor_tensor(g_small[:, 2, :], top[:, :, 0], top[:, :, 1], ALU.add))
                chain.wait()
                chain.step(dve.reciprocal(g_small[:, 3, :], g_small[:, 1, :]))
                chain.wait()
                chain.step(dve.tensor_tensor(g_small[:, 2, :], g_small[:, 2, :], g_small[:, 3, :], ALU.mult))
                chain.wait()
                chain.step(dve.tensor_scalar(g_small[:, 4, :], g_small[:, 2, :], TOPK_EPS, None, ALU.add))
                chain.wait()
                chain.step(dve.reciprocal(g_small[:, 3, :], g_small[:, 4, :]))
                chain.wait()
                dve.tensor_tensor(weight[:], g_small[:, 2, :], g_small[:, 3, :], ALU.mult).then_inc(weight_ready, 1)

            def silu(h, f, j):
                k = 8 * f + j
                dve.wait_ge(tanh_ready, 16 * h + k + 1)
                n = USE_UP[f] + j
                dve.scalar_tensor_tensor(act_buf[j % 2][:], act_buf[j % 2][:], 1.0, proj[n % 2][:], ALU.add, ALU.mult
                                         ).then_inc(silu_ready, 1)

            def low_h(h, f, j):
                k = 8 * f + j
                dve.wait_ge(h_hi, 16 * h + k + 1)
                dve.scalar_tensor_tensor(h_s[1][:, j, :], act_buf[j % 2][:], 0.5, h_s[0][:, j, :].bitcast(F32),
                                         ALU.mult, ALU.subtract).then_inc(h_lo, 1)

            def add_down(h, f, t):
                dve.wait_ge(down_full, 8 * h + 4 * f + t + 1 + CREDIT)
                dve.scalar_tensor_tensor(y[:, t, :], down_bank[t][:], weight[:, t:t + 1], y[:, t, :],
                                         ALU.mult, ALU.add).then_inc(down_read, 1)

            for i in range(2):
                dve.memset(pt_diag[i][:], 0.0).then_inc(diag_ready, 1)
            with dve.Fori(0, HALVES) as h:
                chain.enter(h, 63)
                low_raw_heads(h, 0)
                low_raw_heads(h, 1)
                add_res(h, 0, 0)
                low_raw_heads(h, 2)
                add_res(h, 0, 1)
                low_raw_heads(h, 3)
                layer_norm(h, 0, 0)
                add_res(h, 0, 2)
                layer_norm(h, 0, 1)
                low_xt(h, 0, 0)
                add_res(h, 0, 3)
                layer_norm(h, 0, 2)
                low_xt(h, 0, 1)
                layer_norm(h, 0, 3)
                low_xt(h, 0, 2)
                low_xt(h, 0, 3)
                attention(h, 0)
                chain.wait()
                add_res(h, 1, 0)
                add_res(h, 1, 1)
                dve.wait_ge(stored, 16 * HT * h + CREDIT)
                layer_norm(h, 1, 0)
                add_res(h, 1, 2)
                layer_norm(h, 1, 1)
                rms_norm(h, 1, 0)
                layer_norm(h, 1, 2)
                rms_norm(h, 1, 1)
                low_xt(h, 1, 0)
                add_res(h, 1, 3)
                rms_norm(h, 1, 2)
                low_xt(h, 1, 1)
                layer_norm(h, 1, 3)
                low_xt(h, 1, 2)
                rms_norm(h, 1, 3)
                low_xt(h, 1, 3)
                attention(h, 1)
                add_res(h, 2, 0)
                add_res(h, 2, 1)
                rms_norm(h, 2, 0)
                add_res(h, 2, 2)
                rms_norm(h, 2, 1)
                low_xt(h, 2, 0)
                rms_norm(h, 2, 2)
                add_res(h, 2, 3)
                low_xt(h, 2, 1)
                rms_norm(h, 2, 3)
                low_xt(h, 2, 2)
                low_xt(h, 2, 3)
                for f in range(2):
                    for j in range(9):
                        if j < 8:
                            silu(h, f, j)
                        if f == 0 and j == 0:
                            gate_top(h)
                        if j:
                            low_h(h, f, j - 1)
                        if f == 0 and j == 2:
                            gate_weight(h)
                            dve.wait_ge(weight_ready, h + 1)
                    for t in range(HT):
                        add_down(h, f, t)
                        if f == 1:
                            dve.wait_ge(down_read, 8 * h + 4 * f + t + 1 + CREDIT)
                            dve.tensor_tensor(y[:, t, :], y[:, t, :], res[:, t, :], ALU.add).then_inc(final, 1)
            chain.leave(HALVES)

        @block.tensor
        def _(pe):
            def project(h, stage, t, cs=range(KC)):
                n = USE_WO[stage] + t
                u = (0, 4, 8)[stage]
                if stage == 0:
                    if t == 0:
                        pe.wait_ge(silu_ready, 16 * h + CREDIT)
                    pe.wait_ge(heads_lo, 12 * h + t + 1)
                if cs[0] == 0:
                    pe.wait_ge(*proj_free(n, h))
                for c in cs:
                    if t == 0 and c % 2 == 0:
                        pe.wait_ge(unit_ready, 2 * (NU * h + u) + c // 2 + 1)
                    if stage and (t == 0 or t == 2 and c == 3):
                        pe.wait_ge(*low_part(h, stage - 1, c, t // 2))
                    last = product(pe, proj[n % 2][:], [s[:, c, t * P:(t + 1) * P] for s in heads_s],
                                   [s[:, c, :] for s in unit_s[u % RING]], c == 0, c == KC - 1)
                if c == KC - 1:
                    last.then_inc(p_full[n % 2], 1)

            def transpose_x(h, stage, t):
                n = 4 * stage + t
                pe.wait_ge(x_hat_ready, 12 * h + n + 1)
                pe.wait_ge(t_free[n % 2], 6 * h + n // 2 + CREDIT)
                for c in range(KC):
                    last = pe.transpose(tr[n % 2][:, c * P:(c + 1) * P], x_hat[n % 2][:, c * P:(c + 1) * P], ident[:])
                last.then_inc(t_full[n % 2], 1)

            def values(h, layer, t):
                n = USE_V[layer] + t
                u = (1, 5)[layer]
                if t == 0:
                    pe.wait_ge(unit_ready, 2 * NU * h + 2 * u + 2)
                pe.wait_ge(t_free[t % 2], 6 * h + (4 * layer + t) // 2 + 1 + CREDIT)
                pe.wait_ge(*proj_free(n, h))
                for c in range(KC):
                    last = product(pe, proj[n % 2][:], [s[:, c, t * P:(t + 1) * P] for s in xt_s],
                                   [s[:, c, :] for s in unit_s[u % RING]], c == 0, c == KC - 1)
                last.then_inc(p_full[n % 2], 1)

            def features(h, u, n, m, half=None):
                if m == 0:
                    pe.wait_ge(unit_ready, 2 * NU * h + 2 * u + 2)
                k = n - USE_UP[0]
                if k < 2:
                    pe.wait_ge(*proj_free(n, h))
                else:
                    pe.wait_ge(silu_ready, 16 * h + k - 1 + CREDIT)
                at = slice(0, HALF) if half is None else slice(half * HALF // 2, (half + 1) * HALF // 2)
                for c in range(KC):
                    last = product(pe, proj[n % 2][:, at], [s[:, c, m * P:(m + 1) * P] for s in unit_s[u % RING]],
                                   [s[:, c, at] for s in xt_s], c == 0, c == KC - 1)
                if half != 0:
                    last.then_inc(p_full[n % 2], 1)

            def keys(h, layer, m):
                features(h, (2, 6)[layer], USE_KQ[layer] + 2 * m, m)

            def queries(h, layer, m):
                features(h, (3, 7)[layer], USE_KQ[layer] + 2 * m + 1, m)

            def scores(h, layer, m):
                n = 4 * layer + m
                k = (USE_KQ[layer] + 2 * m) // 2
                pe.wait_ge(p_free[0], FREES * h + k + 1 + CREDIT)
                pe.wait_ge(p_free[1], FREES * h + k + 1 + CREDIT)
                if n < 2:
                    pe.wait_ge(down_read, 8 * h + CREDIT)
                else:
                    pe.wait_ge(shifted, 8 * h + n - 1)
                for t in range(HT):
                    for b in range(4):
                        rows = slice(32 * b, 32 * b + 32)
                        last = pe.matmul(score_bank[n % 2][rows, t * P:(t + 1) * P],
                                         q_t[m % 2][:, t * P + 32 * b:t * P + 32 * b + 32],
                                         k_diag[m % 2][:, 4 * t + b, :], start=True, stop=True)
                last.then_inc(sc_full[n % 2], 1)

            def attend(h, layer, m):
                pe.wait_ge(pt_low, 8 * h + 4 * layer + m + 1 + CREDIT)
                pe.wait_ge(pt_high, 8 * h + 4 * layer + m + 1)
                if m >= 2:
                    pe.wait_ge(*low_part(h, layer, m - 2))
                elif layer == 1:
                    pe.wait_ge(*low_part(h, 0, 3))
                else:
                    pe.wait_ge(down_read, 8 * h + CREDIT)
                for t in range(HT):
                    bank = at_bank(m, t // 2 if m == 3 else None)
                    if m == 3 and t == 2:
                        pe.wait_ge(heads_whole, 2 * h + layer + 1)
                    for a in range(4):
                        rows = slice(32 * a, 32 * a + 32)
                        last = pe.matmul(out_bank[bank][rows, t * P:(t + 1) * P],
                                         v_tok[:, t, m * P + 32 * a:m * P + 32 * a + 32],
                                         pt_diag[m % 2][:, 4 * t + a, :], start=True, stop=True)
                    if t == HT - 1 or m == 3 and t == 1:
                        last.then_inc(at_full[bank], 1)

            def attention(h, layer):
                for m in range(KC):
                    keys(h, layer, m)
                    if m >= 1:
                        scores(h, layer, m - 1)
                    queries(h, layer, m)
                    if m >= 2:
                        attend(h, layer, m - 2)
                scores(h, layer, 3)
                project(h, layer + 1, 0, (0,))
                project(h, layer + 1, 1, (0,))
                attend(h, layer, 2)
                for c in (1, 2):
                    project(h, layer + 1, 0, (c,))
                    project(h, layer + 1, 1, (c,))
                attend(h, layer, 3)
                project(h, layer + 1, 0, (3,))
                project(h, layer + 1, 1, (3,))

            def gate_logits(h):
                pe.wait_ge(shifted, 8 * h + 8)
                for c in range(KC):
                    last = product(pe, gate_bank[:], [s[:, c, :] for s in gate_s], [s[:, c, :] for s in xt_s],
                                   c == 0, c == KC - 1)
                last.then_inc(gate_full, 1)

            def gate_transpose(h):
                pe.wait_ge(logits_ready, h + 1)
                stand_alone(pe, passed_pe)
                for t in range(HT):
                    last = pe.transpose(gate_t_bank[:, t * NE:(t + 1) * NE], logits[:, t * P:(t + 1) * P],
                                        ident[0:NE, 0:NE])
                last.then_inc(gate_t_full, 1)

            def down(h, f):
                for d in range(2):
                    u = (11, 15)[f] + d
                    pe.wait_ge(unit_ready, 2 * NU * h + 2 * u + 2)
                    pe.wait_ge(h_lo, 16 * h + 8 * f + 4 * d + 4)
                    for t in range(HT):
                        if d == 0 and f == 0:
                            if t < 2:
                                pe.wait_ge(top_ready, h + 1)
                            else:
                                pe.wait_ge(*low_part(h, 1, 3))
                        elif d == 0:
                            pe.wait_ge(down_read, 8 * h + t + 1 + CREDIT)
                        for c in range(KC):
                            last = product(pe, down_bank[t][:], [s[:, 4 * d + c, t * P:(t + 1) * P] for s in h_s],
                                           [s[:, c, :] for s in unit_s[u % RING]],
                                           d == 0 and c == 0, d == 1 and c == KC - 1)
                        if d == 1:
                            last.then_inc(down_full, 1)
                        elif t == HT - 1:
                            last.then_inc(down_half, 1)

            for free in [down_half, down_full, *p_full, *p_free, *t_free, silu_ready, pt_low, down_read,
                         square_ready, stored]:
                pe.sem_inc(free, CREDIT)
            with pe.Fori(0, HALVES) as h:
                project(h, 0, 0)
                project(h, 0, 1)
                project(h, 0, 2)
                transpose_x(h, 0, 0)
                project(h, 0, 3)
                transpose_x(h, 0, 1)
                values(h, 0, 0)
                transpose_x(h, 0, 2)
                values(h, 0, 1)
                transpose_x(h, 0, 3)
                values(h, 0, 2)
                values(h, 0, 3)
                attention(h, 0)
                project(h, 1, 2)
                project(h, 1, 3)
                transpose_x(h, 1, 0)
                transpose_x(h, 1, 1)
                values(h, 1, 0)
                transpose_x(h, 1, 2)
                values(h, 1, 1)
                transpose_x(h, 1, 3)
                values(h, 1, 2)
                values(h, 1, 3)
                attention(h, 1)
                project(h, 2, 2)
                transpose_x(h, 2, 0)
                project(h, 2, 3)
                transpose_x(h, 2, 1)
                transpose_x(h, 2, 2)
                pe.wait_ge(t_free[1], 6 * h + 5 + CREDIT)
                features(h, 9, USE_UP[0], 0, half=0)
                transpose_x(h, 2, 3)
                features(h, 9, USE_UP[0] + 1, 1, half=0)
                for bank in range(2):
                    pe.wait_ge(t_free[bank], 6 * h + 6 + CREDIT)
                features(h, 9, USE_UP[0], 0, half=1)
                gate_logits(h)
                features(h, 9, USE_UP[0] + 1, 1, half=1)
                gate_transpose(h)
                for f in range(2):
                    for j in range(2 if f == 0 else 0, 8):
                        features(h, (9, 13)[f] + j // 4, USE_UP[f] + j, j % 4)
                    down(h, f)


_INPUTS = ["x", "ctx_main", "ctx_last", "mask", "wq", "wk", "wv", "units", "gate", "n1", "n2", "bo"]


def kernel(**inputs):
    import numpy as np
    import concourse.bacc as _bacc
    from concourse.bass_utils import run_bass_kernel_spmd as _run

    a = {k: np.asarray(v) for k, v in inputs.items()}

    def by_rows(w):
        return np.ascontiguousarray(w.reshape(-1, P, w.shape[1]).transpose(1, 0, 2))

    ctx = a["ctx_768"]
    qkv, up, down = a["L0_ffn_qkv_w"], a["L0_ffn_up_w"], a["L0_ffn_down_w"]
    mats = {"x_wo": a["L0_xattn_Wo"], "a_v": a["L0_attn_Wv"].T, "a_k": a["L0_attn_Wk"].T,
            "a_q": a["L0_attn_Wq"].T, "a_wo": a["L0_attn_Wo"].T,
            "f_q": qkv[0:D].T, "f_k": qkv[D:2 * D].T, "f_v": qkv[2 * D:3 * D].T, "f_wo": a["L0_ffn_o_w"].T}
    for j in range(4):
        mats[f"up{j}"] = up[D * j:D * (j + 1)].T
        mats[f"down{j}"] = down[:, D * j:D * (j + 1)].T
    arrays = {
        "x": a["x"].reshape(NB * SEQ, D),
        "ctx_main": ctx[:, 0:MAIN].reshape(PAIRS, 2, MAIN, CC, P).transpose(0, 4, 3, 1, 2).reshape(PAIRS, P, CC, 2 * MAIN),
        "ctx_last": ctx[:, MAIN].reshape(NB, CC, P).transpose(2, 1, 0),
        "mask": a["mask_BxS2_bf1"].view(np.uint8),
        "wq": by_rows(a["L0_xattn_Wq"]),
        "wk": by_rows(a["L0_xattn_Wk"]),
        "wv": by_rows(a["L0_xattn_Wv"]),
        "units": np.stack([by_rows(mats[n]) for n in UNITS]),
        "gate": by_rows(a["L0_ffn_gate_w"].T),
        "n1": a["L0_ffn_n1_w"], "n2": a["L0_ffn_n2_w"], "bo": a["L0_attn_bo"],
    }
    nc = _bacc.Bacc("TRN2", target_bir_lowering=False, num_devices=1)
    named, args = {}, []
    for name in _INPUTS:
        named[f"in_{name}"] = np.ascontiguousarray(arrays[name])
        args.append(nc.dram_tensor(f"in_{name}", named[f"in_{name}"].shape,
                                   mybir.dt.from_np(named[f"in_{name}"].dtype), kind="ExternalInput").ap())
    args.append(nc.dram_tensor("out", (NB * SEQ, D), F32, kind="ExternalOutput").ap())
    build(nc, *args)
    got = _run(nc, [named], core_ids=[0])
    return got.results[0]["out"].reshape(NB, SEQ, D)
```
